# Optimizing a Trainium2 kernel written in Bass

```python
import numpy as np
import jax
import jax.numpy as jnp

def _softmax(x, axis=-1):
    return jax.nn.softmax(x, axis=axis)

def _gelu(x):
    return jax.nn.gelu(x, approximate=True)

def _silu(x):
    return jax.nn.silu(x)

def _sigmoid(x):
    return jax.nn.sigmoid(x)

def _layernorm(x, axis=-1, eps=1e-05):
    m = jnp.mean(x, axis=axis, keepdims=True)
    v = jnp.var(x, axis=axis, keepdims=True)
    return (x - m) / jnp.sqrt(v + eps)

def _scatter_add(tgt, idx, src, axis=0):
    return tgt.at[idx].add(src)

def _segment_sum(src, seg, n):
    return jax.ops.segment_sum(src, seg, n)
kernel_name = 'mk_cond_resid_d4_seqx_r4_29bfe0'

def setup_inputs(seed: int=0):
    np.random.seed(seed)
    _w = jnp.asarray

    def _rec_inputs():
        import jax
        import jax.numpy as jnp
        _rk = jax.random.key(seed)
        x = -0.0002928 + 1 * jax.random.normal(jax.random.fold_in(_rk, 1), (64, 64, 256), jnp.float32)
        _lenS = 64 - jax.random.randint(jax.random.fold_in(_rk, 7), (64,), 0, max(1, 64 // 4) + 1, jnp.int32)
        _lenS2 = 64 - jax.random.randint(jax.random.fold_in(_rk, 8), (64,), 0, max(1, 64 // 4) + 1, jnp.int32)
        cond_1024 = 0.000887014 + 1.03683 * jax.random.normal(jax.random.fold_in(_rk, 11), (64, 256), jnp.float32)
        return (x, cond_1024)
    x, cond_1024 = _rec_inputs()

    def _L0_cond_setup():
        import jax, jax.numpy as jnp
        import numpy as np
        D = 256
        H = 16
        DH = D // H
        K = 4
        LN_EPS = 1e-05

        def _ln(x, gamma, beta):
            mu = jnp.mean(x, axis=-1, keepdims=True)
            var = jnp.mean((x - mu) ** 2, axis=-1, keepdims=True)
            return (x - mu) / jnp.sqrt(var + LN_EPS) * gamma + beta

        def _heads(x, B, T):
            return x.reshape(B, T, H, DH).transpose(0, 2, 1, 3)
        key = jax.random.key(seed)
        ks = jax.random.split(key, 32)
        B, T = (2, 512)
        s = 0.02
        inp = {'z': jax.random.normal(ks[0], (B, T, D), jnp.float32), 'g': jax.random.normal(ks[1], (B, D), jnp.float32), 'Wq': jax.random.normal(ks[2], (D, D), jnp.float32) * s, 'bq': jnp.zeros((D,), jnp.float32), 'Wk_is': jax.random.normal(ks[3], (D, D), jnp.float32) * s, 'bk_is': jnp.zeros((D,), jnp.float32), 'Wv_is': jax.random.normal(ks[4], (D, D), jnp.float32) * s, 'bv_is': jnp.zeros((D,), jnp.float32), 'Wg': jax.random.normal(ks[5], (D, D * K), jnp.float32) * s, 'bg': jnp.zeros((D * K,), jnp.float32), 'Wk_cs': jax.random.normal(ks[6], (D, D), jnp.float32) * s, 'bk_cs': jnp.zeros((D,), jnp.float32), 'Wv_cs': jax.random.normal(ks[7], (D, D), jnp.float32) * s, 'bv_cs': jnp.zeros((D,), jnp.float32), 'Wo_is': jax.random.normal(ks[8], (D, D), jnp.float32) * s, 'bo_is': jnp.zeros((D,), jnp.float32), 'Wo_cs': jax.random.normal(ks[9], (D, D), jnp.float32) * s, 'bo_cs': jnp.zeros((D,), jnp.float32), 'Wgate': jax.random.normal(ks[10], (2 * D, D), jnp.float32) * s, 'bgate': jnp.zeros((D,), jnp.float32), 'W1': jax.random.normal(ks[11], (D, 4 * D), jnp.float32) * s, 'b1': jnp.zeros((4 * D,), jnp.float32), 'W2': jax.random.normal(ks[12], (4 * D, D), jnp.float32) * s, 'b2': jnp.zeros((D,), jnp.float32), 'ln1_g': jnp.ones((D,), jnp.float32), 'ln1_b': jnp.zeros((D,), jnp.float32), 'ln2_g': jnp.ones((D,), jnp.float32), 'ln2_b': jnp.zeros((D,), jnp.float32), 'Wout': jax.random.normal(ks[13], (D, D), jnp.float32) * s, 'bout': jnp.zeros((D,), jnp.float32)}
        return inp
    _L0_cond_all = _L0_cond_setup()
    _L0_cond_in = {k: v for k, v in _L0_cond_all.items() if k in ('Wq', 'bq', 'Wk_is', 'bk_is', 'Wv_is', 'bv_is', 'Wg', 'bg', 'Wk_cs', 'bk_cs', 'Wv_cs', 'bv_cs', 'Wo_is', 'bo_is', 'Wo_cs', 'bo_cs', 'Wgate', 'bgate', 'W1', 'b1', 'W2', 'b2', 'ln1_g', 'ln1_b', 'ln2_g', 'ln2_b', 'Wout', 'bout')}
    del _L0_cond_all

    def _L1_cond_setup():
        import jax, jax.numpy as jnp
        import numpy as np
        N, T, D, H = (64, 128, 256, 256)
        key = jax.random.key(seed)
        k1, k2, k3, k4 = jax.random.split(key, 4)
        x = jax.random.normal(k1, (N, T, D), dtype=jnp.float32)
        h0 = jax.random.normal(k2, (N, H), dtype=jnp.float32)
        Wx = jax.random.normal(k3, (D, H), dtype=jnp.float32) / np.sqrt(D)
        Wh = jax.random.normal(k4, (H, H), dtype=jnp.float32) / np.sqrt(H)
        b = jnp.zeros((H,), dtype=jnp.float32)
        return {'x': x, 'h0': h0, 'Wx': Wx, 'Wh': Wh, 'b': b}
    _L1_cond_all = _L1_cond_setup()
    _L1_cond_in = {k: v for k, v in _L1_cond_all.items() if k in ('Wx', 'Wh', 'b')}
    del _L1_cond_all

    def _L2_cond_setup():
        import jax, jax.numpy as jnp
        import numpy as np
        N, T, D, H = (64, 128, 256, 256)

        def lstm_scan(x, h0, Wx, Wh, b):
            xW = jnp.einsum('ntd,dg->ntg', x, Wx) + b
            Hdim = h0.shape[1]
            c0 = jnp.zeros_like(h0)

            def step(carry, xw_t):
                prev_h, prev_c = carry
                a = xw_t + prev_h @ Wh
                i = jax.nn.sigmoid(a[:, :Hdim])
                f = jax.nn.sigmoid(a[:, Hdim:2 * Hdim])
                o = jax.nn.sigmoid(a[:, 2 * Hdim:3 * Hdim])
                g = jnp.tanh(a[:, 3 * Hdim:])
                next_c = f * prev_c + i * g
                next_h = o * jnp.tanh(next_c)
                return ((next_h, next_c), next_h)
            _, hs = jax.lax.scan(step, (h0, c0), jnp.swapaxes(xW, 0, 1))
            return jnp.swapaxes(hs, 0, 1)
        key = jax.random.key(seed)
        k1, k2, k3, k4 = jax.random.split(key, 4)
        x = jax.random.normal(k1, (N, T, D), dtype=jnp.float32)
        h0 = jax.random.normal(k2, (N, H), dtype=jnp.float32)
        Wx = jax.random.normal(k3, (D, 4 * H), dtype=jnp.float32) / np.sqrt(D)
        Wh = jax.random.normal(k4, (H, 4 * H), dtype=jnp.float32) / np.sqrt(H)
        b = jnp.zeros((4 * H,), dtype=jnp.float32)
        return {'x': x, 'h0': h0, 'Wx': Wx, 'Wh': Wh, 'b': b}
    _L2_cond_all = _L2_cond_setup()
    _L2_cond_in = {k: v for k, v in _L2_cond_all.items() if k in ('Wx', 'Wh', 'b')}
    del _L2_cond_all

    def _L3_cond_setup():
        import jax, jax.numpy as jnp
        import numpy as np
        key = jax.random.key(seed)
        ks = jax.random.split(key, 8)
        B, L, D, N, K = (4, 1024, 256, 64, 4)
        return {'x': jax.random.normal(ks[0], (B, L, D), dtype=jnp.float32), 'conv_w': jax.random.normal(ks[1], (K, 1, D), dtype=jnp.float32) * 0.1, 'conv_b': jnp.zeros((D,), dtype=jnp.float32), 'Wp': jax.random.normal(ks[2], (D, 2 * N), dtype=jnp.float32) * (1.0 / np.sqrt(D)), 'bp': jnp.zeros((2 * N,), dtype=jnp.float32), 'Ws': jax.random.normal(ks[3], (D, N), dtype=jnp.float32) * (1.0 / np.sqrt(D)), 'bs': jnp.zeros((N,), dtype=jnp.float32), 'A_log': jax.random.normal(ks[4], (N,), dtype=jnp.float32) * 0.02, 'dt_log': jax.random.normal(ks[5], (N,), dtype=jnp.float32) * 0.02, 'Wo': jax.random.normal(ks[6], (N, D), dtype=jnp.float32) * (1.0 / np.sqrt(N)), 'bo': jnp.zeros((D,), dtype=jnp.float32)}
    _L3_cond_all = _L3_cond_setup()
    _L3_cond_in = {k: v for k, v in _L3_cond_all.items() if k in ('conv_b', 'Wp', 'bp', 'Ws', 'bs', 'A_log', 'dt_log', 'Wo', 'bo')}
    del _L3_cond_all
    return {'x': x, 'cond_1024': cond_1024, 'L0_cond_Wq': _L0_cond_in['Wq'], 'L0_cond_bq': _L0_cond_in['bq'], 'L0_cond_Wk_is': _L0_cond_in['Wk_is'], 'L0_cond_bk_is': _L0_cond_in['bk_is'], 'L0_cond_Wv_is': _L0_cond_in['Wv_is'], 'L0_cond_bv_is': _L0_cond_in['bv_is'], 'L0_cond_Wg': _L0_cond_in['Wg'], 'L0_cond_bg': _L0_cond_in['bg'], 'L0_cond_Wk_cs': _L0_cond_in['Wk_cs'], 'L0_cond_bk_cs': _L0_cond_in['bk_cs'], 'L0_cond_Wv_cs': _L0_cond_in['Wv_cs'], 'L0_cond_bv_cs': _L0_cond_in['bv_cs'], 'L0_cond_Wo_is': _L0_cond_in['Wo_is'], 'L0_cond_bo_is': _L0_cond_in['bo_is'], 'L0_cond_Wo_cs': _L0_cond_in['Wo_cs'], 'L0_cond_bo_cs': _L0_cond_in['bo_cs'], 'L0_cond_Wgate': _L0_cond_in['Wgate'], 'L0_cond_bgate': _L0_cond_in['bgate'], 'L0_cond_W1': _L0_cond_in['W1'], 'L0_cond_b1': _L0_cond_in['b1'], 'L0_cond_W2': _L0_cond_in['W2'], 'L0_cond_b2': _L0_cond_in['b2'], 'L0_cond_ln1_g': _L0_cond_in['ln1_g'], 'L0_cond_ln1_b': _L0_cond_in['ln1_b'], 'L0_cond_ln2_g': _L0_cond_in['ln2_g'], 'L0_cond_ln2_b': _L0_cond_in['ln2_b'], 'L0_cond_Wout': _L0_cond_in['Wout'], 'L0_cond_bout': _L0_cond_in['bout'], 'L1_cond_Wx': _L1_cond_in['Wx'], 'L1_cond_Wh': _L1_cond_in['Wh'], 'L1_cond_b': _L1_cond_in['b'], 'L2_cond_Wx': _L2_cond_in['Wx'], 'L2_cond_Wh': _L2_cond_in['Wh'], 'L2_cond_b': _L2_cond_in['b'], 'L3_cond_conv_b': _L3_cond_in['conv_b'], 'L3_cond_Wp': _L3_cond_in['Wp'], 'L3_cond_bp': _L3_cond_in['bp'], 'L3_cond_Ws': _L3_cond_in['Ws'], 'L3_cond_bs': _L3_cond_in['bs'], 'L3_cond_A_log': _L3_cond_in['A_log'], 'L3_cond_dt_log': _L3_cond_in['dt_log'], 'L3_cond_Wo': _L3_cond_in['Wo'], 'L3_cond_bo': _L3_cond_in['bo']}

def reference(x, cond_1024, L0_cond_Wq, L0_cond_bq, L0_cond_Wk_is, L0_cond_bk_is, L0_cond_Wv_is, L0_cond_bv_is, L0_cond_Wg, L0_cond_bg, L0_cond_Wk_cs, L0_cond_bk_cs, L0_cond_Wv_cs, L0_cond_bv_cs, L0_cond_Wo_is, L0_cond_bo_is, L0_cond_Wo_cs, L0_cond_bo_cs, L0_cond_Wgate, L0_cond_bgate, L0_cond_W1, L0_cond_b1, L0_cond_W2, L0_cond_b2, L0_cond_ln1_g, L0_cond_ln1_b, L0_cond_ln2_g, L0_cond_ln2_b, L0_cond_Wout, L0_cond_bout, L1_cond_Wx, L1_cond_Wh, L1_cond_b, L2_cond_Wx, L2_cond_Wh, L2_cond_b, L3_cond_conv_b, L3_cond_Wp, L3_cond_bp, L3_cond_Ws, L3_cond_bs, L3_cond_A_log, L3_cond_dt_log, L3_cond_Wo, L3_cond_bo):
    import jax
    import jax.numpy as jnp

    def _L0_cond_ref(z, g, Wq, bq, Wk_is, bk_is, Wv_is, bv_is, Wg, bg, Wk_cs, bk_cs, Wv_cs, bv_cs, Wo_is, bo_is, Wo_cs, bo_cs, Wgate, bgate, W1, b1, W2, b2, ln1_g, ln1_b, ln2_g, ln2_b, Wout, bout):
        import jax, jax.numpy as jnp
        import numpy as np
        D = 256
        H = 16
        DH = D // H
        K = 4
        LN_EPS = 1e-05

        def _ln(x, gamma, beta):
            mu = jnp.mean(x, axis=-1, keepdims=True)
            var = jnp.mean((x - mu) ** 2, axis=-1, keepdims=True)
            return (x - mu) / jnp.sqrt(var + LN_EPS) * gamma + beta

        def _heads(x, B, T):
            return x.reshape(B, T, H, DH).transpose(0, 2, 1, 3)
        B, T, _ = z.shape
        scale = 1.0 / jnp.sqrt(jnp.asarray(DH, z.dtype))
        q_is = _heads(z @ Wq + bq, B, T)
        k_is = _heads(z @ Wk_is + bk_is, B, T)
        v_is = _heads(z @ Wv_is + bv_is, B, T)
        scores = jnp.einsum('bhqd,bhkd->bhqk', q_is, k_is) * scale
        causal = jnp.triu(jnp.full((T, T), -jnp.inf, dtype=scores.dtype), k=1)
        scores = scores + causal[None, None]
        attn = jax.nn.softmax(scores, axis=-1)
        is_ctx = jnp.einsum('bhqk,bhkd->bhqd', attn, v_is)
        is_ctx = is_ctx.transpose(0, 2, 1, 3).reshape(B, T, D)
        is_ctx = is_ctx @ Wo_is + bo_is
        g_tokens = (g @ Wg + bg).reshape(B, K, D)
        q_cs = _heads(z @ Wq + bq, B, T)
        k_cs = _heads(g_tokens @ Wk_cs + bk_cs, B, K)
        v_cs = _heads(g_tokens @ Wv_cs + bv_cs, B, K)
        cs_scores = jnp.einsum('bhqd,bhkd->bhqk', q_cs, k_cs) * scale
        cs_attn = jax.nn.softmax(cs_scores, axis=-1)
        cs_ctx = jnp.einsum('bhqk,bhkd->bhqd', cs_attn, v_cs)
        cs_ctx = cs_ctx.transpose(0, 2, 1, 3).reshape(B, T, D)
        cs_ctx = cs_ctx @ Wo_cs + bo_cs
        gate = jax.nn.sigmoid(jnp.concatenate([is_ctx, cs_ctx], axis=-1) @ Wgate + bgate)
        fused = gate * cs_ctx + (1.0 - gate) * is_ctx
        x = _ln(z + fused, ln1_g, ln1_b)
        ffn = jax.nn.gelu(x @ W1 + b1, approximate=False) @ W2 + b2
        x = _ln(x + ffn, ln2_g, ln2_b)
        return x @ Wout + bout

    def _L1_cond_ref(x, h0, Wx, Wh, b):
        import jax, jax.numpy as jnp
        import numpy as np
        N, T, D, H = (64, 128, 256, 256)
        xW = jnp.einsum('ntd,dh->nth', x, Wx) + b
        xW_t = jnp.swapaxes(xW, 0, 1)

        def step(prev_h, xw):
            next_h = jnp.tanh(prev_h @ Wh + xw)
            return (next_h, next_h)
        _, h_t = jax.lax.scan(step, h0, xW_t)
        return jnp.swapaxes(h_t, 0, 1)

    def _L2_cond_ref(x, h0, Wx, Wh, b):
        import jax, jax.numpy as jnp
        import numpy as np
        N, T, D, H = (64, 128, 256, 256)

        def lstm_scan(x, h0, Wx, Wh, b):
            xW = jnp.einsum('ntd,dg->ntg', x, Wx) + b
            Hdim = h0.shape[1]
            c0 = jnp.zeros_like(h0)

            def step(carry, xw_t):
                prev_h, prev_c = carry
                a = xw_t + prev_h @ Wh
                i = jax.nn.sigmoid(a[:, :Hdim])
                f = jax.nn.sigmoid(a[:, Hdim:2 * Hdim])
                o = jax.nn.sigmoid(a[:, 2 * Hdim:3 * Hdim])
                g = jnp.tanh(a[:, 3 * Hdim:])
                next_c = f * prev_c + i * g
                next_h = o * jnp.tanh(next_c)
                return ((next_h, next_c), next_h)
            _, hs = jax.lax.scan(step, (h0, c0), jnp.swapaxes(xW, 0, 1))
            return jnp.swapaxes(hs, 0, 1)
        return lstm_scan(x, h0, Wx, Wh, b)

    def _L3_cond_ref(x, conv_w, conv_b, Wp, bp, Ws, bs, A_log, dt_log, Wo, bo):
        import jax, jax.numpy as jnp
        import numpy as np
        B, L, D = x.shape
        K = conv_w.shape[0]
        N = Ws.shape[1]
        x_pad = jnp.pad(x, ((0, 0), (K - 1, 0), (0, 0)))
        conv = conv_b + sum((x_pad[:, k:k + L, :] * conv_w[k, 0] for k in range(K)))
        proj = conv @ Wp + bp
        B_t = jax.nn.softplus(proj[..., :N])
        C_t = jnp.tanh(proj[..., N:])
        u = x @ Ws + bs
        A = -jax.nn.softplus(A_log)
        dt = jax.nn.softplus(dt_log)
        decay = 1.0 + dt * A

        def step(state, inputs):
            u_t, b_t, c_t = inputs
            state = decay * state + dt * b_t * u_t
            return (state, c_t * state)
        init = jnp.zeros((B, N), dtype=x.dtype)
        xs = tuple((jnp.swapaxes(a, 0, 1) for a in (u, B_t, C_t)))
        _, ys = jax.lax.scan(step, init, xs, unroll=4)
        y = jnp.swapaxes(ys, 0, 1)
        return y @ Wo + bo
    x = x + _L0_cond_ref(x, cond_1024, L0_cond_Wq, L0_cond_bq, L0_cond_Wk_is, L0_cond_bk_is, L0_cond_Wv_is, L0_cond_bv_is, L0_cond_Wg, L0_cond_bg, L0_cond_Wk_cs, L0_cond_bk_cs, L0_cond_Wv_cs, L0_cond_bv_cs, L0_cond_Wo_is, L0_cond_bo_is, L0_cond_Wo_cs, L0_cond_bo_cs, L0_cond_Wgate, L0_cond_bgate, L0_cond_W1, L0_cond_b1, L0_cond_W2, L0_cond_b2, L0_cond_ln1_g, L0_cond_ln1_b, L0_cond_ln2_g, L0_cond_ln2_b, L0_cond_Wout, L0_cond_bout)
    x = x + _L1_cond_ref(x, cond_1024, L1_cond_Wx, L1_cond_Wh, L1_cond_b)
    x = x + _L2_cond_ref(x, cond_1024, L2_cond_Wx, L2_cond_Wh, L2_cond_b)
    x = x + _L3_cond_ref(x, cond_1024[:, None, :], L3_cond_conv_b, L3_cond_Wp, L3_cond_bp, L3_cond_Ws, L3_cond_bs, L3_cond_A_log, L3_cond_dt_log, L3_cond_Wo, L3_cond_bo)
    return x

_drawn_inputs = setup_inputs


def setup_inputs(seed=0):
    import zlib

    import numpy as np

    out = dict(_drawn_inputs(seed))
    spreads = {'L0_cond_bq': (0.0, 0.8),
     'L0_cond_bk_is': (0.0, 2.0),
     'L0_cond_bv_is': (0.0, 0.441),
     'L0_cond_bg': (0.0, 0.8),
     'L0_cond_bk_cs': (0.0, 2.0),
     'L0_cond_bv_cs': (0.0, 0.612),
     'L0_cond_bo_is': (0.0, 0.359),
     'L0_cond_bo_cs': (0.0, 0.329),
     'L0_cond_bgate': (0.0, 0.8),
     'L0_cond_b1': (0.0, 0.1),
     'L0_cond_b2': (0.0, 0.1),
     'L0_cond_ln1_g': (1.0, 0.2),
     'L0_cond_ln1_b': (0.0, 0.1),
     'L0_cond_ln2_g': (1.0, 0.2),
     'L0_cond_ln2_b': (0.0, 0.1),
     'L0_cond_bout': (0.0, 0.1),
     'L1_cond_b': (0.0, 0.1),
     'L2_cond_b': (0.0, 0.1),
     'L3_cond_conv_b': (0.0, 0.1),
     'L3_cond_bp': (0.0, 0.278),
     'L3_cond_bs': (0.0, 0.1),
     'L3_cond_bo': (0.0, 0.423)}
    factors = {'L0_cond_Wq': 8.0,
     'L0_cond_Wk_is': 8.0,
     'L0_cond_Wv_is': 3.935,
     'L0_cond_Wg': 7.563,
     'L0_cond_Wk_cs': 8.0,
     'L0_cond_Wv_cs': 6.975,
     'L0_cond_Wo_cs': 3.596,
     'L0_cond_Wgate': 8.0,
     'L3_cond_A_log': 5.555,
     'L3_cond_dt_log': 3.953}
    for name, (base, spread) in spreads.items():
        noise = np.random.default_rng([zlib.crc32(name.encode()), seed]).standard_normal(out[name].shape)
        drawn = base * np.exp(spread * noise) if base else spread * noise
        out[name] = jnp.asarray(drawn.astype(out[name].dtype))
    for name, factor in factors.items():
        out[name] = (out[name] * factor).astype(out[name].dtype)
    return out
```

```python
from contextlib import ExitStack

import concourse.bass as bass
from concourse import mybir

ALU = mybir.AluOpType
ACT = mybir.ActivationFunctionType
AX = mybir.AxisListType
F32 = mybir.dt.float32
BF16 = mybir.dt.bfloat16

P = 128
B, T, D = 64, 64, 256
H, DH, NK = 16, 16, 4
KT = D // P
HG = P // DH
CB = 8
CN = CB * T
NCH = B // CB
PAIRS = CB // 2
FF = 4 * D
FT = FF // P
NS = 64
SCALE = DH ** -0.5
EPS = 1e-5
COLS0 = ("bq", "bk_is", "bv_is", "bo_is", "bv_cs", "bo_cs", "bk_cs", "ln1_g", "ln1_b", "ln2_g", "ln2_b", "bout", "b1")


def cond_resid_kernel(nc, a, out):
    ctx = ExitStack()
    with ctx:
        def sem(name):
            return ctx.enter_context(nc.semaphore(name))

        arena = ctx.enter_context(nc.sbuf_tensor("arena", [P, 52800], F32))
        psum = ctx.enter_context(nc.psum_tensor("psum", [P, 8, 512], F32))
        taken = [0]

        def carve(*dims):
            n = 1
            for d in dims:
                n *= d
            v = arena[:, taken[0]:taken[0] + n]
            taken[0] += n
            assert taken[0] <= 52800, taken[0]
            names = "abcd"[:len(dims)]
            if len(dims) == 1:
                return v
            return v.rearrange(f"p ({' '.join(names)}) -> p {' '.join(names)}",
                               **{n: d for n, d in zip(names, dims)})

        ident = carve(P)
        xT_all = carve(KT, T, B)
        phase_start = taken[0]

        wq, wk, wv = carve(KT, D), carve(KT, D), carve(KT, D)
        w_is = carve(KT, 2 * D)
        w_cs = carve(KT, 2 * D)
        w1 = carve(KT, FF)
        w2 = carve(FT, D)
        wout = carve(KT, D)
        cols = carve(40)
        bias3 = carve(3 * D)
        ln1_g_row, x1_b_row = carve(D), carve(D)
        hmask = carve(HG)
        vmask = carve(D)
        neg_half = carve(PAIRS)
        kcsT = carve(KT, B, NK)
        kcs_bd = carve(KT, HG, CB * NK)
        vcs_rep = carve(CB, D)
        vcs_bd = carve(CB, D)
        zT = carve(KT, CN)
        qT = carve(KT, CN)
        kT = carve(KT, CN)
        k_bd = carve(KT, HG, CN)
        v_bd = carve(CB, H // 2, 2, DH)
        e = carve(2 * 512)
        pT = carve(2 * PAIRS, P)
        rrep = carve(D)
        rT = carve(KT, P)
        ctxT, csxT = carve(KT, CN), carve(KT, CN)
        cs_e = carve(H, NK)
        cs_pT = carve(P)
        stats = carve(5 * H)
        proj3 = carve(2, 3 * D)
        z_nat = carve(PAIRS, D)
        lnb = carve(PAIRS, D)
        x1_res = carve(PAIRS, D)
        ffT = carve(KT, CN)
        hT = carve(FT, CN)
        xres = carve(KT, CN)
        bn6 = carve(PAIRS, 6)
        mv = carve(PAIRS, 2)
        ve, rstd = carve(PAIRS), carve(PAIRS)
        wog_is = hT[:, 0:2, 0:D]
        wog_cs = hT[:, 2:4, 0:D]
        wgate = hT[:, 4:8, 0:D]
        wg = k_bd[:, 0, 0:4, :].rearrange("p a b -> p (a b)").rearrange("p (k n) -> p k n", k=KT)
        wkcs, wvcs = k_bd[:, 0, 4, :].rearrange("p (k n) -> p k n", k=KT), \
            k_bd[:, 0, 5, :].rearrange("p (k n) -> p k n", k=KT)
        condT = k_bd[:, 0, 6, 0:KT * B].rearrange("p (k n) -> p k n", k=KT)
        gtT = k_bd[:, 1, 0, :].rearrange("p (j k b) -> p j k b", j=NK, k=KT)
        vcs_nat = k_bd[0:B, 1, 1:3, :].rearrange("p a b -> p (a b)").rearrange("p (j n) -> p j n", j=NK)
        mask_f = x1_res[:, 1, 0:T]
        c_is, c_cs = cols[:, 32:34], cols[:, 34:36]

        mask_l = ctx.enter_context(nc.sbuf_tensor("mask_l", [P, T], BF16))
        mask_r = ctx.enter_context(nc.sbuf_tensor("mask_r", [P, T], BF16))
        vcs_dram = nc.dram_tensor("vcs_dram", (NK, B, D), F32, kind="Internal").ap()
        x3_dram = nc.dram_tensor("x3_dram", (B, T, D), F32, kind="Internal").ap()
        x3r_dram = nc.dram_tensor("x3r_dram", (T, B, D), F32, kind="Internal").ap()

        COL = {name: 2 * i for i, name in enumerate(COLS0)}
        NCOLS = 2 * (len(COLS0) - 1) + FT
        bgc = proj3[:, 0, 0:8]

        def col(name, k):
            c = COL[name] + k
            return cols[:, c:c + 1]

        s_ps = psum[:, 0:2, :]
        pT_ps = psum[:, 0:2, :].rearrange("p a (b n) -> p (a b) n", n=P)
        ctx_ps = psum[:, 2, 0:256].rearrange("p (g n) -> p g n", g=KT)
        rT_ps = psum[:, 3, 256:512].rearrange("p (g n) -> p g n", g=KT)
        cs_ps = psum[:, 3, 0:64]
        cspT_ps = psum[0:64, 3, 64:192]
        csx_ps = psum[:, 2, 256:512].rearrange("p (g n) -> p g n", g=KT)

        nmax, rsum, rinv, csm, css = (stats[:, i * H:(i + 1) * H] for i in range(5))

        passed = sem("passed")
        ld_w = sem("ld_w")
        ld_zt = sem("ld_zt")
        ld_zn = sem("ld_zn")
        ld_xr = sem("ld_xr")
        ld_vcs = sem("ld_vcs")
        ld_kbd = sem("ld_kbd")
        st_vcs = sem("st_vcs")
        pe_w = sem("pe_w")
        gm_ps = sem("gm_ps")
        gt_ps = sem("gt_ps")
        gt_done = sem("gt_done")
        kcs_ps = sem("kcs_ps")
        kcs_done = sem("kcs_done")
        vcs_ps = sem("vcs_ps")
        vcs_done = sem("vcs_done")
        cst_ps = sem("cst_ps")
        cst_done = sem("cst_done")
        row_ps = sem("row_ps")
        row_done = sem("row_done")
        zero_done = sem("zero_done")
        half_done = sem("half_done")
        mask_done = sem("mask_done")
        kq_ps = sem("kq_ps")
        v_ps = sem("v_ps")
        scores_ps = sem("scores_ps")
        pt_ps = sem("pt_ps")
        pv_ps = sem("pv_ps")
        a_ps = sem("a_ps")
        x1t_ps = sem("x1t_ps")
        ff_ps = sem("ff_ps")
        c_ps = sem("c_ps")
        x2t_ps = sem("x2t_ps")
        wout_ps = sem("wout_ps")
        kt_done = sem("kt_done")
        qt_done = sem("qt_done")
        v0_done = sem("v0_done")
        v1_done = sem("v1_done")
        nmax_done = sem("nmax_done")
        sub_done = sem("sub_done")
        exp_done = sem("exp_done")
        rsum_done = sem("rsum_done")
        rinv_done = sem("rinv_done")
        rrep_done = sem("rrep_done")
        csmax_done = sem("csmax_done")
        cssub_done = sem("cssub_done")
        csexp_done = sem("csexp_done")
        cssum_done = sem("cssum_done")
        csrec_done = sem("csrec_done")
        csp_done = sem("csp_done")
        pt0_done = sem("pt0_done")
        pt1_done = sem("pt1_done")
        cspt_done = sem("cspt_done")
        rt_done = sem("rt_done")
        ctx_done = sem("ctx_done")
        csx_done = sem("csx_done")
        abias_done = sem("abias_done")
        th_done = sem("th_done")
        dd_done = sem("dd_done")
        iz_done = sem("iz_done")
        gm_done = sem("gm_done")
        f_done = sem("f_done")
        x1t_done = sem("x1t_done")
        x1g_done = sem("x1g_done")
        x1r_done = sem("x1r_done")
        gelu_done = sem("gelu_done")
        y_done = sem("y_done")
        x2t_done = sem("x2t_done")
        xout_done = sem("xout_done")
        kcsbd_done = sem("kcsbd_done")
        vcsbd_done = sem("vcsbd_done")
        st1 = sem("st1")
        mv1 = sem("mv1")
        ve1 = sem("ve1")
        rstd1 = sem("rstd1")
        xh1 = sem("xh1")
        st2 = sem("st2")
        mv2 = sem("mv2")
        ve2 = sem("ve2")
        rstd2 = sem("rstd2")
        xh2 = sem("xh2")

        def count(value):
            return max(value, 0) if isinstance(value, int) else value

        def apart(eng):
            eng.sem_inc(passed, 1)

        def diag_rows(h):
            return slice(h * DH, (h + 1) * DH)

        kp = "(k p) n -> p k n"
        loads = []
        loads.append((wq, a["L0_cond_Wq"].rearrange(kp, p=P)))
        loads.append((wk, a["L0_cond_Wk_is"].rearrange(kp, p=P)))
        loads.append((wv, a["L0_cond_Wv_is"].rearrange(kp, p=P)))
        loads.append((zT, a["xT"].rearrange(kp, p=P)[:, :, 0:CN]))
        loads.append((cols[:, 0:NCOLS], a["cols0"]))
        loads.append((mask_f, a["mask"]))
        loads.append((hmask, a["hmask"]))
        loads.append((ident, a["ident"]))
        loads.append((vmask[0:64, :], a["vmask"]))
        loads.append((bgc, a["bg_cols"]))
        loads.append((w_is[:, :, 0:D], a["L0_cond_Wo_is"].rearrange(kp, p=P)))
        loads.append((w_cs[:, :, 0:D], a["L0_cond_Wo_cs"].rearrange(kp, p=P)))
        loads.append((wog_is, a["Wo_isT"].rearrange(kp, p=P)))
        loads.append((wog_cs, a["Wo_csT"].rearrange(kp, p=P)))
        loads.append((wgate, a["L0_cond_Wgate"].rearrange(kp, p=P)))
        loads.append((condT, a["condT"].rearrange(kp, p=P)))
        loads.append((wg, a["L0_cond_Wg"].rearrange(kp, p=P)))
        loads.append((wkcs, a["L0_cond_Wk_cs"].rearrange(kp, p=P)))
        loads.append((wvcs, a["L0_cond_Wv_cs"].rearrange(kp, p=P)))
        loads.append((w1, a["L0_cond_W1"].rearrange(kp, p=P)))
        loads.append((w2, a["L0_cond_W2"].rearrange(kp, p=P)))
        loads.append((wout, a["L0_cond_Wout"].rearrange(kp, p=P)))
        loads.append((ln1_g_row, a["L0_cond_ln1_g"].partition_broadcast(P)))
        loads.append((x1_b_row, a["L0_cond_ln1_b"].partition_broadcast(P)))
        loads.append((x1_res[:, 0, :], a["L0_cond_b2"].partition_broadcast(P)))
        loads.append((bias3[:, 2 * D:3 * D], a["L0_cond_bgate"].partition_broadcast(P)))
        LD_W = 16 * len(loads)

        taken[0] = phase_start
        toeplitz = carve(T, D)
        x3r = carve(B, D)
        overlay = taken[0]
        wx1, wh1 = carve(KT, D), carve(KT, D)
        wx2, wh2 = carve(KT, 4, D), carve(KT, 4, D)
        x1s = [carve(KT, B), carve(KT, B)]
        x2s = [carve(KT, B), carve(KT, B)]
        x3s = [carve(KT, B), carve(KT, B)]
        x3n = [carve(D), carve(D)]
        h1T, h2T = carve(KT, B), carve(KT, B)
        h1n = carve(P)
        ifo, gg = carve(3, P), carve(P)
        cc, fc, ig, tc, h2n = carve(P), carve(P), carve(P), carve(P), carve(P)
        x3r_flat = x3r.rearrange("p b d -> p (b d)")
        brow = x3r_flat[:, 0:5 * D]
        brest = x3r_flat[:, 5 * D:10 * D]
        pick = carve(3)
        bparts = carve(5 * D // 2).bitcast(BF16)
        bpart = x3r_flat[:, 10 * D:10 * D + 5 * D // 2].bitcast(BF16)
        ones = carve(B // 2).bitcast(BF16)
        taken[0] = overlay
        conv = carve(P, B)
        u = carve(4, CN)
        ws, wp, wo3 = carve(KT, NS), carve(KT, 2 * NS), carve(D)
        cols3 = carve(16)
        after_overlay = taken[0]
        taken[0] = P
        bt, ct, decay_data = carve(4, CN), carve(4, CN), carve(4, CN)
        cvT = carve(KT, CN), carve(KT, CN)
        taken[0] = phase_start + T * D
        x3t = carve(B // 2, D)
        soft = carve(4, CN)
        bo_row = carve(D)
        st3, y3 = carve(4, CN), carve(4, CN)
        ld2 = sem("ld2")
        ld_toe = sem("ld_toe")
        bones = sem("bones")
        brow_d = sem("brow_d")
        x1s_done = sem("x1s_done")
        a1_ps = sem("a1_ps")
        h1_done = sem("h1_done")
        h1t_ps = sem("h1t_ps")
        h1t_done = sem("h1t_done")
        x2_done = sem("x2_done")
        a2_ps = sem("a2_ps")
        ifo_done = sem("ifo_done")
        g_done = sem("g_done")
        fc_done = sem("fc_done")
        ig_done = sem("ig_done")
        c_done = sem("c_done")
        tc_done = sem("tc_done")
        h2_done = sem("h2_done")
        h2t_ps = sem("h2t_ps")
        h2t_done = sem("h2t_done")
        x3_done = sem("x3_done")
        x3_ps = sem("x3_ps")
        x3n_done = sem("x3n_done")
        x3all_done = sem("x3all_done")
        ld3 = sem("ld3")
        ld_x3r = sem("ld_x3r")
        ld_x3t = sem("ld_x3t")
        u_ps = sem("u_ps")
        u_done = sem("u_done")
        conv_ps = sem("conv_ps")
        cvt_ps = sem("cvt_ps")
        cvt_done = sem("cvt_done")
        bc_ps = sem("bc_ps")
        b_done = sem("b_done")
        ct_done = sem("ct_done")
        abs_done = sem("abs_done")
        ex_done = sem("ex_done")
        ln_done = sem("ln_done")
        sp_done = sem("sp_done")
        v_done = sem("v_done")
        col3 = sem("col3")
        scan_done = sem("scan_done")
        yy_done = sem("yy_done")
        yo_ps = sem("yo_ps")
        xb_done = sem("xb_done")
        o_done = sem("o_done")
        st_out = sem("st_out")
        st_x3, st_x3r, conv_done = ([sem(f"{n}_{r}") for r in range(2)] for n in ("st_x3", "st_x3r", "conv_done"))

        LD2 = 16 * 11
        STEPS = T

        def wave(eng, step):
            for t in range(4):
                step(t, t % 2, False)
            with eng.Fori(2, T // 2 - 1) as i:
                step(2 * i, 0, False)
                step(2 * i + 1, 1, False)
            step(T - 2, 0, False)
            step(T - 1, 1, False)
            step(T, 0, True)

        def is_first(t):
            return isinstance(t, int) and t == 0

        def sp_tail(sp):
            def load(landed, dst, src):
                sp.dma_start(dst, src).then_inc(landed, 16)

            sp.wait_ge(xout_done, KT * NCH)
            sp.wait_ge(rstd2, NCH)
            load(ld2, wx1, a["L1_cond_Wx"].rearrange(kp, p=P))
            load(ld2, wh1, a["L1_cond_Wh"].rearrange(kp, p=P))
            load(ld2, brow[:, 0:D], a["L1_cond_b"].partition_broadcast(P))
            load(ld2, brow[:, D:5 * D], a["L2_cond_b"].partition_broadcast(P))
            load(ld2, pick, a["pick"])
            load(ld2, h1T, a["condT"].rearrange(kp, p=P))
            load(ld2, h2T, a["condT"].rearrange(kp, p=P))
            for k in range(KT):
                load(ld2, wx2[:, k], a["L2_cond_Wx"].rearrange("(k p) (g n) -> k p g n", p=P, n=D)[k])
                load(ld2, wh2[:, k], a["L2_cond_Wh"].rearrange("(k p) (g n) -> k p g n", p=P, n=D)[k])
            cp = a["cond_pad"]
            load(ld_toe, toeplitz[0:T].rearrange("p t d -> p (t d)"),
                 bass.AP(cp.tensor, D, [[D, T], [1, T * D]]))

            def store(t, r):
                sp.wait_ge(x3n_done, t + 1)
                apart(sp)
                sp.dma_start(x3_dram[:, bass.ds(t, 1), :].rearrange("b o n -> b (o n)"), x3n[r][0:B]
                             ).then_inc(st_x3[r], 16)
                sp.dma_start(x3r_dram[bass.ds(T - 1 - t, 1)].rearrange("o b n -> (o b) n"), x3n[r][0:B]
                             ).then_inc(st_x3r[r], 16)

            for t in range(2):
                store(t, t)
            with sp.Fori(1, T // 2) as i:
                store(2 * i, 0)
                store(2 * i + 1, 1)
            for r in range(2):
                sp.wait_ge(st_x3r[r], 8 * T)
                sp.wait_ge(st_x3[r], 8 * T)
            load(ld_x3r, x3r[0:T], x3r_dram)
            sp.wait_ge(a2_ps, T)
            sp.wait_ge(h2t_ps, T)
            load(ld3, ws, a["L3_cond_Ws"].rearrange(kp, p=P))
            load(ld3, wp, a["L3_cond_Wp"].rearrange(kp, p=P))
            for h in range(2):
                q = slice(64 * h, 64 * h + 64)
                load(ld3, wo3[q], a["L3_cond_Wo"])
            load(ld3, cols3[:, 0:7], a["cols3"])
            sp.wait_ge(conv_ps, 16)
            x3_tiles = x3_dram.rearrange("(i h) t n -> (h t) i n", h=2)
            load(ld_x3t, bo_row, a["L3_cond_bo"].partition_broadcast(P))
            for q in range(4):
                load(ld_x3t, x3t[:, 8 * q:8 * q + 8, :], x3_tiles[:, 8 * q:8 * q + 8, :])
            out_tiles = out.rearrange("(i h) t n -> (h t) i n", h=2)
            for g in range(8):
                sp.wait_ge(o_done, 4 * (g + 1))
                sp.dma_start(out_tiles[:, 4 * g:4 * g + 4, :], x3t[:, 4 * g:4 * g + 4, :]
                             ).then_inc(st_out, 16)
            sp.wait_ge(st_out, 16 * 8)

        def pe_tail(pe):
            def mm(o, l, r, start, stop):
                return pe.matmul(o, l, r, start=start, stop=stop)

            def halves(bank, n):
                return [psum[64 * h:64 * h + 64, bank, 0:n] for h in range(2)]

            def l1_x(t, r):
                pe.wait_ge(x1s_done, t + 1)
                pe.wait_ge(h1_done, count(t - 1))
                for h, o in enumerate(halves(r, P)):
                    mm(o, ones, bparts[:, h * P:(h + 1) * P], True, False)
                for k in range(KT):
                    for h, o in enumerate(halves(r, P)):
                        mm(o, x1s[r][:, k, :], wx1[:, k, h * P:(h + 1) * P], False, False)

            def l1_h(t, r):
                pe.wait_ge(h1t_done, t)
                for k in range(KT):
                    for h, o in enumerate(halves(r, P)):
                        x = mm(o, h1T[:, k, :], wh1[:, k, h * P:(h + 1) * P], False, k == 1)
                x.then_inc(a1_ps, 1)

            def l2_part(r, k, src, w):
                for h in range(2):
                    x = mm(psum[64 * h:64 * h + 64, 2 + r, :], src[:, k, :], w[:, k, :, h * P:(h + 1) * P],
                           False, w is wh2 and k == 1)
                return x

            def l2_x(t, r, between):
                pe.wait_ge(x2_done, t + 1)
                pe.wait_ge(g_done, count(t - 1))
                bp = bparts[:, D:5 * D].rearrange("p (g n) -> p g n", g=4)
                for h in range(2):
                    mm(psum[64 * h:64 * h + 64, 2 + r, :], ones, bp[:, :, h * P:(h + 1) * P], True, False)
                l2_part(r, 0, x2s[r], wx2)
                between()
                l2_part(r, 1, x2s[r], wx2)

            def l2_h(t, r):
                pe.wait_ge(h2t_done, t)
                l2_part(r, 0, h2T, wh2)
                l2_part(r, 1, h2T, wh2).then_inc(a2_ps, 1)

            def turn_h1(t):
                pe.wait_ge(h1_done, t + 1)
                pe.wait_ge(h1t_done, t)
                pe.wait_ge(x2_done, t)
                pe.transpose(psum[:, 4, 0:P], h1n, ident).then_inc(h1t_ps, 1)

            def turn_h2(t):
                pe.wait_ge(h2_done, t + 1)
                pe.wait_ge(h2t_done, t)
                pe.wait_ge(x3_done, t)
                pe.transpose(psum[:, 5, 0:P], h2n, ident).then_inc(h2t_ps, 1)

            def turn_x3(t, r):
                pe.wait_ge(x3_done, t + 1)
                pe.wait_ge(x3n_done, t)
                apart(pe)
                for k in range(KT):
                    x = pe.transpose(psum[0:B, 6, k * P:(k + 1) * P], x3s[r][:, k, :], ident)
                x.then_inc(x3_ps, 1)

            def step(t, r, last):
                if not is_first(t):
                    l2_h(t - 1, 1 - r)
                if not last:
                    l1_h(t, r)
                    if not (isinstance(t, int) and t == T - 1):
                        l1_x(t + 1, 1 - r)
                if not (isinstance(t, int) and t < 2):
                    turn_x3(t - 2, r)
                if not last:
                    turn_h1(t)
                    l2_x(t, r, (lambda: None) if is_first(t) else (lambda: turn_h2(t - 1)))
                else:
                    turn_h2(t - 1)

            pe.wait_ge(ld2, LD2)
            pe.wait_ge(bones, 4)
            l1_x(0, 0)
            wave(pe, step)
            turn_x3(T - 1, 1)

            pe.wait_ge(ld3, 16 * 5)
            pe.wait_ge(x3all_done, T)
            for j in range(4):
                pe.wait_ge(u_done, count(j - 1))
                for k in range(KT):
                    for h in range(2):
                        rhs = xT_all[:, k, :, h * 32 + j * CB:h * 32 + (j + 1) * CB].rearrange("p t b -> p b t")
                        x = mm(psum[64 * h:64 * h + 64, j % 2, :], ws[:, k, :], rhs, k == 0, k == 1)
                x.then_inc(u_ps, 1)
            pe.wait_ge(ld_toe, 16)
            pe.wait_ge(ld_x3r, 16)
            for i in range(P // 8):
                pe.wait_ge(conv_done[i % 2], count((i - 4) // 2 + 1))
                for j in range(8):
                    for h in range(2):
                        d = h * P + 8 * i + j
                        x = mm(psum[64 * h:64 * h + 64, 2 + i % 4, j * B:(j + 1) * B], toeplitz[0:T, :, d],
                               x3r[0:T, :, d], True, True)
                x.then_inc(conv_ps, 1)

            pe.wait_ge(u_done, 4)
            pe.wait_ge(conv_done[0], 8)
            pe.wait_ge(conv_done[1], 8)
            for j in range(4):
                for h in range(2):
                    for i in range(2):
                        n = 4 * j + 2 * h + i
                        pe.wait_ge(cvt_done, count(2 * (n - 1)))
                        for b in range(4):
                            q = h * 32 + j * CB + i * 4 + b
                            x = pe.transpose(psum[:, n % 2, b * P:(b + 1) * P], conv[:, :, q], ident)
                        x.then_inc(cvt_ps, 1)
                pe.wait_ge(cvt_done, 8 * (j + 1))
                pe.wait_ge(b_done, j)
                pe.wait_ge(ct_done, j)
                pe.wait_ge(x3n_done, T)
                for w in range(2):
                    for k in range(KT):
                        for h in range(2):
                            x = mm(psum[64 * h:64 * h + 64, 6 + w, :], wp[:, k, w * NS:(w + 1) * NS],
                                   cvT[h][:, k, :], k == 0, k == 1)
                x.then_inc(bc_ps, 1)
            for i in range(B // 2):
                if i % 16 == 0:
                    pe.wait_ge(yy_done, 1)
                pe.wait_ge(o_done, count(i - 3))
                h, q = i // 16, i % 16
                y2 = y3.rearrange("p a n -> p (a n)")
                mm(psum[:, i % 4, 0:D], y2[64 * h:64 * h + 64, q * P:(q + 1) * P], wo3[64 * h:64 * h + 64, :],
                   True, True).then_inc(yo_ps, 1)

        def dve_tail(dve):
            tt = dve.tensor_tensor
            dve.wait_ge(ld2, LD2)
            dve.memset(ones, 1.0).then_inc(bones, 1)
            dve.memset(cc, 0.0).then_inc(bones, 1)
            dve.tensor_copy(brest, brow).then_inc(brow_d, 1)
            n = 1
            for i in range(3):
                dve.wait_ge(brow_d, n)
                dve.tensor_copy(bpart, brest).then_inc(brow_d, 1)
                dve.wait_ge(brow_d, n + 1)
                tt(brest, brest, bpart, ALU.subtract).then_inc(brow_d, 1)
                if i == 0:
                    dve.tensor_scalar(bparts, bpart, pick[:, 0:1], None, ALU.mult).then_inc(brow_d, 1)
                else:
                    dve.scalar_tensor_tensor(out=bparts, in0=bpart, scalar=pick[:, i:i + 1], in1=bparts,
                                             op0=ALU.mult, op1=ALU.add).then_inc(brow_d, 1)
                n += 3
            dve.wait_ge(brow_d, n)
            dve.nop().then_inc(bones, 2)

            def cell(t):
                dve.wait_ge(ifo_done, t + 1)
                dve.wait_ge(c_done, t)
                dve.wait_ge(tc_done, t)
                tt(fc, ifo[:, 1, :], cc, ALU.mult).then_inc(fc_done, 1)
                dve.wait_ge(g_done, t + 1)
                tt(ig, ifo[:, 0, :], gg, ALU.mult).then_inc(ig_done, 1)
                dve.wait_ge(fc_done, t + 1)
                dve.wait_ge(ig_done, t + 1)
                tt(cc, fc, ig, ALU.add).then_inc(c_done, 1)

            def layer1(t, r):
                dve.wait_ge(h1t_ps, t + 1)
                hT_ps = psum[:, 4, 0:P].rearrange("p (k b) -> p k b", k=KT)
                dve.wait_ge(h1t_done, t)
                dve.tensor_copy(h1T, hT_ps).then_inc(h1t_done, 1)
                dve.wait_ge(a2_ps, count(t - 1))
                dve.wait_ge(x3_done, count(t - 1))
                dve.wait_ge(x1s_done, t + 1)
                tt(x2s[r], hT_ps, x1s[r], ALU.add).then_inc(x2_done, 1)

            def hidden(t, r):
                dve.wait_ge(tc_done, t + 1)
                dve.wait_ge(h2t_ps, t)
                tt(h2n, ifo[:, 2, :], tc, ALU.mult).then_inc(h2_done, 1)
                dve.wait_ge(h2t_ps, t + 1)
                hT_ps = psum[:, 5, 0:P].rearrange("p (k b) -> p k b", k=KT)
                dve.wait_ge(h2t_done, t)
                dve.tensor_copy(h2T, hT_ps).then_inc(h2t_done, 1)
                dve.wait_ge(x3_ps, count(t - 1))
                dve.wait_ge(x3all_done, count(t - 1))
                dve.wait_ge(x2_done, t + 1)
                tt(x3s[r], hT_ps, x2s[r], ALU.add).then_inc(x3_done, 1)

            def step(t, r, last):
                if not is_first(t):
                    cell(t - 1)
                if not last:
                    layer1(t, r)
                if not is_first(t):
                    hidden(t - 1, 1 - r)

            wave(dve, step)

            dve.wait_ge(ld3, 16 * 5)
            for j in range(4):
                dve.wait_ge(u_ps, j + 1)
                dve.tensor_scalar(u[:, j, :], psum[:, j % 2, :], cols3[:, 0:1], None, ALU.add
                                  ).then_inc(u_done, 1)
            dve.wait_ge(col3, 1)
            dve.scalar_tensor_tensor(out=cols3[:, 9:11], in0=cols3[:, 3:5], scalar=0.0, in1=cols3[:, 7:9],
                                     op0=ALU.max, op1=ALU.add).then_inc(col3, 1)
            dve.wait_ge(col3, 2)
            tt(cols3[:, 11:12], cols3[:, 9:10], cols3[:, 10:11], ALU.mult).then_inc(col3, 1)
            dve.wait_ge(col3, 3)
            dve.tensor_scalar(cols3[:, 12:13], cols3[:, 11:12], -1.0, 1.0, ALU.mult, ALU.add
                              ).then_inc(col3, 1)
            dve.wait_ge(u_ps, 4)
            dd = decay_data.rearrange("p j (b t) -> p (j b) t", t=T)
            dve.memset(dd, 1.0).then_inc(col3, 1)
            dve.wait_ge(col3, 5)
            dve.memset(dd[:, :, 0:1], 0.0).then_inc(col3, 1)
            dve.wait_ge(col3, 6)
            dve.tensor_scalar(dd, dd, cols3[:, 12:13], None, ALU.mult).then_inc(col3, 1)

            for i in range(0, P // 8, 2):
                dve.wait_ge(conv_ps, i + 1)
                dve.tensor_copy(conv[:, 8 * i:8 * i + 8, :], psum[:, 2 + i % 4, :].rearrange("p (d b) -> p d b", b=B)
                                ).then_inc(conv_done[0], 1)
            for j in range(4):
                for h in range(2):
                    for i in range(2):
                        n = 4 * j + 2 * h + i
                        dve.wait_ge(cvt_ps, n + 1)
                        dve.wait_ge(bc_ps, j)
                        for k in range(KT):
                            dve.tensor_scalar(
                                cvT[h][:, k, i * 256:(i + 1) * 256].rearrange("p (b t) -> p b t", t=T),
                                psum[:, n % 2, :].rearrange("p (b k t) -> p b k t", k=KT, t=T)[:, :, k, :],
                                cols3[:, 5 + k:6 + k], None, ALU.add).then_inc(cvt_done, 1)
                dve.wait_ge(bc_ps, j + 1)
                dve.tensor_scalar(bt[:, j, :], psum[:, 6, :], cols3[:, 1:2], None, ALU.add
                                  ).then_inc(b_done, 1)
            dve.wait_ge(ln_done, 1)
            dve.scalar_tensor_tensor(out=bt, in0=bt, scalar=0.0, in1=soft, op0=ALU.max, op1=ALU.add
                                     ).then_inc(sp_done, 1)
            dve.wait_ge(sp_done, 1)
            dve.scalar_tensor_tensor(out=u, in0=u, scalar=cols3[:, 10:11], in1=bt, op0=ALU.mult, op1=ALU.mult
                                     ).then_inc(v_done, 1)
            dve.wait_ge(v_done, 1)
            dve.wait_ge(col3, 7)
            dve.tensor_tensor_scan(st3.rearrange("p j n -> p (j n)"), decay_data.rearrange("p j n -> p (j n)"),
                                   u.rearrange("p j n -> p (j n)"), 0.0, ALU.mult, ALU.add
                                   ).then_inc(scan_done, 1)
            dve.wait_ge(scan_done, 1)
            dve.wait_ge(ct_done, 4)
            tt(y3, st3, ct, ALU.mult).then_inc(yy_done, 1)
            for i in range(B // 2):
                dve.wait_ge(yo_ps, i + 1)
                dve.wait_ge(xb_done, i // 8 + 1)
                tt(x3t[:, i, :], psum[:, i % 4, 0:D], x3t[:, i, :], ALU.add).then_inc(o_done, 1)

        def act_tail(act):
            ac = act.activation

            def gates(t, r):
                a2 = psum[:, 2 + r, :].rearrange("p (g n) -> p g n", g=4)
                act.wait_ge(a2_ps, t + 1)
                act.wait_ge(h2_done, t)
                ac(ifo, a2[:, 0:3], ACT.Sigmoid).then_inc(ifo_done, 1)
                ac(gg, a2[:, 3], ACT.Tanh).then_inc(g_done, 1)

            def layer1(t, r):
                act.wait_ge(a1_ps, t + 1)
                act.wait_ge(h1t_ps, t)
                ac(h1n, psum[:, r, 0:P], ACT.Tanh).then_inc(h1_done, 1)

            def cell_tanh(t):
                act.wait_ge(c_done, t + 1)
                ac(tc, cc, ACT.Tanh).then_inc(tc_done, 1)

            def rows(t, r):
                act.wait_ge(x3_ps, t + 1)
                act.wait_ge(st_x3[r], 8 * (t - r))
                act.wait_ge(st_x3r[r], 8 * (t - r))
                ac(x3n[r][0:B], psum[0:B, 6, 0:D], ACT.Copy).then_inc(x3n_done, 1)

            def step(t, r, last):
                if not is_first(t):
                    gates(t - 1, 1 - r)
                if not last:
                    layer1(t, r)
                if not is_first(t):
                    cell_tanh(t - 1)
                if not (isinstance(t, int) and t < 2):
                    rows(t - 2, r)

            wave(act, step)
            rows(T - 1, 1)

            def log_part(dst, src, n0):
                ac(dst, src, ACT.Abs).then_inc(abs_done, 1)
                act.wait_ge(abs_done, n0 + 1)
                ac(dst, dst, ACT.Exp, scale=-1.0).then_inc(ex_done, 1)
                act.wait_ge(ex_done, n0 + 1)
                return ac(dst, dst, ACT.Ln, bias=1.0)

            act.wait_ge(ld3, 16 * 5)
            log_part(cols3[:, 7:9], cols3[:, 3:5], 0).then_inc(col3, 1)
            for i in range(1, P // 8, 2):
                act.wait_ge(conv_ps, i + 1)
                ac(conv[:, 8 * i:8 * i + 8, :], psum[:, 2 + i % 4, :].rearrange("p (d b) -> p d b", b=B), ACT.Copy
                   ).then_inc(conv_done[1], 1)
            for j in range(4):
                act.wait_ge(bc_ps, j + 1)
                ac(ct[:, j, :], psum[:, 7, :], ACT.Tanh, bias=cols3[:, 2:3]).then_inc(ct_done, 1)
            act.wait_ge(b_done, 4)
            log_part(soft, bt, 1).then_inc(ln_done, 1)

        def pool_tail(pool):
            def stage(t, r):
                pool.wait_ge(x2_done, count(t - 1))
                pool.wait_ge(a1_ps, count(t - 1))
                apart(pool)
                pool.tensor_copy(x1s[r], xT_all[:, :, bass.ds(t, 1), :].rearrange("p k o b -> p k (o b)")
                                 ).then_inc(x1s_done, 1)

            def keep(t, r):
                pool.wait_ge(x3_done, t + 1)
                apart(pool)
                pool.tensor_copy(xT_all[:, :, bass.ds(t, 1), :].rearrange("p k o b -> p k (o b)"), x3s[r]
                                 ).then_inc(x3all_done, 1)

            pool.wait_ge(ld2, LD2)
            stage(0, 0)
            stage(1, 1)
            stage(2, 0)
            stage(3, 1)
            keep(0, 0)
            keep(1, 1)
            with pool.Fori(2, T // 2) as i:
                stage(2 * i, 0)
                keep(2 * i - 2, 0)
                stage(2 * i + 1, 1)
                keep(2 * i - 1, 1)
            keep(T - 2, 0)
            keep(T - 1, 1)
            for q in range(4):
                pool.wait_ge(ld_x3t, 16 * 5)
                pool.tensor_tensor(x3t[:, 8 * q:8 * q + 8, :], x3t[:, 8 * q:8 * q + 8, :],
                                   bo_row.unsqueeze(1).broadcast_to([P, 8, D]), ALU.add
                                   ).then_inc(xb_done, 1)


        block = ctx.enter_context(nc.Block())

        def pipeline(eng, first, step):
            first()
            step(0, None, 1)
            step(1, 0, 2)
            with eng.Fori(2, NCH - 1) as c:
                step(c, c - 1, c + 1)
            step(NCH - 1, NCH - 2, None)
            step(None, NCH - 1, None)

        @block.sync
        def _(sp):
            def load(landed, dst, src):
                sp.dma_start(dst, src).then_inc(landed, 16)

            for dst, dram in loads:
                load(ld_w, dst, dram)
            sp.wait_ge(vcs_done, NK)
            sp.dma_start(vcs_dram.rearrange("j b n -> b j n"), vcs_nat).then_inc(st_vcs, 16)
            sp.wait_ge(st_vcs, 16)

            def load_vcs(c):
                apart(sp)
                src = vcs_dram[:, bass.ds(c * CB, CB), :]
                for h in range(H):
                    sp.dma_start(vcs_rep[4 * h:4 * h + 4], src).then_inc(ld_vcs, 16)

            def spread_k(c):
                apart(sp)
                sp.wait_ge(kt_done, KT * (c + 1))
                apart(sp)
                sp.wait_ge(scores_ps, PAIRS * c)
                for h in range(HG):
                    sp.dma_start(k_bd[diag_rows(h), :, h, :], kT[diag_rows(h)]).then_inc(ld_kbd, 16)

            load_vcs(0)
            sp.wait_ge(zero_done, 1)
            spread_k(0)

            def step(c, q, n):
                if n is not None:
                    sp.wait_ge(v_ps, 2 * n)
                    apart(sp)
                    load(ld_zt, zT, a["xT"].rearrange(kp, p=P)[:, :, bass.ds(n * CN, CN)])
                if q is not None:
                    sp.wait_ge(iz_done, PAIRS * q)
                    apart(sp)
                    load(ld_zn, z_nat, a["x_nat"].rearrange("(c i p) n -> c p i n", i=PAIRS, p=P)[q])
                    sp.wait_ge(xout_done, KT * q)
                    apart(sp)
                    load(ld_xr, xres, a["xT"].rearrange(kp, p=P)[:, :, bass.ds(q * CN, CN)])
                if n is not None:
                    sp.wait_ge(vcsbd_done, n)
                    load_vcs(n)
                    spread_k(n)

            pipeline(sp, lambda: None, step)
            sp_tail(sp)

        @block.tensor
        def _(pe):
            pe.wait_ge(ld_w, LD_W)

            def mm(o, l, r, start, stop):
                return pe.matmul(o, l, r, start=start, stop=stop)

            def setup():
                for i, (wt, g0) in enumerate(((wog_is, 0), (wog_cs, 2))):
                    for m in range(KT):
                        for k in range(KT):
                            x = mm(psum[:, 4 + i, m * D:(m + 1) * D], wt[:, k, m * P:(m + 1) * P], wgate[:, g0 + k, :],
                                   k == 0, k == 1)
                x.then_inc(gm_ps, 1)
                for jk in range(NK * KT):
                    for k in range(KT):
                        x = mm(psum[:, 6, jk * B:(jk + 1) * B], wg[:, k, jk * P:(jk + 1) * P], condT[:, k, :],
                               k == 0, k == 1)
                x.then_inc(gt_ps, 1)
                for i, (w, b) in enumerate(((w_is, "bv_is"), (w_cs, "bv_cs"))):
                    for m in range(KT):
                        for k in range(KT):
                            x = mm(psum[:, 7, 2 * i + m:2 * i + m + 1], w[:, k, m * P:(m + 1) * P], col(b, k),
                                   k == 0, k == 1)
                x.then_inc(cst_ps, 1)
                pe.wait_ge(gt_done, 1)
                for g in range(KT):
                    for k in range(KT):
                        x = mm(psum[:, 6, g * 256:(g + 1) * 256], wkcs[:, k, g * P:(g + 1) * P], gtT[:, :, k, :],
                               k == 0, k == 1)
                x.then_inc(kcs_ps, 1)
                for j in range(NK):
                    for k in range(KT):
                        x = mm(psum[0:B, j // 2, (j % 2) * D:(j % 2 + 1) * D], gtT[:, j, k, :], wvcs[:, k, :],
                               k == 0, k == 1)
                x.then_inc(vcs_ps, 1)
                pe.wait_ge(cst_done, 2)
                for i, c_ in enumerate((c_is, c_cs)):
                    for k in range(KT):
                        x = mm(psum[:, 2 + i, k * P:(k + 1) * P], c_[:, k:k + 1].broadcast_to([P, P]), ident, True, True)
                for i, c_ in enumerate((c_is, c_cs)):
                    for k in range(KT):
                        x = mm(psum[:, 3, 256:512], c_[:, k:k + 1].broadcast_to([P, P]), wgate[:, 2 * i + k, :],
                               i + k == 0, i + k == 2)
                x.then_inc(row_ps, 1)

            def qkv(n, q):
                pe.wait_ge(ld_zt, 16 * n)
                if q is not None:
                    pe.wait_ge(y_done, PAIRS * (q + 1))
                else:
                    pe.wait_ge(v0_done, 2 * n)
                    pe.wait_ge(v1_done, 2 * n)
                    pe.wait_ge(qt_done, KT * n)
                for w, bank in ((wk, 6), (wq, 4)):
                    for g in range(KT):
                        for k in range(KT):
                            x = mm(psum[:, bank + g, :], w[:, k, g * P:(g + 1) * P], zT[:, k, :], k == 0, k == 1)
                        x.then_inc(kq_ps, 1)
                for i in range(2):
                    pe.wait_ge(kt_done, KT * n + i + 1)
                    for b in range(4):
                        for k in range(KT):
                            for h2 in range(2):
                                r = wv[:, k, :].rearrange("p (j h e) -> p h j e", h=2, e=DH)[:, h2]
                                x = mm(psum[h2 * 64:h2 * 64 + 64, 6 + i, b * P:(b + 1) * P],
                                       zT[:, k, (4 * i + b) * T:(4 * i + b + 1) * T], r, k == 0, k == 1)
                    x.then_inc(v_ps, 1)

            def scores(c, p):
                if p == 0:
                    pe.wait_ge(qt_done, KT * (c + 1))
                    pe.wait_ge(ld_kbd, 16 * HG * (c + 1))
                    pe.wait_ge(kcsbd_done, KT * (c + 1))
                pe.wait_ge(pt0_done, PAIRS * c + p)
                pe.wait_ge(pt1_done, PAIRS * c + p)
                pe.wait_ge(rt_done, PAIRS * c + p)
                for g in range(KT):
                    for half in range(2):
                        mm(s_ps[half * 64:half * 64 + 64, g, :], mask_l[:],
                           mask_r[:].unsqueeze(1).broadcast_to([P, HG, T]), True, False)
                    for half in range(2):
                        b = 2 * p + half
                        x = mm(s_ps[half * 64:half * 64 + 64, g, :], qT[:, g, b * T:(b + 1) * T],
                               k_bd[:, g, :, b * T:(b + 1) * T], False, True)
                for g in range(KT):
                    for half in range(2):
                        b = 2 * p + half
                        x = mm(cs_ps[half * 64:half * 64 + 64, g * 32:(g + 1) * 32], qT[:, g, b * T:(b + 1) * T],
                               kcs_bd[:, g, :, b * NK:(b + 1) * NK], True, True)
                x.then_inc(scores_ps, 1)

            def transposes(c, p):
                pe.wait_ge(exp_done, PAIRS * c + p + 1)
                for i in range(2 * PAIRS):
                    pe.transpose(pT_ps[:, i, :], e[:, i * P:(i + 1) * P], ident)
                pe.wait_ge(csp_done, PAIRS * c + p + 1)
                pe.wait_ge(cspt_done, PAIRS * c + p)
                apart(pe)
                pe.transpose(cspT_ps, cs_e.rearrange("p a b -> p (a b)"), ident)
                pe.wait_ge(rrep_done, PAIRS * c + p + 1)
                pe.wait_ge(rt_done, PAIRS * c + p)
                for g in range(KT):
                    x = pe.transpose(rT_ps[:, g, :], rrep[:, g * P:(g + 1) * P], ident)
                x.then_inc(pt_ps, 1)

            def pv(c, p):
                if p == 0:
                    pe.wait_ge(v0_done, 2 * (c + 1))
                    pe.wait_ge(v1_done, 2 * (c + 1))
                    pe.wait_ge(vcsbd_done, c + 1)
                pe.wait_ge(pt0_done, PAIRS * c + p + 1)
                pe.wait_ge(pt1_done, PAIRS * c + p + 1)
                pe.wait_ge(ctx_done, PAIRS * c + p)
                pe.wait_ge(csx_done, PAIRS * c + p)
                for g in range(KT):
                    for half in range(2):
                        for j in range(4):
                            mm(ctx_ps[32 * j:32 * j + 32, g, half * 64:half * 64 + 64],
                               v_bd[:, 2 * p + half, 4 * g + j].rearrange("p h e -> p (h e)"), pT[:, 4 * g + j, half * 64:half * 64 + 64],
                               True, True)
                pe.wait_ge(cspt_done, PAIRS * c + p + 1)
                for g in range(KT):
                    for half in range(2):
                        x = mm(csx_ps[:, g, half * 64:half * 64 + 64], vcs_bd[0:64, 2 * p + half, g * P:(g + 1) * P],
                               cs_pT[0:64, half * 64:half * 64 + 64], True, True)
                x.then_inc(pv_ps, 1)

            def project(q, i, nq):
                if i == 0:
                    pe.wait_ge(ctx_done, PAIRS * (q + 1))
                    pe.wait_ge(csx_done, PAIRS * (q + 1))
                    pe.wait_ge(x2t_done, KT * q)
                    pe.wait_ge(qt_done, KT * nq)
                if i == 1:
                    pe.wait_ge(xout_done, KT * q)
                    pe.wait_ge(v0_done, 2 * nq)
                    pe.wait_ge(v1_done, 2 * nq)
                if i >= 2:
                    pe.wait_ge(abias_done, count(PAIRS * q + i - 1))
                bank = 4 + 2 * (i % 2)
                t = slice(i * P, (i + 1) * P)
                for k in range(KT):
                    mm(psum[:, bank, 0:D], ctxT[:, k, t], w_is[:, k, 0:D], k == 0, k == 1)
                for k in range(KT):
                    mm(psum[:, bank, D:2 * D], csxT[:, k, t], w_cs[:, k, 0:D], k == 0, k == 1)
                for k in range(KT):
                    mm(psum[:, bank + 1, 0:D], ctxT[:, k, t], w_is[:, k, D:2 * D], k == 0, False)
                for k in range(KT):
                    x = mm(psum[:, bank + 1, 0:D], csxT[:, k, t], w_cs[:, k, D:2 * D], False, k == 1)
                x.then_inc(a_ps, 1)

            def turn(turned):
                for k in range(KT):
                    for i in range(PAIRS):
                        x = pe.transpose(psum[:, 4 + k, i * P:(i + 1) * P], lnb[:, i, k * P:(k + 1) * P], ident)
                    x.then_inc(turned, 1)

            def ff_up(q, i):
                if i == 0:
                    pe.wait_ge(x1t_done, KT * (q + 1))
                    pe.wait_ge(abias_done, PAIRS * (q + 1))
                if i >= 4:
                    pe.wait_ge(gelu_done, count(FT * q + i - 3))
                for k in range(KT):
                    x = mm(psum[:, 4 + (i + 2) % 4, :], w1[:, k, i * P:(i + 1) * P], ffT[:, k, :], k == 0, k == 1)
                x.then_inc(ff_ps, 1)

            def ff_down(q, i):
                if i == 0:
                    pe.wait_ge(gelu_done, FT * (q + 1))
                for k in range(FT):
                    x = mm(psum[:, 4 + (i + 2) % 4, 0:D], hT[:, k, i * P:(i + 1) * P], w2[:, k, :], k == 0, k == FT - 1)
                x.then_inc(c_ps, 1)

            def out_proj(q, nq):
                pe.wait_ge(x2t_done, KT * (q + 1))
                pe.wait_ge(v0_done, 2 * nq)
                pe.wait_ge(v1_done, 2 * nq)
                for m in range(KT):
                    for k in range(KT):
                        x = mm(psum[:, 6 + m, :], wout[:, k, m * P:(m + 1) * P], ffT[:, k, :], k == 0, k == 1)
                    x.then_inc(wout_ps, 1)

            def step(c, q, n):
                nq = n if n is not None else NCH
                after = n + 1 if n is not None else NCH
                for p in range(PAIRS):
                    if c is not None:
                        scores(c, p)
                    if q is not None:
                        if p == 0:
                            for i in range(PAIRS):
                                project(q, i, nq)
                        if p == 1:
                            pe.wait_ge(abias_done, PAIRS * q + 3)
                            pe.wait_ge(xh1, PAIRS * (q + 1))
                            turn(x1t_ps)
                            for i in range(4):
                                ff_up(q, i)
                        if p == 2:
                            for i in range(4, 8):
                                ff_up(q, i)
                            for i in range(2):
                                ff_down(q, i)
                        if p == 3:
                            for i in range(2, 4):
                                ff_down(q, i)
                    if c is not None:
                        transposes(c, p)
                        pv(c, p)
                if n is not None:
                    qkv(n, q)
                if q is not None:
                    pe.wait_ge(qt_done, KT * after)
                    pe.wait_ge(y_done, PAIRS * (q + 1))
                    pe.wait_ge(xh2, PAIRS * (q + 1))
                    turn(x2t_ps)
                    out_proj(q, after)

            def first():
                setup()
                pe.wait_ge(gt_done, 2)
                pe.wait_ge(row_done, 2)
                pe.wait_ge(kcs_done, 2)
                pe.wait_ge(pe_w, 2)
                pe.wait_ge(mask_done, 2)
                qkv(0, None)

            pipeline(pe, first, step)
            pe_tail(pe)

        def layer_norm(dve, q, done, ks):
            st, mvs, ves, rs, xh = ks
            for i in range(PAIRS):
                dve.wait_ge(done, PAIRS * q + i + 1)
                dve.bn_stats(bn6[:, i, :], lnb[:, i, :]).then_inc(st, 1)
            for i in range(PAIRS):
                dve.wait_ge(st, PAIRS * q + i + 1)
                apart(dve)
                dve.bn_aggr(mv[:, i, :], bn6[:, i, :]).then_inc(mvs, 1)
            dve.wait_ge(mvs, PAIRS * (q + 1))
            dve.tensor_scalar(ve, mv[:, :, 1], EPS, None, ALU.add).then_inc(ves, 1)
            dve.wait_ge(rs, q + 1)
            for i in range(PAIRS):
                dve.tensor_scalar(lnb[:, i, :], lnb[:, i, :], mv[:, i, 0:1], rstd[:, i:i + 1], ALU.subtract,
                                  ALU.mult).then_inc(xh, 1)

        @block.vector
        def _(dve):
            tt, ts = dve.tensor_tensor, dve.tensor_scalar

            def setup():
                dve.memset(neg_half, -0.5).then_inc(half_done, 1)
                dve.memset(v_bd, 0.0).then_inc(half_done, 1)
                dve.wait_ge(ld_w, LD_W)
                tt(x1_b_row, x1_b_row, x1_res[:, 0, :], ALU.add).then_inc(half_done, 1)
                dve.tensor_copy(mask_l[:], ident[:, 0:T]).then_inc(mask_done, 1)
                dve.tensor_copy(mask_r[:], mask_f).then_inc(mask_done, 1)
                dve.wait_ge(gm_ps, 1)
                for i, w in enumerate((w_is, w_cs)):
                    dve.tensor_copy(w[:, :, D:2 * D], psum[:, 4 + i, :].rearrange("p (m n) -> p m n", m=KT)
                                    ).then_inc(pe_w, 1)
                dve.wait_ge(gt_ps, 1)
                tt(gtT.rearrange("p j k b -> p (j k) b"), psum[:, 6, :].rearrange("p (a b) -> p a b", b=B),
                   bgc.unsqueeze(2).broadcast_to([P, NK * KT, B]), ALU.add).then_inc(gt_done, 1)
                dve.wait_ge(cst_ps, 1)
                tt(c_is, psum[:, 7, 0:2], cols[:, COL["bo_is"]:COL["bo_is"] + 2], ALU.add).then_inc(cst_done, 1)
                tt(c_cs, psum[:, 7, 2:4], cols[:, COL["bo_cs"]:COL["bo_cs"] + 2], ALU.add).then_inc(cst_done, 1)
                dve.wait_ge(kcs_ps, 1)
                for g in range(KT):
                    ts(kcsT[:, g].rearrange("p b j -> p j b"),
                       psum[:, 6, g * 256:(g + 1) * 256].rearrange("p (j b) -> p j b", b=B),
                       col("bk_cs", g), None, ALU.add).then_inc(kcs_done, 1)
                dve.wait_ge(vcs_ps, 1)
                for j in range(NK):
                    dve.tensor_copy(vcs_nat[:, j, :], psum[0:B, j // 2, (j % 2) * D:(j % 2 + 1) * D]
                                    ).then_inc(vcs_done, 1)
                dve.nop().then_inc(gt_done, 1)
                dve.wait_ge(row_ps, 1)
                dve.tensor_copy(bias3[:, 0:2 * D].rearrange("p (i n) -> p i n", i=2),
                                psum[:, 2:4, 0:D]).then_inc(row_done, 1)
                tt(bias3[:, 2 * D:3 * D], psum[:, 3, D:2 * D], bias3[:, 2 * D:3 * D], ALU.add
                   ).then_inc(row_done, 1)
                dve.wait_ge(st_vcs, 16)
                dve.memset(k_bd, 0.0).then_inc(zero_done, 1)

            def qkv(n):
                dve.wait_ge(scores_ps, PAIRS * n)
                for g in range(KT):
                    dve.wait_ge(kq_ps, 4 * n + 3 + g)
                    ts(qT[:, g, :], psum[:, 4 + g, :], col("bq", g), None, ALU.add).then_inc(qt_done, 1)
                dve.wait_ge(pv_ps, PAIRS * n)
                for i in range(2):
                    dve.wait_ge(v_ps, 2 * n + i + 1)
                    dve.tensor_copy(v_bd[64:128, 4 * i:4 * i + 4, :, 1, :], psum[64:128, 6 + i, :].rearrange(
                        "p (b j e) -> p b j e", b=4, e=DH)).then_inc(v1_done, 1)

            def softmax(c, p):
                u = PAIRS * c + p + 1
                s3 = s_ps.rearrange("p g (h k) -> p (g h) k", k=T)
                e3 = e.rearrange("p (h k) -> p h k", k=T)
                cs3 = cs_ps.rearrange("p (h j) -> p h j", j=NK)
                dve.wait_ge(scores_ps, u)
                dve.tensor_reduce(nmax, s3, AX.X, ALU.max).then_inc(nmax_done, 1)
                dve.tensor_reduce(csm, cs3, AX.X, ALU.max).then_inc(csmax_done, 1)
                dve.wait_ge(nmax_done, u)
                dve.wait_ge(pt_ps, count(u - 1))
                tt(e3, s3, nmax.unsqueeze(2).broadcast_to([P, H, T]), ALU.subtract).then_inc(sub_done, 1)
                dve.wait_ge(csmax_done, u)
                tt(cs_e, cs3, csm.unsqueeze(2).broadcast_to([P, H, NK]), ALU.subtract).then_inc(cssub_done, 1)
                dve.wait_ge(exp_done, u)
                dve.tensor_reduce(rsum, e3, AX.X, ALU.add).then_inc(rsum_done, 1)
                dve.wait_ge(csexp_done, u)
                dve.tensor_reduce(css, cs_e, AX.X, ALU.add).then_inc(cssum_done, 1)
                dve.wait_ge(rsum_done, u)
                dve.reciprocal(rinv, rsum).then_inc(rinv_done, 1)
                dve.wait_ge(cssum_done, u)
                dve.reciprocal(css, css).then_inc(csrec_done, 1)
                dve.wait_ge(csrec_done, u)
                tt(cs_e, cs_e, css.unsqueeze(2).broadcast_to([P, H, NK]), ALU.mult).then_inc(csp_done, 1)

            def copy_pT(c, p):
                dve.wait_ge(pt_ps, PAIRS * c + p + 1)
                dve.wait_ge(pv_ps, PAIRS * c + p)
                dve.tensor_copy(pT[:, 0:4, :], pT_ps[:, 0:4, :]).then_inc(pt0_done, 1)

            def context(c, p):
                dve.wait_ge(pv_ps, PAIRS * c + p + 1)
                dve.wait_ge(rt_done, PAIRS * c + p + 1)
                if p == 0:
                    dve.wait_ge(a_ps, PAIRS * c)
                tt(ctxT[:, :, p * P:(p + 1) * P], ctx_ps, rT, ALU.mult).then_inc(ctx_done, 1)

            def add_bias(q, i):
                dve.wait_ge(a_ps, PAIRS * q + i + 1)
                dve.wait_ge(f_done, count(PAIRS * q + i - 1))
                tt(proj3[:, i % 2], psum[:, 4 + 2 * (i % 2):6 + 2 * (i % 2), :].rearrange("p a n -> p (a n)")[:, 0:3 * D],
                   bias3, ALU.add).then_inc(abias_done, 1)

            def fuse(q, i):
                u = PAIRS * q + i + 1
                x3 = proj3[:, i % 2].rearrange("p (a n) -> p a n", a=3)
                dve.wait_ge(th_done, u)
                dve.wait_ge(dd_done, u)
                dve.scalar_tensor_tensor(out=x3[:, 1], in0=x3[:, 2], scalar=1.0, in1=x3[:, 1], op0=ALU.add,
                                         op1=ALU.mult).then_inc(gm_done, 1)
                dve.wait_ge(gm_done, u)
                dve.wait_ge(iz_done, u)
                if i == 0:
                    dve.wait_ge(x2t_ps, KT * q)
                dve.scalar_tensor_tensor(out=lnb[:, i, :], in0=x3[:, 1], scalar=0.5, in1=x3[:, 0], op0=ALU.mult,
                                         op1=ALU.add).then_inc(f_done, 1)

            def copy_xT(q, turned, g, b, copied):
                for k in range(KT):
                    dve.wait_ge(turned, KT * q + k + 1)
                    ts(ffT[:, k, :], psum[:, 4 + k, :], col(g, k), col(b, k), ALU.mult, ALU.add
                       ).then_inc(copied, 1)

            def add_ff(q, i):
                dve.wait_ge(c_ps, PAIRS * q + i + 1)
                if i == 0:
                    dve.wait_ge(x1r_done, q + 1)
                    dve.wait_ge(x1t_ps, KT * (q + 1))
                tt(lnb[:, i, :], psum[:, 4 + (i + 2) % 4, 0:D], x1_res[:, i, :], ALU.add).then_inc(y_done, 1)

            def residual(q):
                dve.wait_ge(ld_xr, 16 * (q + 1))
                for m in range(KT):
                    dve.wait_ge(wout_ps, KT * q + m + 1)
                    dve.scalar_tensor_tensor(
                        out=xT_all[:, m, :, bass.ds(q * CB, CB)].rearrange("p t b -> p b t"),
                        in0=psum[:, 6 + m, :].rearrange("p (b t) -> p b t", t=T), scalar=col("bout", m),
                        in1=xres[:, m, :].rearrange("p (b t) -> p b t", t=T), op0=ALU.add,
                        op1=ALU.add).then_inc(xout_done, 1)

            def step(c, q, n):
                for p in range(PAIRS):
                    if c is not None:
                        softmax(c, p)
                    if q is not None:
                        if p == 0:
                            add_bias(q, 0)
                            add_bias(q, 1)
                            fuse(q, 0)
                            add_bias(q, 2)
                            fuse(q, 1)
                            add_bias(q, 3)
                            fuse(q, 2)
                        if p == 1:
                            dve.wait_ge(wout_ps, KT * q)
                            copy_xT(q, x1t_ps, "ln1_g", "ln1_b", x1t_done)
                        if p == 2:
                            for i in range(2):
                                add_ff(q, i)
                        if p == 3:
                            for i in range(2, 4):
                                add_ff(q, i)
                    if c is not None:
                        copy_pT(c, p)
                    if q is not None and p == 0:
                        fuse(q, 3)
                    if c is not None:
                        context(c, p)
                    if q is not None and p == 0:
                        layer_norm(dve, q, f_done, (st1, mv1, ve1, rstd1, xh1))
                    if q is not None and p == 3:
                        layer_norm(dve, q, y_done, (st2, mv2, ve2, rstd2, xh2))
                if n is not None:
                    qkv(n)
                if q is not None:
                    dve.wait_ge(ff_ps, FT * (q + 1))
                    copy_xT(q, x2t_ps, "ln2_g", "ln2_b", x2t_done)
                    residual(q)

            def first():
                setup()
                dve.wait_ge(half_done, 3)
                qkv(0)

            pipeline(dve, first, step)
            dve_tail(dve)

        @block.scalar
        def _(act):
            ac = act.activation

            def qkv(n):
                act.wait_ge(ld_kbd, 16 * HG * n)
                for g in range(KT):
                    act.wait_ge(kq_ps, 4 * n + g + 1)
                    ac(kT[:, g, :], psum[:, 6 + g, :], ACT.Identity, bias=col("bk_is", g)).then_inc(kt_done, 1)
                act.wait_ge(pv_ps, PAIRS * n)
                for i in range(2):
                    act.wait_ge(v_ps, 2 * n + i + 1)
                    ac(v_bd[0:64, 4 * i:4 * i + 4, :, 0, :], psum[0:64, 6 + i, :].rearrange(
                        "p (b j e) -> p b j e", b=4, e=DH), ACT.Copy).then_inc(v0_done, 1)

            def exps(c, p):
                u = PAIRS * c + p + 1
                act.wait_ge(sub_done, u)
                ac(e, e, ACT.Exp, scale=SCALE).then_inc(exp_done, 1)
                act.wait_ge(cssub_done, u)
                ac(cs_e, cs_e, ACT.Exp, scale=SCALE).then_inc(csexp_done, 1)

            def copies(c, p):
                u = PAIRS * c + p + 1
                act.wait_ge(pt_ps, u)
                act.wait_ge(pv_ps, count(u - 1))
                ac(pT[:, 4:8, :], pT_ps[:, 4:8, :], ACT.Copy).then_inc(pt1_done, 1)
                ac(cs_pT[0:64, :], cspT_ps, ACT.Copy).then_inc(cspt_done, 1)
                act.wait_ge(ctx_done, count(u - 1))
                ac(rT, rT_ps, ACT.Copy).then_inc(rt_done, 1)
                act.wait_ge(pv_ps, u)
                act.wait_ge(ctx_done, u)
                if p == 0:
                    act.wait_ge(a_ps, PAIRS * c)
                ac(csxT[:, :, p * P:(p + 1) * P], csx_ps, ACT.Copy).then_inc(csx_done, 1)

            def gate(q, i):
                act.wait_ge(abias_done, PAIRS * q + i + 1)
                g = proj3[:, i % 2, 2 * D:3 * D]
                ac(g, g, ACT.Tanh, scale=0.5).then_inc(th_done, 1)

            def gelu(q, i):
                act.wait_ge(ff_ps, FT * q + i + 1)
                if i == 0:
                    act.wait_ge(c_ps, PAIRS * q)
                c0 = COL["b1"] + i
                ac(hT[:, i, :], psum[:, 4 + (i + 2) % 4, :], ACT.Gelu, bias=cols[:, c0:c0 + 1]
                   ).then_inc(gelu_done, 1)

            def step(c, q, n):
                for p in range(PAIRS):
                    if c is not None:
                        exps(c, p)
                    if q is not None:
                        if p == 0:
                            for i in range(PAIRS):
                                gate(q, i)
                        if p in (1, 2):
                            for i in range(4 * p - 4, 4 * p):
                                gelu(q, i)
                    if c is not None:
                        copies(c, p)
                if n is not None:
                    qkv(n)

            def first():
                act.wait_ge(half_done, 2)
                act.wait_ge(ld_w, LD_W)
                qkv(0)

            pipeline(act, first, step)
            act_tail(act)

        @block.gpsimd
        def _(pool):
            tt = pool.tensor_tensor

            def spread_cond(c):
                pool.wait_ge(scores_ps, PAIRS * c)
                for g in range(KT):
                    tt(kcs_bd[:, g], kcsT[:, g, bass.ds(c * CB, CB), :].rearrange("p b j -> p (b j)").unsqueeze(1)
                       .broadcast_to([P, HG, CB * NK]), hmask.unsqueeze(2).broadcast_to([P, HG, CB * NK]),
                       ALU.mult).then_inc(kcsbd_done, 1)
                pool.wait_ge(pv_ps, PAIRS * c)
                pool.wait_ge(ld_vcs, 16 * H * (c + 1))
                tt(vcs_bd[0:64], vcs_rep[0:64], vmask[0:64].unsqueeze(1).broadcast_to([64, CB, D]),
                   ALU.mult).then_inc(vcsbd_done, 1)

            def spread_rinv(c, p):
                pool.wait_ge(rinv_done, PAIRS * c + p + 1)
                pool.wait_ge(pt_ps, PAIRS * c + p)
                apart(pool)
                pool.tensor_copy(rrep.rearrange("p (h e) -> p h e", e=DH), rinv.unsqueeze(2).broadcast_to([P, H, DH])
                                 ).then_inc(rrep_done, 1)

            def step(c, q, n):
                for p in range(PAIRS):
                    if c is not None:
                        spread_rinv(c, p)
                    if q is not None:
                        tail(q, p)
                if n is not None:
                    spread_cond(n)

            def tail(q, p):
                if p == 0:
                    for i in range(PAIRS):
                        u = PAIRS * q + i + 1
                        x3 = proj3[:, i % 2].rearrange("p (a n) -> p a n", a=3)
                        pool.wait_ge(abias_done, u)
                        tt(x3[:, 1], x3[:, 1], x3[:, 0], ALU.subtract).then_inc(dd_done, 1)
                        pool.wait_ge(dd_done, u)
                        if i == 0:
                            pool.wait_ge(ld_zn, 16 * (q + 1))
                        tt(x3[:, 0], x3[:, 0], z_nat[:, i, :], ALU.add).then_inc(iz_done, 1)
                    pool.wait_ge(ve1, q + 1)
                    tt(rstd, ve, neg_half, ALU.pow).then_inc(rstd1, 1)
                if p == 1:
                    pool.wait_ge(xh1, PAIRS * (q + 1))
                    pool.wait_ge(y_done, PAIRS * q)
                    tt(x1_res, lnb, ln1_g_row.unsqueeze(1).broadcast_to([P, PAIRS, D]), ALU.mult
                       ).then_inc(x1g_done, 1)
                    pool.wait_ge(x1g_done, q + 1)
                    tt(x1_res, x1_res, x1_b_row.unsqueeze(1).broadcast_to([P, PAIRS, D]), ALU.add
                       ).then_inc(x1r_done, 1)
                if p == 3:
                    pool.wait_ge(ve2, q + 1)
                    tt(rstd, ve, neg_half, ALU.pow).then_inc(rstd2, 1)

            def first():
                pool.wait_ge(ld_w, LD_W)
                pool.wait_ge(half_done, 3)
                pool.wait_ge(kcs_done, 2)
                spread_cond(0)

            pipeline(pool, first, step)
            pool_tail(pool)


def kernel(**inputs):
    import numpy as np
    import concourse.bacc as bacc
    from concourse import mybir as my
    from concourse.bass_utils import run_bass_kernel_spmd

    nc = bacc.Bacc("TRN2", target_bir_lowering=False, num_devices=1)
    arrays = {n: np.asarray(v) for n, v in inputs.items()}
    x, cond = arrays.pop("x"), arrays.pop("cond_1024")
    arrays["xT"] = np.ascontiguousarray(x.reshape(-1, 256).T)
    arrays["x_nat"] = np.ascontiguousarray(x.reshape(-1, 256))
    arrays["condT"] = np.ascontiguousarray(cond.T)
    arrays["cond_pad"] = np.concatenate([np.zeros((64, 256), x.dtype), cond[::-1]])
    arrays["Wo_isT"] = np.ascontiguousarray(arrays["L0_cond_Wo_is"].T)
    arrays["Wo_csT"] = np.ascontiguousarray(arrays["L0_cond_Wo_cs"].T)
    def columns(*names):
        return np.ascontiguousarray(np.concatenate([arrays[n].reshape(-1, 128).T for n in names], 1))

    arrays["cols0"] = columns(*["L0_cond_" + n for n in COLS0])
    arrays["bg_cols"] = columns("L0_cond_bg")
    two = {n: np.tile(arrays[n].reshape(-1, 64), (1, 2)).T for n in ("L3_cond_bs", "L3_cond_bp", "L3_cond_A_log",
                                                                    "L3_cond_dt_log")}
    arrays["cols3"] = np.ascontiguousarray(np.concatenate([*two.values(), columns("L3_cond_conv_b")], 1))
    p = np.arange(128)
    arrays["ident"] = np.eye(128, dtype=np.float32)
    arrays["hmask"] = (p[:, None] // 16 == np.arange(8)[None]).astype(np.float32)
    arrays["vmask"] = (np.arange(64)[:, None] // 4 == np.arange(256)[None] // 16).astype(np.float32)
    arrays["pick"] = (p[:, None] == np.arange(3)[None]).astype(np.float32)
    q = np.arange(64)
    arrays["mask"] = np.where((p[:, None] < q[None]) & (p[:, None] < 64), -1e30, 0.0).astype(np.float32)
    used = COLS0 + ("bg",)
    for n in used:
        if n not in ("ln1_g", "ln1_b"):
            del arrays["L0_cond_" + n]
    for n in ("L3_cond_bs", "L3_cond_bp", "L3_cond_A_log", "L3_cond_dt_log", "L3_cond_conv_b"):
        del arrays[n]
    drams = {n: nc.dram_tensor(f"in_{n}", v.shape, my.dt.from_np(v.dtype), kind="ExternalInput").ap()
             for n, v in arrays.items()}
    out = nc.dram_tensor("out_0", (64, 64, 256), my.dt.float32, kind="ExternalOutput").ap()
    cond_resid_kernel(nc, drams, out)
    r = run_bass_kernel_spmd(nc, [{f"in_{n}": v for n, v in arrays.items()}], core_ids=[0])
    return r.results[0]["out_0"]
```

```python
from contextlib import ExitStack

import concourse.bass as bass
from concourse import mybir

ALU = mybir.AluOpType
ACT = mybir.ActivationFunctionType
AX = mybir.AxisListType
F32 = mybir.dt.float32
BF16 = mybir.dt.bfloat16

P = 128
B, T, D = 64, 64, 256
H, DH, NK = 16, 16, 4
KT = D // P
HG = P // DH
CB = 8
CN = CB * T
NCH = B // CB
PAIRS = CB // 2
FF = 4 * D
FT = FF // P
NS = 64
SCALE = DH ** -0.5
EPS = 1e-5
COLS0 = ("bq", "bk_is", "bv_is", "bo_is", "bv_cs", "bo_cs", "bk_cs", "ln1_g", "ln1_b", "ln2_g", "ln2_b", "bout", "b1")


def cond_resid_kernel(nc, a, out):
    ctx = ExitStack()
    with ctx:
        def sem(name):
            return ctx.enter_context(nc.semaphore(name))

        arena = ctx.enter_context(nc.sbuf_tensor("arena", [P, 52800], F32))
        psum = ctx.enter_context(nc.psum_tensor("psum", [P, 8, 512], F32))
        taken = [0]

        def carve(*dims):
            n = 1
            for d in dims:
                n *= d
            v = arena[:, taken[0]:taken[0] + n]
            taken[0] += n
            assert taken[0] <= 52800, taken[0]
            names = "abcd"[:len(dims)]
            if len(dims) == 1:
                return v
            return v.rearrange(f"p ({' '.join(names)}) -> p {' '.join(names)}",
                               **{n: d for n, d in zip(names, dims)})

        ident = carve(P)
        xT_all = carve(KT, T, B)
        phase_start = taken[0]
        overlay = phase_start + (T + B) * D

        wq, wk, wv = carve(KT, D), carve(KT, D), carve(KT, D)
        w_is = carve(KT, 2 * D)
        w_cs = carve(KT, 2 * D)
        w1 = carve(KT, FF)
        w2 = carve(FT, D)
        wout = carve(KT, D)
        cols = carve(40)
        bias3 = carve(3 * D)
        ln1_g_row, x1_b_row = carve(D), carve(D)
        hmask = carve(HG)
        vmask = carve(D)
        neg_half = carve(PAIRS)
        kcsT = carve(KT, B, NK)
        kcs_bd = carve(KT, HG, CB * NK)
        vcs_rep = carve(CB, D)
        vcs_bd = carve(CB, D)
        v_bd = carve(CB, H // 2, 2, DH)
        e = carve(2 * 512)
        pT = carve(2 * PAIRS, P)
        rrep = carve(D)
        rT = carve(KT, P)
        ctxT, csxT = carve(KT, CN), carve(KT, CN)
        cs_e = carve(H, NK)
        cs_pT = carve(P)
        stats = carve(5 * H)
        proj3 = carve(2, 3 * D)
        z_nat = carve(PAIRS, D)
        lnb = carve(PAIRS, D)
        x1_res = carve(PAIRS, D)
        ffT = carve(KT, CN)
        hT = carve(FT, CN)
        xres = carve(KT, CN)
        bn6 = carve(PAIRS, 6)
        mv = carve(PAIRS, 2)
        ve, rstd = carve(PAIRS), carve(PAIRS)
        assert taken[0] <= overlay
        taken[0] = overlay
        zT, qT, kT = carve(KT, CN), carve(KT, CN), carve(KT, CN)
        k_bd = carve(KT, HG, CN)
        wog_is = hT[:, 0:2, 0:D]
        wog_cs = hT[:, 0:2, D:2 * D]
        wgate = hT[:, 2:4, :].rearrange("p a b -> p (a b)").rearrange("p (k n) -> p k n", k=4)
        wg = hT[:, 4:8, :].rearrange("p a b -> p (a b)").rearrange("p (k n) -> p k n", k=KT)
        wkcs, wvcs = (xres[:, k, :].rearrange("p (k n) -> p k n", k=KT) for k in range(2))
        condT = z_nat[:, 0, 0:KT * B].rearrange("p (k n) -> p k n", k=KT)
        gtT = z_nat[:, 1:3, :].rearrange("p a b -> p (a b)").rearrange("p (j k b) -> p j k b", j=NK, k=KT)
        vcs_nat = lnb[0:B]
        mask_f = x1_res[:, 1, 0:T]
        c_is, c_cs = cols[:, 32:34], cols[:, 34:36]

        mask_l = ctx.enter_context(nc.sbuf_tensor("mask_l", [P, T], BF16))
        mask_r = ctx.enter_context(nc.sbuf_tensor("mask_r", [P, T], BF16))
        vcs_dram = nc.dram_tensor("vcs_dram", (NK, B, D), F32, kind="Internal").ap()
        x3_dram = nc.dram_tensor("x3_dram", (B, T, D), F32, kind="Internal").ap()
        x3r_dram = nc.dram_tensor("x3r_dram", (T, B, D), F32, kind="Internal").ap()

        COL = {name: 2 * i for i, name in enumerate(COLS0)}
        NCOLS = 2 * (len(COLS0) - 1) + FT
        bgc = proj3[:, 0, 0:8]

        def col(name, k):
            c = COL[name] + k
            return cols[:, c:c + 1]

        s_ps = psum[:, 0:2, :]
        pT_ps = psum[:, 0:2, :].rearrange("p a (b n) -> p (a b) n", n=P)
        ctx_ps = psum[:, 2, 0:256].rearrange("p (g n) -> p g n", g=KT)
        rT_ps = psum[:, 3, 256:512].rearrange("p (g n) -> p g n", g=KT)
        cs_ps = psum[:, 3, 0:64]
        cspT_ps = psum[0:64, 3, 64:192]
        csx_ps = psum[:, 2, 256:512].rearrange("p (g n) -> p g n", g=KT)

        nmax, rsum, rinv, csm, css = (stats[:, i * H:(i + 1) * H] for i in range(5))

        passed = sem("passed")
        ld_w = sem("ld_w")
        ld_first = sem("ld_first")
        ld_cond = sem("ld_cond")
        ld_gate = sem("ld_gate")
        ld_zt = sem("ld_zt")
        ld_zn = sem("ld_zn")
        ld_xr = sem("ld_xr")
        ld_vcs = sem("ld_vcs")
        ld_kbd = sem("ld_kbd")
        st_vcs = sem("st_vcs")
        pe_w = sem("pe_w")
        gm_ps = sem("gm_ps")
        gt_ps = sem("gt_ps")
        gt_done = sem("gt_done")
        kcs_ps = sem("kcs_ps")
        kcs_done = sem("kcs_done")
        vcs_ps = sem("vcs_ps")
        vcs_done = sem("vcs_done")
        cst_ps = sem("cst_ps")
        cst_done = sem("cst_done")
        row_ps = sem("row_ps")
        row_done = sem("row_done")
        zero_done = sem("zero_done")
        half_done = sem("half_done")
        mask_done = sem("mask_done")
        kq_ps = sem("kq_ps")
        v_ps = sem("v_ps")
        scores_ps = sem("scores_ps")
        pt_ps = sem("pt_ps")
        pv_ps = sem("pv_ps")
        a_ps = sem("a_ps")
        x1t_ps = sem("x1t_ps")
        ff_ps = sem("ff_ps")
        c_ps = sem("c_ps")
        x2t_ps = sem("x2t_ps")
        wout_ps = sem("wout_ps")
        kt_done = sem("kt_done")
        qt_done = sem("qt_done")
        v0_done = sem("v0_done")
        v1_done = sem("v1_done")
        nmax_done = sem("nmax_done")
        sub_done = sem("sub_done")
        exp_done = sem("exp_done")
        rsum_done = sem("rsum_done")
        rinv_done = sem("rinv_done")
        rrep_done = sem("rrep_done")
        csmax_done = sem("csmax_done")
        cssub_done = sem("cssub_done")
        csexp_done = sem("csexp_done")
        cssum_done = sem("cssum_done")
        csrec_done = sem("csrec_done")
        csp_done = sem("csp_done")
        pt0_done = sem("pt0_done")
        pt1_done = sem("pt1_done")
        cspt_done = sem("cspt_done")
        rt_done = sem("rt_done")
        ctx_done = sem("ctx_done")
        csx_done = sem("csx_done")
        abias_done = sem("abias_done")
        th_done = sem("th_done")
        dd_done = sem("dd_done")
        iz_done = sem("iz_done")
        gm_done = sem("gm_done")
        f_done = sem("f_done")
        x1t_done = sem("x1t_done")
        x1g_done = sem("x1g_done")
        x1r_done = sem("x1r_done")
        gelu_done = sem("gelu_done")
        y_done = sem("y_done")
        x2t_done = sem("x2t_done")
        xout_done = sem("xout_done")
        kcsbd_done = sem("kcsbd_done")
        vcsbd_done = sem("vcsbd_done")
        st1 = sem("st1")
        mv1 = sem("mv1")
        ve1 = sem("ve1")
        rstd1 = sem("rstd1")
        xh1 = sem("xh1")
        st2 = sem("st2")
        mv2 = sem("mv2")
        ve2 = sem("ve2")
        rstd2 = sem("rstd2")
        xh2 = sem("xh2")

        def count(value):
            return max(value, 0) if isinstance(value, int) else value

        def apart(eng):
            eng.sem_inc(passed, 1)

        def diag_rows(h):
            return slice(h * DH, (h + 1) * DH)

        kp = "(k p) n -> p k n"
        loads = []
        loads.append((wq, a["L0_cond_Wq"].rearrange(kp, p=P)))
        loads.append((wk, a["L0_cond_Wk_is"].rearrange(kp, p=P)))
        loads.append((wv, a["L0_cond_Wv_is"].rearrange(kp, p=P)))
        loads.append((zT, a["xT"].rearrange(kp, p=P)[:, :, 0:CN]))
        loads.append((cols[:, 0:NCOLS], a["cols0"]))
        first_loads, loads = loads, []
        loads.append((condT, a["condT"].rearrange(kp, p=P)))
        loads.append((wg, a["L0_cond_Wg"].rearrange(kp, p=P)))
        loads.append((bgc, a["bg_cols"]))
        loads.append((wvcs, a["L0_cond_Wv_cs"].rearrange(kp, p=P)))
        loads.append((wkcs, a["L0_cond_Wk_cs"].rearrange(kp, p=P)))
        loads.append((mask_f, a["mask"]))
        loads.append((hmask, a["hmask"]))
        loads.append((ident, a["ident"]))
        loads.append((vmask[0:64, :], a["vmask"]))
        cond_loads, loads = loads, []
        loads.append((w_is[:, :, 0:D], a["L0_cond_Wo_is"].rearrange(kp, p=P)))
        loads.append((w_cs[:, :, 0:D], a["L0_cond_Wo_cs"].rearrange(kp, p=P)))
        loads.append((wog_is, a["Wo_isT"].rearrange(kp, p=P)))
        loads.append((wog_cs, a["Wo_csT"].rearrange(kp, p=P)))
        loads.append((wgate, a["L0_cond_Wgate"].rearrange(kp, p=P)))
        gate_loads, loads = loads, []
        loads.append((w1, a["L0_cond_W1"].rearrange(kp, p=P)))
        loads.append((w2, a["L0_cond_W2"].rearrange(kp, p=P)))
        loads.append((wout, a["L0_cond_Wout"].rearrange(kp, p=P)))
        loads.append((ln1_g_row, a["L0_cond_ln1_g"].partition_broadcast(P)))
        loads.append((x1_b_row, a["L0_cond_ln1_b"].partition_broadcast(P)))
        loads.append((x1_res[:, 0, :], a["L0_cond_b2"].partition_broadcast(P)))
        loads.append((bias3[:, 2 * D:3 * D], a["L0_cond_bgate"].partition_broadcast(P)))
        LD_W = 16 * len(loads)
        LD_GATE = 16 * len(gate_loads)
        LD_FIRST = 16 * len(first_loads)
        LD_COND = 16 * len(cond_loads)

        taken[0] = phase_start
        toeplitz = carve(T, D)
        x3r = carve(B, D)
        assert taken[0] == overlay
        ws, wp, wo3 = carve(KT, NS), carve(KT, 2 * NS), carve(D)
        cols3 = carve(16)
        buffers = taken[0]
        wx1, wh1 = carve(KT, D), carve(KT, D)
        wx2, wh2 = carve(KT, 4, D), carve(KT, 4, D)
        x1s = [carve(KT, B), carve(KT, B)]
        x2s = [carve(KT, B), carve(KT, B)]
        x3s = [carve(KT, B), carve(KT, B)]
        x3n = [carve(D), carve(D)]
        h1T, h2T = carve(KT, B), carve(KT, B)
        h1n = carve(P)
        ifo, gg = carve(3, P), carve(P)
        cc, fc, ig, tc, h2n = carve(P), carve(P), carve(P), carve(P), carve(P)
        brow = carve(5 * D)
        bparts = carve(5 * D // 2).bitcast(BF16)
        bpart = carve(5 * D // 2).bitcast(BF16)
        ones = carve(B // 2).bitcast(BF16)
        taken[0] = buffers
        conv = carve(P, B)
        u = carve(4, CN)
        taken[0] = P
        decay_data = carve(CN)
        cvT = carve(KT, CN), carve(KT, CN)
        bt, ct, soft, st3, y3 = (carve(2, CN) for _ in range(5))
        taken[0] = phase_start + T * D
        x3t = carve(B // 2, D)
        bo_row = carve(D)
        ld2 = sem("ld2")
        ld_toe = sem("ld_toe")
        bones = sem("bones")
        bpart_done = sem("bpart_done")
        brest_done = sem("brest_done")
        ld_bias = sem("ld_bias")
        x1s_done = sem("x1s_done")
        a1_ps = sem("a1_ps")
        h1_done = sem("h1_done")
        h1t_ps = sem("h1t_ps")
        h1t_done = sem("h1t_done")
        x2_done = sem("x2_done")
        a2_ps = sem("a2_ps")
        ifo_done = sem("ifo_done")
        g_done = sem("g_done")
        fc_done = sem("fc_done")
        ig_done = sem("ig_done")
        c_done = sem("c_done")
        tc_done = sem("tc_done")
        h2_done = sem("h2_done")
        h2t_ps = sem("h2t_ps")
        h2t_done = sem("h2t_done")
        x3_done = sem("x3_done")
        x3_ps = sem("x3_ps")
        x3n_done = sem("x3n_done")
        x3all_done = sem("x3all_done")
        ld3 = sem("ld3")
        ld_x3r = sem("ld_x3r")
        ld_x3t = sem("ld_x3t")
        u_ps = sem("u_ps")
        u_done = sem("u_done")
        conv_ps = sem("conv_ps")
        cvt_ps = sem("cvt_ps")
        cvt_done = sem("cvt_done")
        bc_ps = sem("bc_ps")
        b_done = sem("b_done")
        ct_done = sem("ct_done")
        abs_done = sem("abs_done")
        ex_done = sem("ex_done")
        ln_done = sem("ln_done")
        sp_done = sem("sp_done")
        v_done = sem("v_done")
        col3 = sem("col3")
        scan_done = sem("scan_done")
        yy_done = sem("yy_done")
        yo_ps = sem("yo_ps")
        xb_done = sem("xb_done")
        o_done = sem("o_done")
        st_out = sem("st_out")
        st_x3, st_x3r, conv_done = ([sem(f"{n}_{r}") for r in range(2)] for n in ("st_x3", "st_x3r", "conv_done"))

        LD2 = 16 * 8
        LATE = 3 * T // 4

        def tiles(g):
            j, h = g // 2, g % 2
            return slice(16 * h + 4 * j, 16 * h + 4 * j + 4)

        STEPS = T

        def wave(eng, step):
            for t in range(4):
                step(t, t % 2)
            with eng.Fori(2, T // 2 - 1) as i:
                step(2 * i, 0)
                step(2 * i + 1, 1)
            for t in range(T - 2, T + 1):
                step(t, t % 2)

        def before(t, end):
            return not isinstance(t, int) or t < end

        def since(t, begin):
            return not isinstance(t, int) or t >= begin

        def sp_tail(sp):
            def load(landed, dst, src):
                sp.dma_start(dst, src).then_inc(landed, 16)

            sp.wait_ge(pv_ps, PAIRS * NCH)
            sp.wait_ge(rt_done, PAIRS * NCH)
            load(ld_bias, brow[:, 0:D], a["L1_cond_b"].partition_broadcast(P))
            load(ld_bias, brow[:, D:5 * D], a["L2_cond_b"].partition_broadcast(P))
            load(ld2, wx1, a["L1_cond_Wx"].rearrange(kp, p=P))
            load(ld2, wh1, a["L1_cond_Wh"].rearrange(kp, p=P))
            load(ld2, h1T, a["condT"].rearrange(kp, p=P))
            load(ld2, h2T, a["condT"].rearrange(kp, p=P))
            for k in range(KT):
                load(ld2, wx2[:, k], a["L2_cond_Wx"].rearrange("(k p) (g n) -> k p g n", p=P, n=D)[k])
                load(ld2, wh2[:, k], a["L2_cond_Wh"].rearrange("(k p) (g n) -> k p g n", p=P, n=D)[k])
            load(ld3, ws, a["L3_cond_Ws"].rearrange(kp, p=P))
            load(ld3, wp, a["L3_cond_Wp"].rearrange(kp, p=P))
            for h in range(2):
                load(ld3, wo3[64 * h:64 * h + 64], a["L3_cond_Wo"])
            load(ld3, cols3[:, 0:7], a["cols3"])
            sp.wait_ge(xout_done, KT * NCH)
            cp = a["cond_pad"]
            load(ld_toe, toeplitz[0:T].rearrange("p t d -> p (t d)"),
                 bass.AP(cp.tensor, D, [[D, T], [1, T * D]]))

            def store(t, r):
                sp.wait_ge(x3n_done, t + 1)
                apart(sp)
                sp.dma_start(x3_dram[:, bass.ds(t, 1), :].rearrange("b o n -> b (o n)"), x3n[r][0:B]
                             ).then_inc(st_x3[r], 16)
                sp.dma_start(x3r_dram[bass.ds(T - 1 - t, 1)].rearrange("o b n -> (o b) n"), x3n[r][0:B]
                             ).then_inc(st_x3r[r], 16)

            for t in range(2):
                store(t, t)
            with sp.Fori(1, LATE // 2) as i:
                store(2 * i, 0)
                store(2 * i + 1, 1)
            for r in range(2):
                sp.wait_ge(st_x3r[r], 8 * LATE)
            load(ld_x3r, x3r[T - LATE:T], x3r_dram[T - LATE:T])
            with sp.Fori(LATE // 2, T // 2) as i:
                store(2 * i, 0)
                store(2 * i + 1, 1)
            for r in range(2):
                sp.wait_ge(st_x3r[r], 8 * T)
                sp.wait_ge(st_x3[r], 8 * T)
            load(ld_x3r, x3r[0:T - LATE], x3r_dram[0:T - LATE])
            sp.wait_ge(conv_ps, 16)
            x3_tiles = x3_dram.rearrange("(i h) t n -> (h t) i n", h=2)
            load(ld_x3t, bo_row, a["L3_cond_bo"].partition_broadcast(P))
            for g in range(8):
                load(ld_x3t, x3t[:, 4 * g:4 * g + 4, :], x3_tiles[:, tiles(g), :])
            out_tiles = out.rearrange("(i h) t n -> (h t) i n", h=2)
            for g in range(8):
                sp.wait_ge(o_done, 2 * (g + 1))
                sp.dma_start(out_tiles[:, tiles(g), :], x3t[:, 4 * g:4 * g + 4, :]
                             ).then_inc(st_out, 16)
            sp.wait_ge(st_out, 16 * 8)

        def pe_tail(pe):
            mm = pe.matmul

            def halves(bank, n):
                return [psum[64 * h:64 * h + 64, bank, 0:n] for h in range(2)]

            def l1_x(t, r):
                pe.wait_ge(x1s_done, t + 1)
                pe.wait_ge(h1_done, count(t - 1))
                for h, o in enumerate(halves(r, P)):
                    mm(o, ones, bparts[:, h * P:(h + 1) * P], start=True, stop=False)
                for k in range(KT):
                    for h, o in enumerate(halves(r, P)):
                        mm(o, x1s[r][:, k, :], wx1[:, k, h * P:(h + 1) * P], start=False, stop=False)

            def l1_h(t, r):
                pe.wait_ge(h1t_done, t)
                for k in range(KT):
                    for h, o in enumerate(halves(r, P)):
                        x = mm(o, h1T[:, k, :], wh1[:, k, h * P:(h + 1) * P], start=False, stop=k == 1)
                x.then_inc(a1_ps, 1)

            def l2_part(r, k, src, w):
                for h in range(2):
                    x = mm(psum[64 * h:64 * h + 64, 2 + r, :], src[:, k, :], w[:, k, :, h * P:(h + 1) * P],
                           start=False, stop=w is wh2 and k == 1)
                return x

            def l2_bias(t, r):
                pe.wait_ge(x2_done, t + 1)
                pe.wait_ge(g_done, count(t - 1))
                bp = bparts[:, D:5 * D].rearrange("p (g n) -> p g n", g=4)
                for h in range(2):
                    mm(psum[64 * h:64 * h + 64, 2 + r, :], ones, bp[:, :, h * P:(h + 1) * P], start=True, stop=False)

            def l2_h(t, r):
                pe.wait_ge(h2t_done, t)
                l2_part(r, 0, h2T, wh2)
                l2_part(r, 1, h2T, wh2).then_inc(a2_ps, 1)

            def turn_h1(t):
                pe.wait_ge(h1_done, t + 1)
                pe.wait_ge(h1t_done, t)
                pe.wait_ge(x2_done, t)
                pe.transpose(psum[:, 4, 0:P], h1n, ident).then_inc(h1t_ps, 1)

            def turn_h2(t):
                pe.wait_ge(h2_done, t + 1)
                pe.wait_ge(h2t_done, t)
                pe.wait_ge(x3_done, t)
                pe.transpose(psum[:, 5, 0:P], h2n, ident).then_inc(h2t_ps, 1)

            def turn_x3(t, r):
                pe.wait_ge(x3_done, t + 1)
                pe.wait_ge(x3n_done, t)
                apart(pe)
                for k in range(KT):
                    x = pe.transpose(psum[0:B, 6, k * P:(k + 1) * P], x3s[r][:, k, :], ident)
                x.then_inc(x3_ps, 1)

            def step(t, r):
                if since(t, 1):
                    l2_h(t - 1, 1 - r)
                if before(t, T - 1):
                    l1_h(t + 1, 1 - r)
                if before(t, T - 2):
                    l1_x(t + 2, r)
                if since(t, 2):
                    turn_x3(t - 2, r)
                if before(t, T - 1):
                    turn_h1(t + 1)
                if before(t, T):
                    l2_bias(t, r)
                    l2_part(r, 0, x2s[r], wx2)
                if since(t, 1):
                    turn_h2(t - 1)
                if before(t, T):
                    l2_part(r, 1, x2s[r], wx2)

            pe.wait_ge(ld2, LD2)
            pe.wait_ge(bones, 3)
            pe.wait_ge(bpart_done, 5)
            l1_x(0, 0)
            l1_h(0, 0)
            l1_x(1, 1)
            turn_h1(0)
            wave(pe, step)
            turn_x3(T - 1, 1)

            pe.wait_ge(ld3, 16 * 5)
            pe.wait_ge(x3all_done, T)
            for j in range(4):
                pe.wait_ge(u_done, count(j - 1))
                for k in range(KT):
                    for h in range(2):
                        rhs = xT_all[:, k, :, h * 32 + j * CB:h * 32 + (j + 1) * CB].rearrange("p t b -> p b t")
                        x = mm(psum[64 * h:64 * h + 64, j % 2, :], ws[:, k, :], rhs, start=k == 0, stop=k == 1)
                x.then_inc(u_ps, 1)
            pe.wait_ge(ld_toe, 16)
            pe.wait_ge(ld_x3r, 32)
            for i in range(P // 8):
                pe.wait_ge(conv_done[i % 2], count((i - 4) // 2 + 1))
                for j in range(8):
                    for h in range(2):
                        d = h * P + 8 * i + j
                        x = mm(psum[64 * h:64 * h + 64, 2 + i % 4, j * B:(j + 1) * B], toeplitz[0:T, :, d],
                               x3r[0:T, :, d], start=True, stop=True)
                x.then_inc(conv_ps, 1)

            pe.wait_ge(u_done, 4)
            pe.wait_ge(conv_done[0], 8)
            pe.wait_ge(conv_done[1], 8)
            def out_rows(j):
                pe.wait_ge(yy_done, j + 1)
                for h in range(2):
                    for i in range(2):
                        m = 4 * j + 2 * h + i
                        pe.wait_ge(o_done, count(m - 3))
                        for q in range(2):
                            t = 2 * i + q
                            x = mm(psum[:, 2 + m % 4, q * D:(q + 1) * D],
                                   y3[64 * h:64 * h + 64, j % 2, t * P:(t + 1) * P], wo3[64 * h:64 * h + 64, :],
                                   start=True, stop=True)
                        x.then_inc(yo_ps, 1)

            for j in range(4):
                for h in range(2):
                    for i in range(2):
                        n = 4 * j + 2 * h + i
                        pe.wait_ge(cvt_done, count(2 * (n - 1)))
                        for b in range(4):
                            q = h * 32 + j * CB + i * 4 + b
                            x = pe.transpose(psum[:, n % 2, b * P:(b + 1) * P], conv[:, :, q], ident)
                        x.then_inc(cvt_ps, 1)
                pe.wait_ge(cvt_done, 8 * (j + 1))
                pe.wait_ge(b_done, j)
                pe.wait_ge(ct_done, j)
                pe.wait_ge(x3n_done, T)
                for w in range(2):
                    for k in range(KT):
                        for h in range(2):
                            x = mm(psum[64 * h:64 * h + 64, 6 + w, :], wp[:, k, w * NS:(w + 1) * NS],
                                   cvT[h][:, k, :], start=k == 0, stop=k == 1)
                x.then_inc(bc_ps, 1)
                if j:
                    out_rows(j - 1)
            out_rows(3)

        def dve_tail(dve):
            tt = dve.tensor_tensor
            def cell(t):
                dve.wait_ge(ifo_done, t + 1)
                dve.wait_ge(c_done, t)
                dve.wait_ge(tc_done, t)
                tt(fc, ifo[:, 1, :], cc, ALU.mult).then_inc(fc_done, 1)
                dve.wait_ge(g_done, t + 1)
                tt(ig, ifo[:, 0, :], gg, ALU.mult).then_inc(ig_done, 1)
                dve.wait_ge(fc_done, t + 1)
                dve.wait_ge(ig_done, t + 1)
                tt(cc, fc, ig, ALU.add).then_inc(c_done, 1)

            h1T_ps = psum[:, 4, 0:P].rearrange("p (k b) -> p k b", k=KT)

            def copy_h1(t):
                dve.wait_ge(h1t_ps, t + 1)
                dve.wait_ge(h1t_done, t)
                dve.tensor_copy(h1T, h1T_ps).then_inc(h1t_done, 1)

            def layer1_out(t, r):
                dve.wait_ge(a2_ps, count(t - 1))
                dve.wait_ge(x3_done, count(t - 1))
                dve.wait_ge(x1s_done, t + 1)
                tt(x2s[r], h1T_ps, x1s[r], ALU.add).then_inc(x2_done, 1)

            def hidden(t, r):
                dve.wait_ge(tc_done, t + 1)
                dve.wait_ge(h2t_ps, t)
                tt(h2n, ifo[:, 2, :], tc, ALU.mult).then_inc(h2_done, 1)
                dve.wait_ge(h2t_ps, t + 1)
                hT_ps = psum[:, 5, 0:P].rearrange("p (k b) -> p k b", k=KT)
                dve.wait_ge(h2t_done, t)
                dve.tensor_copy(h2T, hT_ps).then_inc(h2t_done, 1)
                dve.wait_ge(x3_ps, count(t - 1))
                dve.wait_ge(x3all_done, count(t - 1))
                dve.wait_ge(x2_done, t + 1)
                tt(x3s[r], hT_ps, x2s[r], ALU.add).then_inc(x3_done, 1)

            def step(t, r):
                if since(t, 1):
                    cell(t - 1)
                if before(t, T - 1):
                    copy_h1(t + 1)
                if since(t, 1):
                    hidden(t - 1, 1 - r)
                if before(t, T - 1):
                    layer1_out(t + 1, 1 - r)

            copy_h1(0)
            layer1_out(0, 0)
            wave(dve, step)

            dve.wait_ge(ld3, 16 * 5)
            for j in range(4):
                dve.wait_ge(u_ps, j + 1)
                dve.tensor_scalar(u[:, j, :], psum[:, j % 2, :], cols3[:, 0:1], None, ALU.add
                                  ).then_inc(u_done, 1)
            dve.wait_ge(col3, 1)
            dve.scalar_tensor_tensor(out=cols3[:, 9:11], in0=cols3[:, 3:5], scalar=0.0, in1=cols3[:, 7:9],
                                     op0=ALU.max, op1=ALU.add).then_inc(col3, 1)
            dve.wait_ge(col3, 2)
            tt(cols3[:, 11:12], cols3[:, 9:10], cols3[:, 10:11], ALU.mult).then_inc(col3, 1)
            dve.wait_ge(col3, 3)
            dve.tensor_scalar(cols3[:, 12:13], cols3[:, 11:12], -1.0, 1.0, ALU.mult, ALU.add
                              ).then_inc(col3, 1)
            dve.wait_ge(u_ps, 4)
            dd = decay_data.rearrange("p (b t) -> p b t", t=T)
            dve.memset(dd, 1.0).then_inc(col3, 1)
            dve.wait_ge(col3, 5)
            dve.memset(dd[:, :, 0:1], 0.0).then_inc(col3, 1)
            dve.wait_ge(col3, 6)
            dve.tensor_scalar(dd, dd, cols3[:, 12:13], None, ALU.mult).then_inc(col3, 1)

            for i in range(0, P // 8, 2):
                dve.wait_ge(conv_ps, i + 1)
                dve.tensor_copy(conv[:, 8 * i:8 * i + 8, :], psum[:, 2 + i % 4, :].rearrange("p (d b) -> p d b", b=B)
                                ).then_inc(conv_done[0], 1)
            def softplus(j):
                r = j % 2
                dve.wait_ge(ln_done, j + 1)
                dve.scalar_tensor_tensor(out=bt[:, r, :], in0=bt[:, r, :], scalar=0.0, in1=soft[:, r, :], op0=ALU.max,
                                         op1=ALU.add).then_inc(sp_done, 1)

            def drive(j):
                dve.wait_ge(sp_done, j + 1)
                dve.scalar_tensor_tensor(out=u[:, j, :], in0=u[:, j, :], scalar=cols3[:, 10:11], in1=bt[:, j % 2, :],
                                         op0=ALU.mult, op1=ALU.mult).then_inc(v_done, 1)

            def scan(j):
                dve.wait_ge(v_done, j + 1)
                dve.wait_ge(col3, 7)
                dve.wait_ge(yy_done, count(j - 1))
                dve.tensor_tensor_scan(st3[:, j % 2, :], decay_data, u[:, j, :], 0.0, ALU.mult, ALU.add
                                       ).then_inc(scan_done, 1)

            def read_out(j):
                dve.wait_ge(scan_done, j + 1)
                dve.wait_ge(ct_done, j + 1)
                dve.wait_ge(yo_ps, count(4 * (j - 1)))
                tt(y3[:, j % 2, :], st3[:, j % 2, :], ct[:, j % 2, :], ALU.mult).then_inc(yy_done, 1)

            def out_add(m):
                dve.wait_ge(xb_done, m // 4 + 1)
                dve.wait_ge(yo_ps, m + 1)
                rows = x3t[:, 2 * m:2 * m + 2, :].rearrange("p a n -> p (a n)")
                tt(rows, psum[:, 2 + m % 4, :], rows, ALU.add).then_inc(o_done, 1)

            def copy_conv(j, h, i):
                n = 4 * j + 2 * h + i
                dve.wait_ge(cvt_ps, n + 1)
                dve.wait_ge(bc_ps, j)
                for k in range(KT):
                    dve.tensor_scalar(
                        cvT[h][:, k, i * 256:(i + 1) * 256].rearrange("p (b t) -> p b t", t=T),
                        psum[:, n % 2, :].rearrange("p (b k t) -> p b k t", k=KT, t=T)[:, :, k, :],
                        cols3[:, 5 + k:6 + k], None, ALU.add).then_inc(cvt_done, 1)

            for j in range(4):
                copy_conv(j, 0, 0)
                copy_conv(j, 0, 1)
                if j:
                    softplus(j - 1)
                copy_conv(j, 1, 0)
                if j:
                    drive(j - 1)
                copy_conv(j, 1, 1)
                if j:
                    scan(j - 1)
                    read_out(j - 1)
                dve.wait_ge(bc_ps, j + 1)
                dve.wait_ge(v_done, count(j - 1))
                dve.tensor_scalar(bt[:, j % 2, :], psum[:, 6, :], cols3[:, 1:2], None, ALU.add
                                  ).then_inc(b_done, 1)
                if j:
                    for m in range(4 * j - 4, 4 * j):
                        out_add(m)
            softplus(3)
            drive(3)
            scan(3)
            read_out(3)
            for m in range(12, 16):
                out_add(m)

        def act_tail(act):
            ac = act.activation

            def gates(t, r):
                a2 = psum[:, 2 + r, :].rearrange("p (g n) -> p g n", g=4)
                act.wait_ge(a2_ps, t + 1)
                act.wait_ge(h2_done, t)
                ac(ifo, a2[:, 0:3], ACT.Sigmoid).then_inc(ifo_done, 1)
                ac(gg, a2[:, 3], ACT.Tanh).then_inc(g_done, 1)

            def layer1(t, r):
                act.wait_ge(a1_ps, t + 1)
                act.wait_ge(h1t_ps, t)
                ac(h1n, psum[:, r, 0:P], ACT.Tanh).then_inc(h1_done, 1)

            def cell_tanh(t):
                act.wait_ge(c_done, t + 1)
                ac(tc, cc, ACT.Tanh).then_inc(tc_done, 1)

            def rows(t, r):
                act.wait_ge(x3_ps, t + 1)
                act.wait_ge(st_x3[r], 8 * (t - r))
                act.wait_ge(st_x3r[r], 8 * (t - r))
                ac(x3n[r][0:B], psum[0:B, 6, 0:D], ACT.Copy).then_inc(x3n_done, 1)

            def step(t, r):
                if since(t, 1):
                    gates(t - 1, 1 - r)
                if before(t, T - 1):
                    layer1(t + 1, 1 - r)
                if since(t, 1):
                    cell_tanh(t - 1)
                if since(t, 2):
                    rows(t - 2, r)

            layer1(0, 0)
            wave(act, step)
            rows(T - 1, 1)

            def log_part(dst, src, n0):
                ac(dst, src, ACT.Abs).then_inc(abs_done, 1)
                act.wait_ge(abs_done, n0 + 1)
                ac(dst, dst, ACT.Exp, scale=-1.0).then_inc(ex_done, 1)
                act.wait_ge(ex_done, n0 + 1)
                return ac(dst, dst, ACT.Ln, bias=1.0)

            act.wait_ge(ld3, 16 * 5)
            log_part(cols3[:, 7:9], cols3[:, 3:5], 0).then_inc(col3, 1)
            for i in range(1, P // 8, 2):
                act.wait_ge(conv_ps, i + 1)
                ac(conv[:, 8 * i:8 * i + 8, :], psum[:, 2 + i % 4, :].rearrange("p (d b) -> p d b", b=B), ACT.Copy
                   ).then_inc(conv_done[1], 1)
            for j in range(4):
                r = j % 2
                act.wait_ge(b_done, j + 1)
                act.wait_ge(sp_done, count(j - 1))
                log_part(soft[:, r, :], bt[:, r, :], j + 1).then_inc(ln_done, 1)
                act.wait_ge(bc_ps, j + 1)
                act.wait_ge(yy_done, count(j - 1))
                ac(ct[:, r, :], psum[:, 7, :], ACT.Tanh, bias=cols3[:, 2:3]).then_inc(ct_done, 1)

        def pool_tail(pool):
            def stage(t, r):
                pool.wait_ge(x2_done, count(t - 1))
                pool.wait_ge(a1_ps, count(t - 1))
                apart(pool)
                pool.tensor_copy(x1s[r], xT_all[:, :, bass.ds(t, 1), :].rearrange("p k o b -> p k (o b)")
                                 ).then_inc(x1s_done, 1)

            def keep(t, r):
                pool.wait_ge(x3_done, t + 1)
                apart(pool)
                pool.tensor_copy(xT_all[:, :, bass.ds(t, 1), :].rearrange("p k o b -> p k (o b)"), x3s[r]
                                 ).then_inc(x3all_done, 1)

            pool.wait_ge(xout_done, KT * NCH)
            for t in range(4):
                stage(t, t % 2)
            keep(0, 0)
            with pool.Fori(2, T // 2) as i:
                stage(2 * i, 0)
                keep(2 * i - 3, 1)
                stage(2 * i + 1, 1)
                keep(2 * i - 2, 0)
            for t in range(T - 3, T):
                keep(t, t % 2)
            for q in range(4):
                pool.wait_ge(ld_x3t, 16 * 9)
                pool.tensor_tensor(x3t[:, 8 * q:8 * q + 8, :], x3t[:, 8 * q:8 * q + 8, :],
                                   bo_row.unsqueeze(1).broadcast_to([P, 8, D]), ALU.add
                                   ).then_inc(xb_done, 1)


        block = ctx.enter_context(nc.Block())

        def pipeline(eng, first, step):
            first()
            step(0, None, 1)
            step(1, 0, 2)
            with eng.Fori(2, NCH - 1) as c:
                step(c, c - 1, c + 1)
            step(NCH - 1, NCH - 2, None)
            step(None, NCH - 1, None)

        @block.sync
        def _(sp):
            def load(landed, dst, src):
                sp.dma_start(dst, src).then_inc(landed, 16)

            def load_vcs(c):
                apart(sp)
                src = vcs_dram[:, bass.ds(c * CB, CB), :]
                for h in range(H):
                    sp.dma_start(vcs_rep[4 * h:4 * h + 4], src).then_inc(ld_vcs, 16)

            def spread_k(c):
                sp.wait_ge(zero_done, 1)
                apart(sp)
                sp.wait_ge(kt_done, KT * (c + 1))
                apart(sp)
                sp.wait_ge(scores_ps, PAIRS * c)
                for h in range(HG):
                    sp.dma_start(k_bd[diag_rows(h), :, h, :], kT[diag_rows(h)]).then_inc(ld_kbd, 16)

            for dst, dram in first_loads:
                load(ld_first, dst, dram)
            for dst, dram in cond_loads:
                load(ld_cond, dst, dram)
            spread_k(0)
            for dst, dram in gate_loads:
                load(ld_gate, dst, dram)
            sp.wait_ge(vcs_done, NK)
            sp.dma_start(vcs_dram.rearrange("j b n -> b j n"), vcs_nat).then_inc(st_vcs, 16)
            sp.wait_ge(st_vcs, 16)
            load_vcs(0)
            for dst, dram in loads:
                load(ld_w, dst, dram)

            def step(c, q, n):
                if n is not None:
                    sp.wait_ge(v_ps, 2 * n)
                    apart(sp)
                    load(ld_zt, zT, a["xT"].rearrange(kp, p=P)[:, :, bass.ds(n * CN, CN)])
                if q is not None:
                    sp.wait_ge(iz_done, PAIRS * q)
                    apart(sp)
                    load(ld_zn, z_nat, a["x_nat"].rearrange("(c i p) n -> c p i n", i=PAIRS, p=P)[q])
                    sp.wait_ge(xout_done, KT * q)
                    apart(sp)
                    load(ld_xr, xres, a["xT"].rearrange(kp, p=P)[:, :, bass.ds(q * CN, CN)])
                if n is not None:
                    sp.wait_ge(vcsbd_done, n)
                    load_vcs(n)
                    spread_k(n)

            pipeline(sp, lambda: None, step)
            sp_tail(sp)

        @block.tensor
        def _(pe):

            mm = pe.matmul

            def condition():
                for jk in range(NK * KT):
                    for k in range(KT):
                        x = mm(psum[:, 6, jk * B:(jk + 1) * B], wg[:, k, jk * P:(jk + 1) * P], condT[:, k, :],
                               start=k == 0, stop=k == 1)
                x.then_inc(gt_ps, 1)
                pe.wait_ge(gt_done, 1)
                pe.wait_ge(v0_done, 2)
                pe.wait_ge(v1_done, 2)
                for j in range(NK):
                    for k in range(KT):
                        x = mm(psum[0:B, 4 + j // 2, (j % 2) * D:(j % 2 + 1) * D], gtT[:, j, k, :], wvcs[:, k, :],
                               start=k == 0, stop=k == 1)
                x.then_inc(vcs_ps, 1)
                for g in range(KT):
                    for k in range(KT):
                        x = mm(psum[:, 7, g * 256:(g + 1) * 256], wkcs[:, k, g * P:(g + 1) * P], gtT[:, :, k, :],
                               start=k == 0, stop=k == 1)
                x.then_inc(kcs_ps, 1)

            def gate_weights():
                pe.wait_ge(ld_gate, LD_GATE)
                pe.wait_ge(vcs_done, NK)
                for i, (wt, g0) in enumerate(((wog_is, 0), (wog_cs, 2))):
                    for m in range(KT):
                        for k in range(KT):
                            x = mm(psum[:, 4 + i, m * D:(m + 1) * D], wt[:, k, m * P:(m + 1) * P], wgate[:, g0 + k, :],
                                   start=k == 0, stop=k == 1)
                x.then_inc(gm_ps, 1)
                for i, (w, b) in enumerate(((w_is, "bv_is"), (w_cs, "bv_cs"))):
                    for m in range(KT):
                        for k in range(KT):
                            x = mm(psum[:, 6, 2 * i + m:2 * i + m + 1], w[:, k, m * P:(m + 1) * P], col(b, k),
                                   start=k == 0, stop=k == 1)
                x.then_inc(cst_ps, 1)

            def bias_rows():
                pe.wait_ge(ld_w, LD_W)
                pe.wait_ge(cst_done, 2)
                pe.wait_ge(kcs_done, 2)
                for i, c_ in enumerate((c_is, c_cs)):
                    for k in range(KT):
                        x = mm(psum[:, 7, i * D + k * P:i * D + (k + 1) * P], c_[:, k:k + 1].broadcast_to([P, P]), ident,
                               start=True, stop=True)
                for i, c_ in enumerate((c_is, c_cs)):
                    for k in range(KT):
                        x = mm(psum[:, 6, D:2 * D], c_[:, k:k + 1].broadcast_to([P, P]), wgate[:, 2 * i + k, :],
                               start=i + k == 0, stop=i + k == 2)
                x.then_inc(row_ps, 1)
                pe.wait_ge(pe_w, 2)
                pe.wait_ge(row_done, 2)

            def keys(n, q):
                pe.wait_ge(ld_zt, 16 * n)
                if q is not None:
                    pe.wait_ge(y_done, PAIRS * q + 2)
                else:
                    pe.wait_ge(v0_done, 2 * n)
                    pe.wait_ge(v1_done, 2 * n)
                for g in range(KT):
                    for k in range(KT):
                        x = mm(psum[:, 4 + g, :], wk[:, k, g * P:(g + 1) * P], zT[:, k, :], start=k == 0, stop=k == 1)
                    x.then_inc(kq_ps, 1)

            def queries(n, q):
                if q is not None:
                    pe.wait_ge(y_done, PAIRS * (q + 1))
                else:
                    pe.wait_ge(qt_done, KT * n)
                for g in range(KT):
                    for k in range(KT):
                        x = mm(psum[:, 6 + g, :], wq[:, k, g * P:(g + 1) * P], zT[:, k, :], start=k == 0, stop=k == 1)
                    x.then_inc(kq_ps, 1)

            def values(n):
                for i in range(2):
                    pe.wait_ge(kt_done, KT * n + i + 1)
                    for b in range(4):
                        for k in range(KT):
                            for h2 in range(2):
                                r = wv[:, k, :].rearrange("p (j h e) -> p h j e", h=2, e=DH)[:, h2]
                                x = mm(psum[h2 * 64:h2 * 64 + 64, 4 + i, b * P:(b + 1) * P],
                                       zT[:, k, (4 * i + b) * T:(4 * i + b + 1) * T], r, start=k == 0, stop=k == 1)
                    x.then_inc(v_ps, 1)

            def scores(c, p):
                if p == 0:
                    pe.wait_ge(qt_done, KT * (c + 1))
                    pe.wait_ge(ld_kbd, 16 * HG * (c + 1))
                    pe.wait_ge(kcsbd_done, KT * (c + 1))
                pe.wait_ge(pt0_done, PAIRS * c + p)
                pe.wait_ge(pt1_done, PAIRS * c + p)
                pe.wait_ge(rt_done, PAIRS * c + p)
                for g in range(KT):
                    for half in range(2):
                        mm(s_ps[half * 64:half * 64 + 64, g, :], mask_l[:],
                           mask_r[:].unsqueeze(1).broadcast_to([P, HG, T]), start=True, stop=False)
                    for half in range(2):
                        b = 2 * p + half
                        x = mm(s_ps[half * 64:half * 64 + 64, g, :], qT[:, g, b * T:(b + 1) * T],
                               k_bd[:, g, :, b * T:(b + 1) * T], start=False, stop=True)
                for g in range(KT):
                    for half in range(2):
                        b = 2 * p + half
                        x = mm(cs_ps[half * 64:half * 64 + 64, g * 32:(g + 1) * 32], qT[:, g, b * T:(b + 1) * T],
                               kcs_bd[:, g, :, b * NK:(b + 1) * NK], start=True, stop=True)
                x.then_inc(scores_ps, 1)

            def transposes(c, p):
                pe.wait_ge(exp_done, PAIRS * c + p + 1)
                for i in range(2 * PAIRS):
                    pe.transpose(pT_ps[:, i, :], e[:, i * P:(i + 1) * P], ident)
                pe.wait_ge(csp_done, PAIRS * c + p + 1)
                pe.wait_ge(cspt_done, PAIRS * c + p)
                apart(pe)
                pe.transpose(cspT_ps, cs_e.rearrange("p a b -> p (a b)"), ident)
                pe.wait_ge(rrep_done, PAIRS * c + p + 1)
                pe.wait_ge(rt_done, PAIRS * c + p)
                for g in range(KT):
                    x = pe.transpose(rT_ps[:, g, :], rrep[:, g * P:(g + 1) * P], ident)
                x.then_inc(pt_ps, 1)

            def pv(c, p):
                if p == 0:
                    pe.wait_ge(v0_done, 2 * (c + 1))
                    pe.wait_ge(v1_done, 2 * (c + 1))
                    pe.wait_ge(vcsbd_done, c + 1)
                pe.wait_ge(pt0_done, PAIRS * c + p + 1)
                pe.wait_ge(pt1_done, PAIRS * c + p + 1)
                pe.wait_ge(ctx_done, PAIRS * c + p)
                pe.wait_ge(csx_done, PAIRS * c + p)
                for g in range(KT):
                    for half in range(2):
                        for j in range(4):
                            mm(ctx_ps[32 * j:32 * j + 32, g, half * 64:half * 64 + 64],
                               v_bd[:, 2 * p + half, 4 * g + j].rearrange("p h e -> p (h e)"), pT[:, 4 * g + j, half * 64:half * 64 + 64],
                               start=True, stop=True)
                pe.wait_ge(cspt_done, PAIRS * c + p + 1)
                for g in range(KT):
                    for half in range(2):
                        x = mm(csx_ps[:, g, half * 64:half * 64 + 64], vcs_bd[0:64, 2 * p + half, g * P:(g + 1) * P],
                               cs_pT[0:64, half * 64:half * 64 + 64], start=True, stop=True)
                x.then_inc(pv_ps, 1)

            def project(q, i, nq):
                if i == 0:
                    pe.wait_ge(ctx_done, PAIRS * (q + 1))
                    pe.wait_ge(csx_done, PAIRS * (q + 1))
                    pe.wait_ge(v0_done, 2 * nq)
                    pe.wait_ge(v1_done, 2 * nq)
                if i == 1:
                    pe.wait_ge(x2t_done, KT * q)
                    pe.wait_ge(qt_done, KT * nq)
                if i >= 2:
                    pe.wait_ge(abias_done, count(PAIRS * q + i - 1))
                bank = 4 + 2 * (i % 2)
                t = slice(i * P, (i + 1) * P)
                for k in range(KT):
                    mm(psum[:, bank, 0:D], ctxT[:, k, t], w_is[:, k, 0:D], start=k == 0, stop=k == 1)
                for k in range(KT):
                    mm(psum[:, bank, D:2 * D], csxT[:, k, t], w_cs[:, k, 0:D], start=k == 0, stop=k == 1)
                for k in range(KT):
                    mm(psum[:, bank + 1, 0:D], ctxT[:, k, t], w_is[:, k, D:2 * D], start=k == 0, stop=False)
                for k in range(KT):
                    x = mm(psum[:, bank + 1, 0:D], csxT[:, k, t], w_cs[:, k, D:2 * D], start=False, stop=k == 1)
                x.then_inc(a_ps, 1)

            def turn(turned, bank):
                for k in range(KT):
                    for i in range(PAIRS):
                        x = pe.transpose(psum[:, bank + k, i * P:(i + 1) * P], lnb[:, i, k * P:(k + 1) * P], ident)
                    x.then_inc(turned, 1)

            def ff_up(q, i):
                if i == 0:
                    pe.wait_ge(x1t_done, KT * (q + 1))
                if i == 2:
                    pe.wait_ge(abias_done, PAIRS * (q + 1))
                    pe.wait_ge(xout_done, KT * q)
                if i >= 4:
                    pe.wait_ge(gelu_done, count(FT * q + i - 3))
                for k in range(KT):
                    x = mm(psum[:, 4 + i % 4, :], w1[:, k, i * P:(i + 1) * P], ffT[:, k, :], start=k == 0, stop=k == 1)
                x.then_inc(ff_ps, 1)

            def ff_down(q, i):
                for k in range(FT):
                    if i == 0 and k >= FT - 4:
                        pe.wait_ge(gelu_done, FT * q + k + 1)
                    elif i == 0 and k == 0:
                        pe.wait_ge(gelu_done, FT * q + 5)
                    elif i > 0 and k == 0:
                        pe.wait_ge(gelu_done, FT * q + FT)
                    x = mm(psum[:, 4 + i, 0:D], hT[:, k, i * P:(i + 1) * P], w2[:, k, :], start=k == 0, stop=k == FT - 1)
                x.then_inc(c_ps, 1)

            def out_proj(q):
                pe.wait_ge(x2t_done, KT * (q + 1))
                for m in range(KT):
                    for k in range(KT):
                        x = mm(psum[:, 6 + m, :], wout[:, k, m * P:(m + 1) * P], ffT[:, k, :], start=k == 0, stop=k == 1)
                    x.then_inc(wout_ps, 1)

            def step(c, q, n):
                nq = n if n is not None else NCH
                after = n + 1 if n is not None else NCH
                for p in range(PAIRS):
                    if c is not None:
                        scores(c, p)
                    if q is None and p == 0:
                        gate_weights()
                    if q is None and p == 1:
                        bias_rows()
                        keys(n, None)
                    if q is None and p == 2:
                        queries(n, None)
                    if q is None and p == 3:
                        values(n)
                    if q is not None:
                        if p == 0:
                            for i in range(3):
                                project(q, i, nq)
                        if p == 1:
                            pe.wait_ge(abias_done, PAIRS * (q + 1))
                            if since(q, 1):
                                out_proj(q - 1)
                            pe.wait_ge(xh1, PAIRS * (q + 1))
                            turn(x1t_ps, 4)
                            for i in range(4):
                                ff_up(q, i)
                        if p == 2:
                            for i in range(5, 8):
                                ff_up(q, i)
                            ff_down(q, 0)
                        if p == 3:
                            ff_down(q, 2)
                            ff_down(q, 3)
                    if c is not None:
                        transposes(c, p)
                    if q is not None:
                        if p == 0:
                            project(q, 3, nq)
                        if p == 1:
                            ff_up(q, 4)
                        if p == 2:
                            ff_down(q, 1)
                    if n is not None and q is not None and p == 3:
                        keys(n, q)
                    if c is not None:
                        pv(c, p)
                if n is not None and q is not None:
                    queries(n, q)
                    values(n)
                if q is not None:
                    pe.wait_ge(qt_done, KT * after)
                    pe.wait_ge(y_done, PAIRS * (q + 1))
                    pe.wait_ge(xh2, PAIRS * (q + 1))
                    turn(x2t_ps, 6)

            def first():
                pe.wait_ge(ld_first, LD_FIRST)
                keys(0, None)
                queries(0, None)
                values(0)
                pe.wait_ge(ld_cond, LD_COND)
                pe.wait_ge(qt_done, KT)
                condition()
                pe.wait_ge(mask_done, 2)

            pipeline(pe, first, step)
            out_proj(NCH - 1)
            pe_tail(pe)

        def layer_norm(dve, q, done, ks):
            st, mvs, ves, rs, xh = ks
            for i in range(PAIRS):
                dve.wait_ge(done, PAIRS * q + i + 1)
                dve.bn_stats(bn6[:, i, :], lnb[:, i, :]).then_inc(st, 1)
            for i in range(PAIRS):
                dve.wait_ge(st, PAIRS * q + i + 1)
                apart(dve)
                dve.bn_aggr(mv[:, i, :], bn6[:, i, :]).then_inc(mvs, 1)
            dve.wait_ge(mvs, PAIRS * (q + 1))
            dve.tensor_scalar(ve, mv[:, :, 1], EPS, None, ALU.add).then_inc(ves, 1)
            dve.wait_ge(rs, q + 1)
            for i in range(PAIRS):
                dve.tensor_scalar(lnb[:, i, :], lnb[:, i, :], mv[:, i, 0:1], rstd[:, i:i + 1], ALU.subtract,
                                  ALU.mult).then_inc(xh, 1)

        @block.vector
        def _(dve):
            tt, ts = dve.tensor_tensor, dve.tensor_scalar

            def setup():
                dve.wait_ge(ld_cond, LD_COND)
                dve.tensor_copy(mask_l[:], ident[:, 0:T]).then_inc(mask_done, 1)
                dve.tensor_copy(mask_r[:], mask_f).then_inc(mask_done, 1)
                dve.wait_ge(gt_ps, 1)
                tt(gtT.rearrange("p j k b -> p (j k) b"), psum[:, 6, :].rearrange("p (a b) -> p a b", b=B),
                   bgc.unsqueeze(2).broadcast_to([P, NK * KT, B]), ALU.add).then_inc(gt_done, 1)
                dve.wait_ge(vcs_ps, 1)
                for j in range(NK):
                    dve.tensor_copy(vcs_nat[:, j, :], psum[0:B, 4 + j // 2, (j % 2) * D:(j % 2 + 1) * D]
                                    ).then_inc(vcs_done, 1)
                dve.wait_ge(kcs_ps, 1)
                for g in range(KT):
                    ts(kcsT[:, g].rearrange("p b j -> p j b"),
                       psum[:, 7, g * 256:(g + 1) * 256].rearrange("p (j b) -> p j b", b=B),
                       col("bk_cs", g), None, ALU.add).then_inc(kcs_done, 1)

            def gate_weights():
                dve.wait_ge(gm_ps, 1)
                for i, w in enumerate((w_is, w_cs)):
                    dve.tensor_copy(w[:, :, D:2 * D], psum[:, 4 + i, :].rearrange("p (m n) -> p m n", m=KT)
                                    ).then_inc(pe_w, 1)
                dve.wait_ge(cst_ps, 1)
                tt(c_is, psum[:, 6, 0:2], cols[:, COL["bo_is"]:COL["bo_is"] + 2], ALU.add).then_inc(cst_done, 1)
                tt(c_cs, psum[:, 6, 2:4], cols[:, COL["bo_cs"]:COL["bo_cs"] + 2], ALU.add).then_inc(cst_done, 1)

            def bias_rows():
                dve.wait_ge(ld_w, LD_W)
                tt(x1_b_row, x1_b_row, x1_res[:, 0, :], ALU.add).then_inc(half_done, 1)
                dve.wait_ge(row_ps, 1)
                dve.tensor_copy(bias3[:, 0:2 * D], psum[:, 7, :]).then_inc(row_done, 1)
                tt(bias3[:, 2 * D:3 * D], psum[:, 6, D:2 * D], bias3[:, 2 * D:3 * D], ALU.add
                   ).then_inc(row_done, 1)
                dve.wait_ge(st_vcs, 16)

            def qkv(n):
                dve.wait_ge(scores_ps, PAIRS * n)
                for g in range(KT):
                    dve.wait_ge(kq_ps, 4 * n + 3 + g)
                    ts(qT[:, g, :], psum[:, 6 + g, :], col("bq", g), None, ALU.add).then_inc(qt_done, 1)
                dve.wait_ge(pv_ps, PAIRS * n)
                for i in range(2):
                    dve.wait_ge(v_ps, 2 * n + i + 1)
                    dve.tensor_copy(v_bd[64:128, 4 * i:4 * i + 4, :, 1, :], psum[64:128, 4 + i, :].rearrange(
                        "p (b j e) -> p b j e", b=4, e=DH)).then_inc(v1_done, 1)

            s3 = s_ps.rearrange("p g (h k) -> p (g h) k", k=T)
            e3 = e.rearrange("p (h k) -> p h k", k=T)
            cs3 = cs_ps.rearrange("p (h j) -> p h j", j=NK)

            def maxima(c, p):
                dve.wait_ge(scores_ps, PAIRS * c + p + 1)
                dve.tensor_reduce(nmax, s3, AX.X, ALU.max).then_inc(nmax_done, 1)
                dve.tensor_reduce(csm, cs3, AX.X, ALU.max).then_inc(csmax_done, 1)

            def shift(c, p):
                u = PAIRS * c + p + 1
                dve.wait_ge(nmax_done, u)
                dve.wait_ge(pt_ps, count(u - 1))
                tt(e3, s3, nmax.unsqueeze(2).broadcast_to([P, H, T]), ALU.subtract).then_inc(sub_done, 1)
                dve.wait_ge(csmax_done, u)
                tt(cs_e, cs3, csm.unsqueeze(2).broadcast_to([P, H, NK]), ALU.subtract).then_inc(cssub_done, 1)

            def sums(c, p):
                u = PAIRS * c + p + 1
                dve.wait_ge(exp_done, u)
                dve.tensor_reduce(rsum, e3, AX.X, ALU.add).then_inc(rsum_done, 1)
                dve.wait_ge(csexp_done, u)
                dve.tensor_reduce(css, cs_e, AX.X, ALU.add).then_inc(cssum_done, 1)
                dve.wait_ge(rsum_done, u)
                dve.reciprocal(rinv, rsum).then_inc(rinv_done, 1)
                dve.wait_ge(cssum_done, u)
                dve.reciprocal(css, css).then_inc(csrec_done, 1)
                dve.wait_ge(csrec_done, u)
                tt(cs_e, cs_e, css.unsqueeze(2).broadcast_to([P, H, NK]), ALU.mult).then_inc(csp_done, 1)

            def copy_pT(c, p):
                dve.wait_ge(pt_ps, PAIRS * c + p + 1)
                dve.wait_ge(pv_ps, PAIRS * c + p)
                dve.tensor_copy(pT[:, 0:4, :], pT_ps[:, 0:4, :]).then_inc(pt0_done, 1)

            def context(c, p):
                dve.wait_ge(pv_ps, PAIRS * c + p + 1)
                dve.wait_ge(rt_done, PAIRS * c + p + 1)
                if p == 0:
                    dve.wait_ge(a_ps, PAIRS * c)
                tt(ctxT[:, :, p * P:(p + 1) * P], ctx_ps, rT, ALU.mult).then_inc(ctx_done, 1)

            def add_bias(q, i):
                dve.wait_ge(a_ps, PAIRS * q + i + 1)
                dve.wait_ge(f_done, count(PAIRS * q + i - 1))
                tt(proj3[:, i % 2], psum[:, 4 + 2 * (i % 2):6 + 2 * (i % 2), :].rearrange("p a n -> p (a n)")[:, 0:3 * D],
                   bias3, ALU.add).then_inc(abias_done, 1)

            def fuse(q, i):
                u = PAIRS * q + i + 1
                x3 = proj3[:, i % 2].rearrange("p (a n) -> p a n", a=3)
                dve.wait_ge(th_done, u)
                dve.wait_ge(dd_done, u)
                dve.scalar_tensor_tensor(out=x3[:, 1], in0=x3[:, 2], scalar=1.0, in1=x3[:, 1], op0=ALU.add,
                                         op1=ALU.mult).then_inc(gm_done, 1)
                dve.wait_ge(gm_done, u)
                dve.wait_ge(iz_done, u)
                if i == 0:
                    dve.wait_ge(x2t_ps, KT * q)
                dve.scalar_tensor_tensor(out=lnb[:, i, :], in0=x3[:, 1], scalar=0.5, in1=x3[:, 0], op0=ALU.mult,
                                         op1=ALU.add).then_inc(f_done, 1)

            def copy_xT(q, turned, bank, g, b, copied):
                for k in range(KT):
                    dve.wait_ge(turned, KT * q + k + 1)
                    ts(ffT[:, k, :], psum[:, bank + k, :], col(g, k), col(b, k), ALU.mult, ALU.add
                       ).then_inc(copied, 1)

            def add_ff(q, i):
                dve.wait_ge(c_ps, PAIRS * q + i + 1)
                if i == 0:
                    dve.wait_ge(x1r_done, q + 1)
                    dve.wait_ge(x1t_ps, KT * (q + 1))
                tt(lnb[:, i, :], psum[:, 4 + i, 0:D], x1_res[:, i, :], ALU.add).then_inc(y_done, 1)

            def residual(q):
                dve.wait_ge(ld_xr, 16 * (q + 1))
                for m in range(KT):
                    dve.wait_ge(wout_ps, KT * q + m + 1)
                    dve.scalar_tensor_tensor(
                        out=xT_all[:, m, :, bass.ds(q * CB, CB)].rearrange("p t b -> p b t"),
                        in0=psum[:, 6 + m, :].rearrange("p (b t) -> p b t", t=T), scalar=col("bout", m),
                        in1=xres[:, m, :].rearrange("p (b t) -> p b t", t=T), op0=ALU.add,
                        op1=ALU.add).then_inc(xout_done, 1)

            def split_biases():
                dve.wait_ge(ld_bias, 32)
                dve.wait_ge(bones, 3)
                for i in range(3):
                    row = slice(32 * i, 32 * i + 1)
                    dve.wait_ge(brest_done, i)
                    dve.tensor_copy(bparts[row], brow[row]).then_inc(bpart_done, 1)
                    if i < 2:
                        dve.tensor_copy(bpart, brow).then_inc(bpart_done, 1)
                        dve.wait_ge(bpart_done, 2 * i + 2)
                        tt(brow, brow, bpart, ALU.subtract).then_inc(brest_done, 1)

            def step(c, q, n):
                for p in range(PAIRS):
                    if c is not None:
                        maxima(c, p)
                    if q is not None and p == 1:
                        dve.wait_ge(wout_ps, KT * q)
                        copy_xT(q, x1t_ps, 4, "ln1_g", "ln1_b", x1t_done)
                    if c is not None:
                        shift(c, p)
                    if q is not None and p == 0:
                        add_bias(q, 0)
                    if p == 1 and q is not None and since(q, 1):
                        residual(q - 1)
                        if c is None:
                            split_biases()
                    if c is not None:
                        sums(c, p)
                    if q is None and p == 0:
                        gate_weights()
                    if q is None and p == 1:
                        bias_rows()
                    if q is not None:
                        if p == 0:
                            add_bias(q, 1)
                            fuse(q, 0)
                            add_bias(q, 2)
                        if p == 2:
                            add_ff(q, 0)
                        if p == 3:
                            add_ff(q, 2)
                            add_ff(q, 3)
                    if c is not None:
                        copy_pT(c, p)
                    if q is not None:
                        if p == 0:
                            fuse(q, 1)
                            add_bias(q, 3)
                            fuse(q, 2)
                        if p == 2:
                            add_ff(q, 1)
                    if c is not None:
                        context(c, p)
                    if q is not None and p == 0:
                        fuse(q, 3)
                        layer_norm(dve, q, f_done, (st1, mv1, ve1, rstd1, xh1))
                    if q is not None and p == 3:
                        layer_norm(dve, q, y_done, (st2, mv2, ve2, rstd2, xh2))
                if n is not None:
                    qkv(n)
                if q is not None:
                    dve.wait_ge(ff_ps, FT * (q + 1))
                    copy_xT(q, x2t_ps, 6, "ln2_g", "ln2_b", x2t_done)

            def first():
                dve.memset(neg_half, -0.5).then_inc(half_done, 1)
                dve.memset(v_bd, 0.0).then_inc(half_done, 1)
                dve.wait_ge(half_done, 2)
                dve.wait_ge(ld_first, LD_FIRST)
                qkv(0)
                setup()

            pipeline(dve, first, step)
            residual(NCH - 1)
            dve_tail(dve)

        @block.scalar
        def _(act):
            ac = act.activation

            def keys(n):
                act.wait_ge(ld_kbd, 16 * HG * n)
                for g in range(KT):
                    act.wait_ge(kq_ps, 4 * n + g + 1)
                    ac(kT[:, g, :], psum[:, 4 + g, :], ACT.Identity, bias=col("bk_is", g)).then_inc(kt_done, 1)

            def values(n):
                act.wait_ge(pv_ps, PAIRS * n)
                for i in range(2):
                    act.wait_ge(v_ps, 2 * n + i + 1)
                    ac(v_bd[0:64, 4 * i:4 * i + 4, :, 0, :], psum[0:64, 4 + i, :].rearrange(
                        "p (b j e) -> p b j e", b=4, e=DH), ACT.Copy).then_inc(v0_done, 1)

            def exps(c, p):
                u = PAIRS * c + p + 1
                act.wait_ge(sub_done, u)
                ac(e, e, ACT.Exp, scale=SCALE).then_inc(exp_done, 1)
                act.wait_ge(cssub_done, u)
                ac(cs_e, cs_e, ACT.Exp, scale=SCALE).then_inc(csexp_done, 1)

            def copies(c, p):
                u = PAIRS * c + p + 1
                act.wait_ge(pt_ps, u)
                act.wait_ge(pv_ps, count(u - 1))
                ac(pT[:, 4:8, :], pT_ps[:, 4:8, :], ACT.Copy).then_inc(pt1_done, 1)
                ac(cs_pT[0:64, :], cspT_ps, ACT.Copy).then_inc(cspt_done, 1)
                act.wait_ge(ctx_done, count(u - 1))
                ac(rT, rT_ps, ACT.Copy).then_inc(rt_done, 1)

            def copy_csx(c, p):
                u = PAIRS * c + p + 1
                act.wait_ge(pv_ps, u)
                act.wait_ge(ctx_done, u)
                if p == 0:
                    act.wait_ge(a_ps, PAIRS * c)
                ac(csxT[:, :, p * P:(p + 1) * P], csx_ps, ACT.Copy).then_inc(csx_done, 1)

            def gate(q, i):
                act.wait_ge(abias_done, PAIRS * q + i + 1)
                g = proj3[:, i % 2, 2 * D:3 * D]
                ac(g, g, ACT.Tanh, scale=0.5).then_inc(th_done, 1)

            def gelu(q, i):
                act.wait_ge(ff_ps, FT * q + i + 1)
                if i == 0:
                    act.wait_ge(c_ps, PAIRS * q)
                c0 = COL["b1"] + i
                ac(hT[:, i, :], psum[:, 4 + i % 4, :], ACT.Gelu, bias=cols[:, c0:c0 + 1]
                   ).then_inc(gelu_done, 1)

            def step(c, q, n):
                for p in range(PAIRS):
                    if c is not None:
                        exps(c, p)
                    if q is None and p == 1:
                        keys(n)
                    if q is not None:
                        if p == 0:
                            gate(q, 0)
                            gate(q, 1)
                        if p == 1:
                            for i in range(4):
                                gelu(q, i)
                        if p == 2:
                            for i in range(5, 8):
                                gelu(q, i)
                    if c is not None:
                        copies(c, p)
                    if q is not None:
                        if p == 0:
                            gate(q, 2)
                            gate(q, 3)
                        if p == 1:
                            gelu(q, 4)
                    if n is not None and q is not None and p == 3:
                        keys(n)
                    if c is not None:
                        copy_csx(c, p)
                if n is not None:
                    values(n)

            def first():
                act.wait_ge(half_done, 2)
                act.wait_ge(ld_first, LD_FIRST)
                keys(0)
                values(0)

            pipeline(act, first, step)
            act_tail(act)

        @block.gpsimd
        def _(pool):
            tt = pool.tensor_tensor

            def spread_cond(c):
                pool.wait_ge(scores_ps, PAIRS * c)
                for g in range(KT):
                    tt(kcs_bd[:, g], kcsT[:, g, bass.ds(c * CB, CB), :].rearrange("p b j -> p (b j)").unsqueeze(1)
                       .broadcast_to([P, HG, CB * NK]), hmask.unsqueeze(2).broadcast_to([P, HG, CB * NK]),
                       ALU.mult).then_inc(kcsbd_done, 1)
                pool.wait_ge(pv_ps, PAIRS * c)
                pool.wait_ge(ld_vcs, 16 * H * (c + 1))
                tt(vcs_bd[0:64], vcs_rep[0:64], vmask[0:64].unsqueeze(1).broadcast_to([64, CB, D]),
                   ALU.mult).then_inc(vcsbd_done, 1)

            def clear_biases():
                pool.wait_ge(ld_bias, 32)
                pool.memset(bparts, 0.0).then_inc(bones, 1)
                pool.memset(ones, 1.0).then_inc(bones, 1)
                pool.memset(cc, 0.0).then_inc(bones, 1)

            def spread_rinv(c, p):
                pool.wait_ge(rinv_done, PAIRS * c + p + 1)
                pool.wait_ge(pt_ps, PAIRS * c + p)
                apart(pool)
                pool.tensor_copy(rrep.rearrange("p (h e) -> p h e", e=DH), rinv.unsqueeze(2).broadcast_to([P, H, DH])
                                 ).then_inc(rrep_done, 1)

            def step(c, q, n):
                for p in range(PAIRS):
                    if q is not None and p == 0:
                        mix(q, 0)
                    if c is not None:
                        spread_rinv(c, p)
                    if q is not None:
                        tail(q, p)
                if q is None:
                    pool.wait_ge(ld_w, LD_W)
                    pool.wait_ge(half_done, 3)
                if n is not None:
                    spread_cond(n)

            def mix(q, i):
                u = PAIRS * q + i + 1
                x3 = proj3[:, i % 2].rearrange("p (a n) -> p a n", a=3)
                pool.wait_ge(abias_done, u)
                tt(x3[:, 1], x3[:, 1], x3[:, 0], ALU.subtract).then_inc(dd_done, 1)
                pool.wait_ge(dd_done, u)
                if i == 0:
                    pool.wait_ge(ld_zn, 16 * (q + 1))
                tt(x3[:, 0], x3[:, 0], z_nat[:, i, :], ALU.add).then_inc(iz_done, 1)

            def tail(q, p):
                if p == 0:
                    for i in range(1, PAIRS):
                        mix(q, i)
                    pool.wait_ge(ve1, q + 1)
                    tt(rstd, ve, neg_half, ALU.pow).then_inc(rstd1, 1)
                if p == 1:
                    pool.wait_ge(xh1, PAIRS * (q + 1))
                    pool.wait_ge(y_done, PAIRS * q)
                    tt(x1_res, lnb, ln1_g_row.unsqueeze(1).broadcast_to([P, PAIRS, D]), ALU.mult
                       ).then_inc(x1g_done, 1)
                    pool.wait_ge(x1g_done, q + 1)
                    tt(x1_res, x1_res, x1_b_row.unsqueeze(1).broadcast_to([P, PAIRS, D]), ALU.add
                       ).then_inc(x1r_done, 1)
                if p == 0 and isinstance(q, int) and q == NCH - 1:
                    clear_biases()
                if p == 3:
                    pool.wait_ge(ve2, q + 1)
                    tt(rstd, ve, neg_half, ALU.pow).then_inc(rstd2, 1)

            def first():
                pool.memset(k_bd, 0.0).then_inc(zero_done, 1)
                pool.wait_ge(ld_cond, LD_COND)
                pool.wait_ge(kcs_done, 2)
                spread_cond(0)

            pipeline(pool, first, step)
            pool_tail(pool)


def kernel(**inputs):
    import numpy as np
    import concourse.bacc as bacc
    from concourse import mybir as my
    from concourse.bass_utils import run_bass_kernel_spmd

    nc = bacc.Bacc("TRN2", target_bir_lowering=False, num_devices=1)
    arrays = {n: np.asarray(v) for n, v in inputs.items()}
    x, cond = arrays.pop("x"), arrays.pop("cond_1024")
    arrays["xT"] = np.ascontiguousarray(x.reshape(-1, 256).T)
    arrays["x_nat"] = np.ascontiguousarray(x.reshape(-1, 256))
    arrays["condT"] = np.ascontiguousarray(cond.T)
    arrays["cond_pad"] = np.concatenate([np.zeros((64, 256), x.dtype), cond[::-1]])
    arrays["Wo_isT"] = np.ascontiguousarray(arrays["L0_cond_Wo_is"].T)
    arrays["Wo_csT"] = np.ascontiguousarray(arrays["L0_cond_Wo_cs"].T)
    def columns(*names):
        return np.ascontiguousarray(np.concatenate([arrays[n].reshape(-1, 128).T for n in names], 1))

    arrays["cols0"] = columns(*["L0_cond_" + n for n in COLS0])
    arrays["bg_cols"] = columns("L0_cond_bg")
    two = {n: np.tile(arrays[n].reshape(-1, 64), (1, 2)).T for n in ("L3_cond_bs", "L3_cond_bp", "L3_cond_A_log",
                                                                    "L3_cond_dt_log")}
    arrays["cols3"] = np.ascontiguousarray(np.concatenate([*two.values(), columns("L3_cond_conv_b")], 1))
    p = np.arange(128)
    arrays["ident"] = np.eye(128, dtype=np.float32)
    arrays["hmask"] = (p[:, None] // 16 == np.arange(8)[None]).astype(np.float32)
    arrays["vmask"] = (np.arange(64)[:, None] // 4 == np.arange(256)[None] // 16).astype(np.float32)
    q = np.arange(64)
    arrays["mask"] = np.where((p[:, None] < q[None]) & (p[:, None] < 64), -1e30, 0.0).astype(np.float32)
    used = COLS0 + ("bg",)
    for n in used:
        if n not in ("ln1_g", "ln1_b"):
            del arrays["L0_cond_" + n]
    for n in ("L3_cond_bs", "L3_cond_bp", "L3_cond_A_log", "L3_cond_dt_log", "L3_cond_conv_b"):
        del arrays[n]
    drams = {n: nc.dram_tensor(f"in_{n}", v.shape, my.dt.from_np(v.dtype), kind="ExternalInput").ap()
             for n, v in arrays.items()}
    out = nc.dram_tensor("out_0", (64, 64, 256), my.dt.float32, kind="ExternalOutput").ap()
    cond_resid_kernel(nc, drams, out)
    r = run_bass_kernel_spmd(nc, [{f"in_{n}": v for n, v in arrays.items()}], core_ids=[0])
    return r.results[0]["out_0"]
```

```python
from contextlib import ExitStack

import concourse.bass as bass
from concourse import mybir

ALU = mybir.AluOpType
ACT = mybir.ActivationFunctionType
AX = mybir.AxisListType
F32 = mybir.dt.float32
BF16 = mybir.dt.bfloat16

P = 128
B, T, D = 64, 64, 256
H, DH, NK = 16, 16, 4
KT = D // P
HG = P // DH
CB = 8
CN = CB * T
NCH = B // CB
PAIRS = CB // 2
FF = 4 * D
FT = FF // P
NS = 64
SCALE = DH ** -0.5
EPS = 1e-5
COLS0 = ("bq", "bk_is", "bv_is", "bo_is", "bv_cs", "bo_cs", "bk_cs", "ln1_g", "ln1_b", "ln2_g", "ln2_b", "bout", "b1")


def cond_resid_kernel(nc, a, out):
    ctx = ExitStack()
    with ctx:
        def sem(name):
            return ctx.enter_context(nc.semaphore(name))

        arena = ctx.enter_context(nc.sbuf_tensor("arena", [P, 52800], F32))
        psum = ctx.enter_context(nc.psum_tensor("psum", [P, 8, 512], F32))
        taken = [0]

        def carve(*dims):
            n = 1
            for d in dims:
                n *= d
            v = arena[:, taken[0]:taken[0] + n]
            taken[0] += n
            assert taken[0] <= 52800, taken[0]
            names = "abcd"[:len(dims)]
            if len(dims) == 1:
                return v
            return v.rearrange(f"p ({' '.join(names)}) -> p {' '.join(names)}",
                               **{n: d for n, d in zip(names, dims)})

        ident = carve(P)
        xT_all = carve(KT, T, B)
        phase_start = taken[0]
        overlay = phase_start + (T + B) * D

        wq, wk, wv = carve(KT, D), carve(KT, D), carve(KT, D)
        w_is = carve(KT, 2 * D)
        w_cs = carve(KT, 2 * D)
        w1 = carve(KT, FF)
        w2 = carve(FT, D)
        wout = carve(KT, D)
        cols = carve(40)
        bias3 = carve(3 * D)
        ln1_g_row, x1_b_row = carve(D), carve(D)
        hmask = carve(HG)
        vmask = carve(D)
        neg_half = carve(PAIRS)
        kcsT = carve(KT, B, NK)
        kcs_bd = carve(KT, HG, CB * NK)
        vcs_rep = carve(PAIRS, D)
        vcs_bd = carve(PAIRS, D)
        v_bd = carve(CB, H // 2, 2, DH)
        e = carve(2 * 512)
        pT = carve(2 * PAIRS, P)
        contexts = carve(2 * KT, CN)
        ctxT, csxT = contexts[:, 0:KT], contexts[:, KT:2 * KT]
        cs_e = carve(H, NK)
        cs_pT = carve(P)
        stats = carve(5 * H)
        proj3 = carve(2, 3 * D)
        z_nat = carve(PAIRS, D)
        lnb = carve(PAIRS, D)
        x1_res = carve(PAIRS, D)
        ffT = carve(KT, CN)
        hT = carve(FT, CN)
        xres = carve(KT, CN)
        bn6 = carve(PAIRS, 6)
        mv = carve(PAIRS, 2)
        ve, rstd = carve(PAIRS), carve(PAIRS)
        assert taken[0] <= overlay
        taken[0] = overlay
        zT, qT, kT = carve(KT, CN), carve(KT, CN), carve(KT, CN)
        k_bd = carve(KT, HG, CN)
        x2T = hT[:, 4:4 + KT, :]
        wog_is = hT[:, 0:2, 0:D]
        wog_cs = hT[:, 0:2, D:2 * D]
        wgate = hT[:, 2:4, :].rearrange("p a b -> p (a b)").rearrange("p (k n) -> p k n", k=4)
        wg = hT[:, 4:8, :].rearrange("p a b -> p (a b)").rearrange("p (k n) -> p k n", k=KT)
        wkcs, wvcs = (xres[:, k, :].rearrange("p (k n) -> p k n", k=KT) for k in range(2))
        condT = z_nat[:, 0, 0:KT * B].rearrange("p (k n) -> p k n", k=KT)
        gtT = z_nat[:, 1:3, :].rearrange("p a b -> p (a b)").rearrange("p (j k b) -> p j k b", j=NK, k=KT)
        vcs_nat = lnb[0:B]
        mask_f = x1_res[:, 1, 0:T]
        c_is, c_cs = cols[:, 32:34], cols[:, 34:36]

        mask_l = ctx.enter_context(nc.sbuf_tensor("mask_l", [P, T], BF16))
        mask_r = ctx.enter_context(nc.sbuf_tensor("mask_r", [P, T], BF16))
        vcs_dram = nc.dram_tensor("vcs_dram", (NK, B, D), F32, kind="Internal").ap()
        x3_dram = nc.dram_tensor("x3_dram", (T, B, D), F32, kind="Internal").ap()
        x3r_dram = nc.dram_tensor("x3r_dram", (T, B, D), F32, kind="Internal").ap()

        COL = {name: 2 * i for i, name in enumerate(COLS0)}
        NCOLS = 2 * (len(COLS0) - 1) + FT
        bgc = proj3[:, 0, 0:8]

        def col(name, k):
            c = COL[name] + k
            return cols[:, c:c + 1]

        s_ps = psum[:, 0:2, :]
        pT_ps = psum[:, 0:2, :].rearrange("p a (b n) -> p (a b) n", n=P)
        ctx_ps = psum[:, 2, 0:256].rearrange("p (g n) -> p g n", g=KT)
        cs_ps = psum[:, 3, 0:64]
        cspT_ps = psum[0:64, 3, 64:192]
        contexts_ps = psum[:, 2, :].rearrange("p (g n) -> p g n", n=P)
        csx_ps = psum[:, 2, 256:512].rearrange("p (g n) -> p g n", g=KT)

        nmax, rsum, rinv, csm, css = (stats[:, i * H:(i + 1) * H] for i in range(5))

        passed = sem("passed")
        ld_w = sem("ld_w")
        ld_first = sem("ld_first")
        ld_cond = sem("ld_cond")
        ld_gate = sem("ld_gate")
        ld_zt = sem("ld_zt")
        ld_zn = sem("ld_zn")
        ld_xr = sem("ld_xr")
        ld_vcs = sem("ld_vcs")
        ld_kbd = sem("ld_kbd")
        st_vcs = sem("st_vcs")
        pe_w = sem("pe_w")
        gm_ps = sem("gm_ps")
        gt_ps = sem("gt_ps")
        gt_done = sem("gt_done")
        kcs_ps = sem("kcs_ps")
        kcs_done = sem("kcs_done")
        vcs_ps = sem("vcs_ps")
        vcs_done = sem("vcs_done")
        cst_ps = sem("cst_ps")
        cst_done = sem("cst_done")
        row_ps = sem("row_ps")
        row_done = sem("row_done")
        zero_done = sem("zero_done")
        half_done = sem("half_done")
        mask_done = sem("mask_done")
        kq_ps = sem("kq_ps")
        v_ps = sem("v_ps")
        scores_ps = sem("scores_ps")
        pt_ps = sem("pt_ps")
        pv_ps = sem("pv_ps")
        a_ps = sem("a_ps")
        x1t_ps = sem("x1t_ps")
        ff_ps = sem("ff_ps")
        c_ps = sem("c_ps")
        x2t_ps = sem("x2t_ps")
        wout_ps = sem("wout_ps")
        kt_done = sem("kt_done")
        qt_done = sem("qt_done")
        v0_done = sem("v0_done")
        v1_done = sem("v1_done")
        nmax_done = sem("nmax_done")
        sub_done = sem("sub_done")
        exp_done = sem("exp_done")
        rsum_done = sem("rsum_done")
        rinv_done = sem("rinv_done")
        p_done = sem("p_done")
        csmax_done = sem("csmax_done")
        cssub_done = sem("cssub_done")
        csexp_done = sem("csexp_done")
        cssum_done = sem("cssum_done")
        csrec_done = sem("csrec_done")
        csp_done = sem("csp_done")
        pt0_done = sem("pt0_done")
        pt1_done = sem("pt1_done")
        cspt_done = sem("cspt_done")
        ctx_done = sem("ctx_done")
        abias_done = sem("abias_done")
        th_done = sem("th_done")
        dd_done = sem("dd_done")
        iz_done = sem("iz_done")
        gm_done = sem("gm_done")
        f_done = sem("f_done")
        x1t_done = sem("x1t_done")
        x1g_done = sem("x1g_done")
        x1r_done = sem("x1r_done")
        gelu_done = sem("gelu_done")
        y_done = sem("y_done")
        x2t_done = sem("x2t_done")
        xout_done = sem("xout_done")
        kcsbd_done = sem("kcsbd_done")
        vcsbd_done = sem("vcsbd_done")
        st1 = sem("st1")
        mv1 = sem("mv1")
        ve1 = sem("ve1")
        rstd1 = sem("rstd1")
        xh1 = sem("xh1")
        st2 = sem("st2")
        mv2 = sem("mv2")
        ve2 = sem("ve2")
        rstd2 = sem("rstd2")
        xh2 = sem("xh2")

        def count(value):
            return max(value, 0) if isinstance(value, int) else value

        def apart(eng):
            eng.sem_inc(passed, 1)

        def diag_rows(h):
            return slice(h * DH, (h + 1) * DH)

        kp = "(k p) n -> p k n"
        loads = []
        loads.append((wq, a["L0_cond_Wq"].rearrange(kp, p=P)))
        loads.append((wk, a["L0_cond_Wk_is"].rearrange(kp, p=P)))
        loads.append((wv, a["L0_cond_Wv_is"].rearrange(kp, p=P)))
        loads.append((zT, a["xT"].rearrange(kp, p=P)[:, :, 0:CN]))
        loads.append((cols[:, 0:NCOLS], a["cols0"]))
        first_loads, loads = loads, []
        loads.append((condT, a["condT"].rearrange(kp, p=P)))
        loads.append((wg, a["L0_cond_Wg"].rearrange(kp, p=P)))
        loads.append((bgc, a["bg_cols"]))
        loads.append((wvcs, a["L0_cond_Wv_cs"].rearrange(kp, p=P)))
        loads.append((wkcs, a["L0_cond_Wk_cs"].rearrange(kp, p=P)))
        loads.append((mask_f, a["mask"]))
        loads.append((hmask, a["hmask"]))
        loads.append((ident, a["ident"]))
        loads.append((vmask, a["vmask"]))
        cond_loads, loads = loads, []
        loads.append((w_is[:, :, 0:D], a["L0_cond_Wo_is"].rearrange(kp, p=P)))
        loads.append((w_cs[:, :, 0:D], a["L0_cond_Wo_cs"].rearrange(kp, p=P)))
        loads.append((wog_is, a["Wo_isT"].rearrange(kp, p=P)))
        loads.append((wog_cs, a["Wo_csT"].rearrange(kp, p=P)))
        loads.append((wgate, a["L0_cond_Wgate"].rearrange(kp, p=P)))
        gate_loads, loads = loads, []
        loads.append((w1, a["L0_cond_W1"].rearrange(kp, p=P)))
        loads.append((w2, a["L0_cond_W2"].rearrange(kp, p=P)))
        loads.append((wout, a["L0_cond_Wout"].rearrange(kp, p=P)))
        loads.append((ln1_g_row, a["L0_cond_ln1_g"].partition_broadcast(P)))
        loads.append((x1_b_row, a["L0_cond_ln1_b"].partition_broadcast(P)))
        loads.append((x1_res[:, 0, :], a["L0_cond_b2"].partition_broadcast(P)))
        loads.append((bias3[:, 2 * D:3 * D], a["L0_cond_bgate"].partition_broadcast(P)))
        LD_W = 16 * len(loads)
        LD_GATE = 16 * len(gate_loads)
        LD_FIRST = 16 * len(first_loads)
        LD_COND = 16 * len(cond_loads)

        taken[0] = phase_start
        toeplitz = carve(T, D)
        x3r = carve(B, D)
        assert taken[0] == overlay
        ws, wp, wo3 = carve(KT, NS), carve(KT, 2 * NS), carve(D)
        cols3 = carve(16)
        buffers = taken[0]
        wx1, wh1 = carve(KT, D), carve(KT, D)
        wx2, wh2 = carve(KT, 4, D), carve(KT, 4, D)
        x1s = [carve(KT, B), carve(KT, B)]
        x2s = [carve(KT, B), carve(KT, B)]
        x3pair = carve(KT, 2, B)
        x3s = [x3pair[:, :, r, :] for r in range(2)]
        x3n = carve(D)
        h1T, h2T = carve(KT, B), carve(KT, B)
        h1n = carve(P)
        ifo, gg = carve(3, P), carve(P)
        cc, fc, ig, tc, h2n = carve(P), carve(P), carve(P), carve(P), carve(P)
        brow = carve(5 * D)
        bparts = carve(5 * D // 2).bitcast(BF16)
        bpart = carve(5 * D // 2).bitcast(BF16)
        ones = carve(B // 2).bitcast(BF16)
        taken[0] = buffers
        conv = carve(P, B)
        u = carve(4, CN)
        taken[0] = P
        decay_data = carve(CN)
        cvT = carve(KT, CN), carve(KT, CN)
        bt, ct, soft, st3, y3 = (carve(2, CN) for _ in range(5))
        taken[0] = phase_start + T * D
        x3t = carve(B // 2, D)
        bo_row = carve(D)
        ld2 = sem("ld2")
        ld_toe = sem("ld_toe")
        bones = sem("bones")
        bpart_done = sem("bpart_done")
        brest_done = sem("brest_done")
        ld_bias = sem("ld_bias")
        x1s_done = sem("x1s_done")
        a1_ps = sem("a1_ps")
        h1_done = sem("h1_done")
        h1t_ps = sem("h1t_ps")
        h1t_done = sem("h1t_done")
        x2_done = sem("x2_done")
        a2_ps = sem("a2_ps")
        ifo_done = sem("ifo_done")
        g_done = sem("g_done")
        fc_done = sem("fc_done")
        ig_done = sem("ig_done")
        c_done = sem("c_done")
        tc_done = sem("tc_done")
        h2_done = sem("h2_done")
        h2t_ps = sem("h2t_ps")
        h2t_done = sem("h2t_done")
        x3_done = sem("x3_done")
        x3_ps = sem("x3_ps")
        x3n_done = sem("x3n_done")
        x3all_done = sem("x3all_done")
        ld3 = sem("ld3")
        ld_x3r = sem("ld_x3r")
        ld_x3t = sem("ld_x3t")
        u_ps = sem("u_ps")
        u_done = sem("u_done")
        conv_ps = sem("conv_ps")
        cvt_ps = sem("cvt_ps")
        cvt_done = sem("cvt_done")
        bc_ps = sem("bc_ps")
        b_done = sem("b_done")
        ct_done = sem("ct_done")
        abs_done = sem("abs_done")
        ex_done = sem("ex_done")
        ln_done = sem("ln_done")
        sp_done = sem("sp_done")
        v_done = sem("v_done")
        col3 = sem("col3")
        scan_done = sem("scan_done")
        yy_done = sem("yy_done")
        yo_ps = sem("yo_ps")
        xb_done = sem("xb_done")
        o_done = sem("o_done")
        st_out = sem("st_out")
        st_x3 = sem("st_x3")
        st_x3r = sem("st_x3r")
        conv_done = [sem(f"conv_done_{r}") for r in range(2)]

        LD2 = 16 * 8
        LATE = 3 * T // 4

        def tiles(g):
            j, h = g // 2, g % 2
            return slice(16 * h + 4 * j, 16 * h + 4 * j + 4)

        STEPS = T

        def wave(eng, step):
            for t in range(4):
                step(t, t % 2)
            with eng.Fori(2, T // 2 - 1) as i:
                step(2 * i, 0)
                step(2 * i + 1, 1)
            for t in range(T - 2, T + 1):
                step(t, t % 2)

        def before(t, end):
            return not isinstance(t, int) or t < end

        def since(t, begin):
            return not isinstance(t, int) or t >= begin

        def sp_tail(sp):
            def load(landed, dst, src):
                sp.dma_start(dst, src).then_inc(landed, 16)

            sp.wait_ge(pv_ps, PAIRS * NCH)
            load(ld_bias, brow[:, 0:D], a["L1_cond_b"].partition_broadcast(P))
            load(ld_bias, brow[:, D:5 * D], a["L2_cond_b"].partition_broadcast(P))
            load(ld2, wx1, a["L1_cond_Wx"].rearrange(kp, p=P))
            load(ld2, wh1, a["L1_cond_Wh"].rearrange(kp, p=P))
            load(ld2, h1T, a["condT"].rearrange(kp, p=P))
            load(ld2, h2T, a["condT"].rearrange(kp, p=P))
            for k in range(KT):
                load(ld2, wx2[:, k], a["L2_cond_Wx"].rearrange("(k p) (g n) -> k p g n", p=P, n=D)[k])
                load(ld2, wh2[:, k], a["L2_cond_Wh"].rearrange("(k p) (g n) -> k p g n", p=P, n=D)[k])
            load(ld3, ws, a["L3_cond_Ws"].rearrange(kp, p=P))
            load(ld3, wp, a["L3_cond_Wp"].rearrange(kp, p=P))
            for h in range(2):
                load(ld3, wo3[64 * h:64 * h + 64], a["L3_cond_Wo"])
            load(ld3, cols3[:, 0:7], a["cols3"])
            sp.wait_ge(xout_done, KT * NCH)
            cp = a["cond_pad"]
            load(ld_toe, toeplitz[0:T].rearrange("p t d -> p (t d)"),
                 bass.AP(cp.tensor, D, [[D, T], [1, T * D]]))

            def store(t):
                sp.wait_ge(x3n_done, t + 1)
                apart(sp)
                sp.dma_start(x3_dram[bass.ds(t - 1, 2)].rearrange("o b n -> (o b) n"), x3n).then_inc(st_x3, 16)
                for r in range(2):
                    sp.dma_start(x3r_dram[bass.ds(T - t - r, 1)].rearrange("o b n -> (o b) n"),
                                 x3n[B * r:B * (r + 1)]).then_inc(st_x3r, 16)

            store(1)
            with sp.Fori(1, LATE // 2) as i:
                store(2 * i + 1)
            sp.wait_ge(st_x3r, 16 * LATE)
            load(ld_x3r, x3r[T - LATE:T], x3r_dram[T - LATE:T])
            with sp.Fori(LATE // 2, T // 2) as i:
                store(2 * i + 1)
            sp.wait_ge(st_x3, 8 * T)
            sp.wait_ge(st_x3r, 16 * T)
            load(ld_x3r, x3r[0:T - LATE], x3r_dram[0:T - LATE])
            sp.wait_ge(conv_ps, 16)
            x3_tiles = x3_dram.rearrange("t (i s) n -> s t i n", s=2)
            load(ld_x3t, bo_row, a["L3_cond_bo"].partition_broadcast(P))
            for g in range(8):
                for h in range(2):
                    load(ld_x3t, x3t[T * h:T * h + T, 4 * g:4 * g + 4, :], x3_tiles[h][:, tiles(g), :])
            out_tiles = out.rearrange("(i h) t n -> (h t) i n", h=2)
            for g in range(8):
                sp.wait_ge(o_done, 2 * (g + 1))
                sp.dma_start(out_tiles[:, tiles(g), :], x3t[:, 4 * g:4 * g + 4, :]
                             ).then_inc(st_out, 16)
            sp.wait_ge(st_out, 16 * 8)

        def pe_tail(pe):
            mm = pe.matmul

            def halves(bank, n):
                return [psum[64 * h:64 * h + 64, bank, 0:n] for h in range(2)]

            def l1_x(t, r):
                pe.wait_ge(x1s_done, t + 1)
                pe.wait_ge(h1_done, count(t - 1))
                for h, o in enumerate(halves(r, P)):
                    mm(o, ones, bparts[:, h * P:(h + 1) * P], start=True, stop=False)
                for k in range(KT):
                    for h, o in enumerate(halves(r, P)):
                        mm(o, x1s[r][:, k, :], wx1[:, k, h * P:(h + 1) * P], start=False, stop=False)

            def l1_h(t, r):
                pe.wait_ge(h1t_done, t)
                for k in range(KT):
                    for h, o in enumerate(halves(r, P)):
                        x = mm(o, h1T[:, k, :], wh1[:, k, h * P:(h + 1) * P], start=False, stop=k == 1)
                x.then_inc(a1_ps, 1)

            def l2_part(r, k, src, w):
                for h in range(2):
                    x = mm(psum[64 * h:64 * h + 64, 2 + r, :], src[:, k, :], w[:, k, :, h * P:(h + 1) * P],
                           start=False, stop=w is wh2 and k == 1)
                return x

            def l2_bias(t, r):
                pe.wait_ge(x2_done, t + 1)
                pe.wait_ge(g_done, count(t - 1))
                bp = bparts[:, D:5 * D].rearrange("p (g n) -> p g n", g=4)
                for h in range(2):
                    mm(psum[64 * h:64 * h + 64, 2 + r, :], ones, bp[:, :, h * P:(h + 1) * P], start=True, stop=False)

            def l2_h(t, r):
                pe.wait_ge(h2t_done, t)
                l2_part(r, 0, h2T, wh2)
                l2_part(r, 1, h2T, wh2).then_inc(a2_ps, 1)

            def turn_h1(t):
                pe.wait_ge(h1_done, t + 1)
                pe.wait_ge(h1t_done, t)
                pe.wait_ge(x2_done, t)
                pe.transpose(psum[:, 4, 0:P], h1n, ident).then_inc(h1t_ps, 1)

            def turn_h2(t):
                pe.wait_ge(h2_done, t + 1)
                pe.wait_ge(h2t_done, t)
                pe.wait_ge(x3_done, t)
                pe.transpose(psum[:, 5, 0:P], h2n, ident).then_inc(h2t_ps, 1)

            def turn_x3(t):
                pe.wait_ge(x3_done, t + 1)
                pe.wait_ge(x3n_done, t - 1)
                apart(pe)
                for k in range(KT):
                    x = pe.transpose(psum[:, 6, k * P:(k + 1) * P], x3pair[:, k].rearrange("p r b -> p (r b)"), ident)
                x.then_inc(x3_ps, 2)

            def step(t, r):
                if since(t, 1):
                    l2_h(t - 1, 1 - r)
                if before(t, T - 1):
                    l1_h(t + 1, 1 - r)
                if since(t, 2) and r == 1:
                    turn_x3(t - 2)
                if before(t, T):
                    l2_bias(t, r)
                    l2_part(r, 0, x2s[r], wx2)
                if before(t, T - 1):
                    turn_h1(t + 1)
                if before(t, T):
                    l2_part(r, 1, x2s[r], wx2)
                if since(t, 1):
                    turn_h2(t - 1)
                if before(t, T - 2):
                    l1_x(t + 2, r)

            pe.wait_ge(ld2, LD2)
            pe.wait_ge(bones, 3)
            pe.wait_ge(bpart_done, 5)
            l1_x(0, 0)
            l1_h(0, 0)
            l1_x(1, 1)
            turn_h1(0)
            wave(pe, step)
            turn_x3(T - 1)

            pe.wait_ge(ld3, 16 * 5)
            pe.wait_ge(x3all_done, T)
            for j in range(4):
                pe.wait_ge(u_done, count(j - 1))
                for k in range(KT):
                    for h in range(2):
                        rhs = xT_all[:, k, :, h * 32 + j * CB:h * 32 + (j + 1) * CB].rearrange("p t b -> p b t")
                        x = mm(psum[64 * h:64 * h + 64, j % 2, :], ws[:, k, :], rhs, start=k == 0, stop=k == 1)
                x.then_inc(u_ps, 1)
            pe.wait_ge(ld_toe, 16)
            pe.wait_ge(ld_x3r, 32)
            for i in range(P // 8):
                pe.wait_ge(conv_done[i % 2], count((i - 4) // 2 + 1))
                for j in range(8):
                    for h in range(2):
                        d = h * P + 8 * i + j
                        x = mm(psum[64 * h:64 * h + 64, 2 + i % 4, j * B:(j + 1) * B], toeplitz[0:T, :, d],
                               x3r[0:T, :, d], start=True, stop=True)
                x.then_inc(conv_ps, 1)

            pe.wait_ge(u_done, 4)
            pe.wait_ge(conv_done[0], 8)
            pe.wait_ge(conv_done[1], 8)

            def out_rows(m):
                j, h, i = m // 4, m // 2 % 2, m % 2
                pe.wait_ge(yy_done, j + 1)
                pe.wait_ge(o_done, count(m - 3))
                for q in range(2):
                    t = 2 * i + q
                    x = mm(psum[:, 2 + m % 4, q * D:(q + 1) * D],
                           y3[64 * h:64 * h + 64, j % 2, t * P:(t + 1) * P], wo3[64 * h:64 * h + 64, :],
                           start=True, stop=True)
                x.then_inc(yo_ps, 1)

            for j in range(4):
                for g in range(4):
                    n = 4 * j + g
                    h, i = g // 2, g % 2
                    pe.wait_ge(cvt_done, count(2 * (n - 1)))
                    for b in range(4):
                        q = h * 32 + j * CB + i * 4 + b
                        x = pe.transpose(psum[:, n % 2, b * P:(b + 1) * P], conv[:, :, q], ident)
                    x.then_inc(cvt_ps, 1)
                    if j > 1 and g > 0:
                        out_rows(4 * (j - 2) + g - 1)
                if j > 1:
                    out_rows(4 * (j - 2) + 3)
                pe.wait_ge(cvt_done, 8 * (j + 1))
                pe.wait_ge(b_done, j)
                pe.wait_ge(ct_done, j)
                pe.wait_ge(x3n_done, T)
                for w in range(2):
                    for k in range(KT):
                        for h in range(2):
                            x = mm(psum[64 * h:64 * h + 64, 6 + w, :], wp[:, k, w * NS:(w + 1) * NS],
                                   cvT[h][:, k, :], start=k == 0, stop=k == 1)
                x.then_inc(bc_ps, 1)
            for m in range(8, 16):
                out_rows(m)

        def dve_tail(dve):
            tt = dve.tensor_tensor
            def cell(t):
                dve.wait_ge(ifo_done, t + 1)
                dve.wait_ge(c_done, t)
                dve.wait_ge(tc_done, t)
                tt(fc, ifo[:, 1, :], cc, ALU.mult).then_inc(fc_done, 1)
                dve.wait_ge(g_done, t + 1)
                tt(ig, ifo[:, 0, :], gg, ALU.mult).then_inc(ig_done, 1)
                dve.wait_ge(fc_done, t + 1)
                dve.wait_ge(ig_done, t + 1)
                tt(cc, fc, ig, ALU.add).then_inc(c_done, 1)

            h1T_ps = psum[:, 4, 0:P].rearrange("p (k b) -> p k b", k=KT)

            def copy_h1(t):
                dve.wait_ge(h1t_ps, t + 1)
                dve.wait_ge(h1t_done, t)
                dve.tensor_copy(h1T, h1T_ps).then_inc(h1t_done, 1)

            def layer1_out(t, r):
                dve.wait_ge(a2_ps, count(t - 1))
                dve.wait_ge(x3_done, count(t - 1))
                dve.wait_ge(x1s_done, t + 1)
                tt(x2s[r], h1T_ps, x1s[r], ALU.add).then_inc(x2_done, 1)

            def hidden(t, r):
                dve.wait_ge(tc_done, t + 1)
                dve.wait_ge(h2t_ps, t)
                tt(h2n, ifo[:, 2, :], tc, ALU.mult).then_inc(h2_done, 1)
                dve.wait_ge(h2t_ps, t + 1)
                hT_ps = psum[:, 5, 0:P].rearrange("p (k b) -> p k b", k=KT)
                dve.wait_ge(h2t_done, t)
                dve.tensor_copy(h2T, hT_ps).then_inc(h2t_done, 1)
                dve.wait_ge(x3_ps, t - r)
                dve.wait_ge(x3all_done, count(t - 1))
                dve.wait_ge(x2_done, t + 1)
                tt(x3s[r], hT_ps, x2s[r], ALU.add).then_inc(x3_done, 1)

            def step(t, r):
                if since(t, 1):
                    cell(t - 1)
                if before(t, T - 1):
                    copy_h1(t + 1)
                if since(t, 1):
                    hidden(t - 1, 1 - r)
                if before(t, T - 1):
                    layer1_out(t + 1, 1 - r)

            copy_h1(0)
            layer1_out(0, 0)
            wave(dve, step)

            dve.wait_ge(ld3, 16 * 5)
            for j in range(4):
                dve.wait_ge(u_ps, j + 1)
                dve.tensor_scalar(u[:, j, :], psum[:, j % 2, :], cols3[:, 0:1], None, ALU.add
                                  ).then_inc(u_done, 1)
            dve.wait_ge(col3, 1)
            dve.scalar_tensor_tensor(out=cols3[:, 9:11], in0=cols3[:, 3:5], scalar=0.0, in1=cols3[:, 7:9],
                                     op0=ALU.max, op1=ALU.add).then_inc(col3, 1)
            dve.wait_ge(col3, 2)
            tt(cols3[:, 11:12], cols3[:, 9:10], cols3[:, 10:11], ALU.mult).then_inc(col3, 1)
            dve.wait_ge(col3, 3)
            dve.tensor_scalar(cols3[:, 12:13], cols3[:, 11:12], -1.0, 1.0, ALU.mult, ALU.add
                              ).then_inc(col3, 1)
            dve.wait_ge(u_ps, 4)
            dd = decay_data.rearrange("p (b t) -> p b t", t=T)
            dve.memset(dd, 1.0).then_inc(col3, 1)
            dve.wait_ge(col3, 5)
            dve.memset(dd[:, :, 0:1], 0.0).then_inc(col3, 1)
            dve.wait_ge(col3, 6)
            dve.tensor_scalar(dd, dd, cols3[:, 12:13], None, ALU.mult).then_inc(col3, 1)

            for i in range(0, P // 8, 2):
                dve.wait_ge(conv_ps, i + 1)
                dve.tensor_copy(conv[:, 8 * i:8 * i + 8, :], psum[:, 2 + i % 4, :].rearrange("p (d b) -> p d b", b=B)
                                ).then_inc(conv_done[0], 1)
            def softplus(j):
                r = j % 2
                dve.wait_ge(ln_done, j + 1)
                dve.scalar_tensor_tensor(out=bt[:, r, :], in0=bt[:, r, :], scalar=0.0, in1=soft[:, r, :], op0=ALU.max,
                                         op1=ALU.add).then_inc(sp_done, 1)

            def drive(j):
                dve.wait_ge(sp_done, j + 1)
                dve.scalar_tensor_tensor(out=u[:, j, :], in0=u[:, j, :], scalar=cols3[:, 10:11], in1=bt[:, j % 2, :],
                                         op0=ALU.mult, op1=ALU.mult).then_inc(v_done, 1)

            def scan(j):
                dve.wait_ge(v_done, j + 1)
                dve.wait_ge(col3, 7)
                dve.wait_ge(yy_done, count(j - 1))
                dve.tensor_tensor_scan(st3[:, j % 2, :], decay_data, u[:, j, :], 0.0, ALU.mult, ALU.add
                                       ).then_inc(scan_done, 1)

            def read_out(j):
                dve.wait_ge(scan_done, j + 1)
                dve.wait_ge(ct_done, j + 1)
                dve.wait_ge(yo_ps, count(4 * (j - 1)))
                tt(y3[:, j % 2, :], st3[:, j % 2, :], ct[:, j % 2, :], ALU.mult).then_inc(yy_done, 1)

            def out_add(m):
                dve.wait_ge(xb_done, m // 4 + 1)
                dve.wait_ge(yo_ps, m + 1)
                rows = x3t[:, 2 * m:2 * m + 2, :].rearrange("p a n -> p (a n)")
                tt(rows, psum[:, 2 + m % 4, :], rows, ALU.add).then_inc(o_done, 1)

            def copy_conv(j, g):
                n = 4 * j + g
                conv_t = psum[:, n % 2, :].rearrange("p (b k t) -> p b k t", k=KT, t=T)
                dve.wait_ge(cvt_ps, n + 1)
                dve.wait_ge(bc_ps, j)
                for k in range(KT):
                    dve.tensor_scalar(
                        cvT[g // 2][:, k, g % 2 * 256:(g % 2 + 1) * 256].rearrange("p (b t) -> p b t", t=T),
                        conv_t[:, :, k, :], cols3[:, 5 + k:6 + k], None, ALU.add).then_inc(cvt_done, 1)

            for j in range(4):
                copy_conv(j, 0)
                copy_conv(j, 1)
                if j > 1:
                    out_add(4 * (j - 2))
                copy_conv(j, 2)
                if j > 1:
                    out_add(4 * (j - 2) + 1)
                copy_conv(j, 3)
                if j:
                    softplus(j - 1)
                    drive(j - 1)
                if j > 1:
                    out_add(4 * (j - 2) + 2)
                if j:
                    scan(j - 1)
                    read_out(j - 1)
                if j > 1:
                    out_add(4 * (j - 2) + 3)
                dve.wait_ge(bc_ps, j + 1)
                dve.wait_ge(v_done, count(j - 1))
                dve.tensor_scalar(bt[:, j % 2, :], psum[:, 6, :], cols3[:, 1:2], None, ALU.add
                                  ).then_inc(b_done, 1)
            for m in (8, 9, 10):
                out_add(m)
            softplus(3)
            drive(3)
            scan(3)
            read_out(3)
            for m in range(11, 16):
                out_add(m)

        def act_tail(act):
            ac = act.activation

            def gates(t, r):
                a2 = psum[:, 2 + r, :].rearrange("p (g n) -> p g n", g=4)
                act.wait_ge(a2_ps, t + 1)
                act.wait_ge(h2_done, t)
                ac(ifo, a2[:, 0:3], ACT.Sigmoid).then_inc(ifo_done, 1)
                ac(gg, a2[:, 3], ACT.Tanh).then_inc(g_done, 1)

            def layer1(t, r):
                act.wait_ge(a1_ps, t + 1)
                act.wait_ge(h1t_ps, t)
                ac(h1n, psum[:, r, 0:P], ACT.Tanh).then_inc(h1_done, 1)

            def cell_tanh(t):
                act.wait_ge(c_done, t + 1)
                ac(tc, cc, ACT.Tanh).then_inc(tc_done, 1)

            def rows(t):
                act.wait_ge(x3_ps, t + 1)
                act.wait_ge(st_x3, 8 * (t - 1))
                act.wait_ge(st_x3r, 16 * (t - 1))
                ac(x3n, psum[:, 6, 0:D], ACT.Copy).then_inc(x3n_done, 2)

            def step(t, r):
                if since(t, 1):
                    gates(t - 1, 1 - r)
                if before(t, T - 1):
                    layer1(t + 1, 1 - r)
                if since(t, 1):
                    cell_tanh(t - 1)
                if since(t, 2) and r == 1:
                    rows(t - 2)

            layer1(0, 0)
            wave(act, step)
            rows(T - 1)

            def log_part(dst, src, n0):
                ac(dst, src, ACT.Abs).then_inc(abs_done, 1)
                act.wait_ge(abs_done, n0 + 1)
                ac(dst, dst, ACT.Exp, scale=-1.0).then_inc(ex_done, 1)
                act.wait_ge(ex_done, n0 + 1)
                return ac(dst, dst, ACT.Ln, bias=1.0)

            act.wait_ge(ld3, 16 * 5)
            log_part(cols3[:, 7:9], cols3[:, 3:5], 0).then_inc(col3, 1)
            for i in range(1, P // 8, 2):
                act.wait_ge(conv_ps, i + 1)
                ac(conv[:, 8 * i:8 * i + 8, :], psum[:, 2 + i % 4, :].rearrange("p (d b) -> p d b", b=B), ACT.Copy
                   ).then_inc(conv_done[1], 1)
            for j in range(4):
                r = j % 2
                act.wait_ge(b_done, j + 1)
                act.wait_ge(sp_done, count(j - 1))
                log_part(soft[:, r, :], bt[:, r, :], j + 1).then_inc(ln_done, 1)
                act.wait_ge(bc_ps, j + 1)
                act.wait_ge(yy_done, count(j - 1))
                ac(ct[:, r, :], psum[:, 7, :], ACT.Tanh, bias=cols3[:, 2:3]).then_inc(ct_done, 1)

        def pool_tail(pool):
            def stage(t, r):
                pool.wait_ge(x2_done, count(t - 1))
                pool.wait_ge(a1_ps, count(t - 1))
                apart(pool)
                pool.tensor_copy(x1s[r], xT_all[:, :, bass.ds(t, 1), :].rearrange("p k o b -> p k (o b)")
                                 ).then_inc(x1s_done, 1)

            def keep(t, r):
                pool.wait_ge(x3_done, t + 1)
                apart(pool)
                pool.tensor_copy(xT_all[:, :, bass.ds(t, 1), :].rearrange("p k o b -> p k (o b)"), x3s[r]
                                 ).then_inc(x3all_done, 1)

            pool.wait_ge(xout_done, KT * NCH)
            for t in range(4):
                stage(t, t % 2)
            keep(0, 0)
            with pool.Fori(2, T // 2) as i:
                stage(2 * i, 0)
                keep(2 * i - 3, 1)
                stage(2 * i + 1, 1)
                keep(2 * i - 2, 0)
            for t in range(T - 3, T):
                keep(t, t % 2)
            for q in range(4):
                pool.wait_ge(ld_x3t, 16 * 17)
                pool.tensor_tensor(x3t[:, 8 * q:8 * q + 8, :], x3t[:, 8 * q:8 * q + 8, :],
                                   bo_row.unsqueeze(1).broadcast_to([P, 8, D]), ALU.add
                                   ).then_inc(xb_done, 1)


        block = ctx.enter_context(nc.Block())

        def pipeline(eng, first, step):
            first()
            step(0, None, 1)
            step(1, 0, 2)
            with eng.Fori(2, NCH - 1) as c:
                step(c, c - 1, c + 1)
            step(NCH - 1, NCH - 2, None)
            step(None, NCH - 1, None)

        @block.sync
        def _(sp):
            def load(landed, dst, src):
                sp.dma_start(dst, src).then_inc(landed, 16)

            def load_zt(n):
                sp.wait_ge(v_ps, 2 * n)
                apart(sp)
                load(ld_zt, zT, a["xT"].rearrange(kp, p=P)[:, :, bass.ds(n * CN, CN)])

            def load_vcs(c):
                apart(sp)
                src = vcs_dram.rearrange("j (i s) n -> s j i n", s=2)[:, :, bass.ds(c * PAIRS, PAIRS), :]
                for half in range(2):
                    for j in range(NK):
                        sp.dma_start(vcs_rep[64 * half + j:64 * half + 64:NK],
                                     src[half, j].unsqueeze(0).broadcast_to([H, PAIRS, D])).then_inc(ld_vcs, 16)

            def spread_k(c):
                sp.wait_ge(zero_done, 1)
                apart(sp)
                sp.wait_ge(kt_done, KT * (c + 1))
                apart(sp)
                sp.wait_ge(scores_ps, PAIRS * c)
                for h in range(HG):
                    sp.dma_start(k_bd[diag_rows(h), :, h, :], kT[diag_rows(h)]).then_inc(ld_kbd, 16)

            for dst, dram in first_loads:
                load(ld_first, dst, dram)
            for dst, dram in cond_loads:
                load(ld_cond, dst, dram)
            spread_k(0)
            for dst, dram in gate_loads:
                load(ld_gate, dst, dram)
            sp.wait_ge(vcs_done, NK)
            sp.dma_start(vcs_dram.rearrange("j b n -> b j n"), vcs_nat).then_inc(st_vcs, 16)
            sp.wait_ge(st_vcs, 16)
            load_vcs(0)
            load_zt(1)
            for dst, dram in loads:
                load(ld_w, dst, dram)

            def step(c, q, n):
                if n is not None and since(n, 2):
                    load_zt(n)
                if q is not None:
                    sp.wait_ge(iz_done, PAIRS * q)
                    apart(sp)
                    load(ld_zn, z_nat, a["x_nat"].rearrange("(c i p) n -> c p i n", i=PAIRS, p=P)[q])
                    sp.wait_ge(xout_done, KT * q)
                    apart(sp)
                    load(ld_xr, xres, a["xT"].rearrange(kp, p=P)[:, :, bass.ds(q * CN, CN)])
                if n is not None:
                    sp.wait_ge(vcsbd_done, n)
                    load_vcs(n)
                    spread_k(n)

            pipeline(sp, lambda: None, step)
            sp_tail(sp)

        @block.tensor
        def _(pe):

            mm = pe.matmul

            def condition():
                for jk in range(NK * KT):
                    for k in range(KT):
                        x = mm(psum[:, 6, jk * B:(jk + 1) * B], wg[:, k, jk * P:(jk + 1) * P], condT[:, k, :],
                               start=k == 0, stop=k == 1)
                x.then_inc(gt_ps, 1)
                pe.wait_ge(gt_done, 1)
                pe.wait_ge(v0_done, 4)
                pe.wait_ge(v1_done, 4)
                for j in range(NK):
                    for k in range(KT):
                        x = mm(psum[0:B, 4 + j // 2, (j % 2) * D:(j % 2 + 1) * D], gtT[:, j, k, :], wvcs[:, k, :],
                               start=k == 0, stop=k == 1)
                x.then_inc(vcs_ps, 1)
                for g in range(KT):
                    for k in range(KT):
                        x = mm(psum[:, 7, g * 256:(g + 1) * 256], wkcs[:, k, g * P:(g + 1) * P], gtT[:, :, k, :],
                               start=k == 0, stop=k == 1)
                x.then_inc(kcs_ps, 1)

            def gate_weights():
                pe.wait_ge(ld_gate, LD_GATE)
                pe.wait_ge(vcs_done, NK)
                for i, (wt, g0) in enumerate(((wog_is, 0), (wog_cs, 2))):
                    for m in range(KT):
                        for k in range(KT):
                            x = mm(psum[:, 4 + i, m * D:(m + 1) * D], wt[:, k, m * P:(m + 1) * P], wgate[:, g0 + k, :],
                                   start=k == 0, stop=k == 1)
                x.then_inc(gm_ps, 1)
                for i, (w, b) in enumerate(((w_is, "bv_is"), (w_cs, "bv_cs"))):
                    for m in range(KT):
                        for k in range(KT):
                            x = mm(psum[:, 6, 2 * i + m:2 * i + m + 1], w[:, k, m * P:(m + 1) * P], col(b, k),
                                   start=k == 0, stop=k == 1)
                x.then_inc(cst_ps, 1)

            def bias_rows():
                pe.wait_ge(ld_w, LD_W)
                pe.wait_ge(cst_done, 2)
                pe.wait_ge(kcs_done, 2)
                for i, c_ in enumerate((c_is, c_cs)):
                    for k in range(KT):
                        x = mm(psum[:, 7, i * D + k * P:i * D + (k + 1) * P], c_[:, k:k + 1].broadcast_to([P, P]),
                               ident, start=True, stop=True)
                for i, c_ in enumerate((c_is, c_cs)):
                    for k in range(KT):
                        x = mm(psum[:, 6, D:2 * D], c_[:, k:k + 1].broadcast_to([P, P]), wgate[:, 2 * i + k, :],
                               start=i + k == 0, stop=i + k == 2)
                x.then_inc(row_ps, 1)
                pe.wait_ge(pe_w, 2)

            def keys(n, q):
                pe.wait_ge(ld_zt, 16 * n)
                if q is not None:
                    pe.wait_ge(y_done, PAIRS * q + 2)
                else:
                    pe.wait_ge(v0_done, 4 * n)
                    pe.wait_ge(v1_done, 4 * n)
                for g in range(KT):
                    for k in range(KT):
                        x = mm(psum[:, 4 + g, :], wk[:, k, g * P:(g + 1) * P], zT[:, k, :], start=k == 0, stop=k == 1)
                    x.then_inc(kq_ps, 1)

            def queries(n, q):
                if q is not None:
                    pe.wait_ge(y_done, PAIRS * (q + 1))
                else:
                    pe.wait_ge(qt_done, KT * n)
                for g in range(KT):
                    for k in range(KT):
                        x = mm(psum[:, 6 + g, :], wq[:, k, g * P:(g + 1) * P], zT[:, k, :], start=k == 0, stop=k == 1)
                    x.then_inc(kq_ps, 1)

            def values(n):
                for i in range(2):
                    pe.wait_ge(kt_done, KT * n + i + 1)
                    for b in range(2):
                        for k in range(KT):
                            x = mm(psum[:, 4 + i, b * D:(b + 1) * D], zT[:, k, (2 * i + b) * P:(2 * i + b + 1) * P],
                                   wv[:, k, :], start=k == 0, stop=k == 1)
                    x.then_inc(v_ps, 1)

            def scores(c, p):
                if p == 0:
                    pe.wait_ge(qt_done, KT * (c + 1))
                    pe.wait_ge(ld_kbd, 16 * HG * (c + 1))
                    pe.wait_ge(kcsbd_done, KT * (c + 1))
                pe.wait_ge(pt0_done, PAIRS * c + p)
                pe.wait_ge(pt1_done, PAIRS * c + p)
                pe.wait_ge(cspt_done, 2 * (PAIRS * c + p))
                for g in range(KT):
                    for half in range(2):
                        mm(s_ps[half * 64:half * 64 + 64, g, :], mask_l[:],
                           mask_r[:].unsqueeze(1).broadcast_to([P, HG, T]), start=True, stop=False)
                    for half in range(2):
                        b = 2 * p + half
                        x = mm(s_ps[half * 64:half * 64 + 64, g, :], qT[:, g, b * T:(b + 1) * T],
                               k_bd[:, g, :, b * T:(b + 1) * T], start=False, stop=True)
                for g in range(KT):
                    for half in range(2):
                        b = 2 * p + half
                        x = mm(cs_ps[half * 64:half * 64 + 64, g * 32:(g + 1) * 32], qT[:, g, b * T:(b + 1) * T],
                               kcs_bd[:, g, :, b * NK:(b + 1) * NK], start=True, stop=True)
                x.then_inc(scores_ps, 1)

            def transposes(c, p):
                pe.wait_ge(p_done, PAIRS * c + p + 1)
                for i in range(2 * PAIRS):
                    pe.transpose(pT_ps[:, i, :], e[:, i * P:(i + 1) * P], ident)
                pe.wait_ge(csp_done, PAIRS * c + p + 1)
                pe.wait_ge(cspt_done, 2 * (PAIRS * c + p))
                apart(pe)
                pe.transpose(cspT_ps, cs_e.rearrange("p a b -> p (a b)"), ident).then_inc(pt_ps, 1)

            def pv(c, p):
                if p == 0:
                    pe.wait_ge(v0_done, 4 * (c + 1))
                    pe.wait_ge(v1_done, 4 * (c + 1))
                    pe.wait_ge(vcsbd_done, c + 1)
                pe.wait_ge(pt0_done, PAIRS * c + p + 1)
                pe.wait_ge(pt1_done, PAIRS * c + p + 1)
                pe.wait_ge(ctx_done, PAIRS * c + p)
                for g in range(KT):
                    for half in range(2):
                        for j in range(4):
                            mm(ctx_ps[32 * j:32 * j + 32, g, half * 64:half * 64 + 64],
                               v_bd[:, 2 * p + half, 4 * g + j].rearrange("p h e -> p (h e)"),
                               pT[:, 4 * g + j, half * 64:half * 64 + 64], start=True, stop=True)
                pe.wait_ge(cspt_done, 2 * (PAIRS * c + p + 1))
                for g in range(KT):
                    x = mm(csx_ps[:, g, :], vcs_bd[:, p, g * P:(g + 1) * P], cs_pT[:], start=True, stop=True)
                x.then_inc(pv_ps, 1)

            def project(q, i, nq):
                if i == 0:
                    pe.wait_ge(ctx_done, PAIRS * (q + 1))
                    pe.wait_ge(v0_done, 4 * nq)
                    pe.wait_ge(v1_done, 4 * nq)
                if i == 1:
                    pe.wait_ge(x2t_done, KT * q)
                    pe.wait_ge(qt_done, KT * nq)
                if i >= 2:
                    pe.wait_ge(abias_done, count(PAIRS * q + i - 1))
                bank = 4 + 2 * (i % 2)
                t = slice(i * P, (i + 1) * P)
                for k in range(KT):
                    mm(psum[:, bank, 0:D], ctxT[:, k, t], w_is[:, k, 0:D], start=k == 0, stop=k == 1)
                for k in range(KT):
                    mm(psum[:, bank, D:2 * D], csxT[:, k, t], w_cs[:, k, 0:D], start=k == 0, stop=k == 1)
                for k in range(KT):
                    mm(psum[:, bank + 1, 0:D], ctxT[:, k, t], w_is[:, k, D:2 * D], start=k == 0, stop=False)
                for k in range(KT):
                    x = mm(psum[:, bank + 1, 0:D], csxT[:, k, t], w_cs[:, k, D:2 * D], start=False, stop=k == 1)
                x.then_inc(a_ps, 1)

            def turn(q, normalised, turned, bank):
                for k in range(KT):
                    for i in range(PAIRS):
                        if k == 0:
                            pe.wait_ge(normalised, PAIRS * q + i + 1)
                        x = pe.transpose(psum[:, bank + k, i * P:(i + 1) * P], lnb[:, i, k * P:(k + 1) * P], ident)
                    x.then_inc(turned, 1)

            def ff_up(q, i):
                if i == 0:
                    pe.wait_ge(x1t_done, KT * (q + 1))
                if i == 2:
                    pe.wait_ge(abias_done, PAIRS * (q + 1))
                    pe.wait_ge(xout_done, KT * q)
                if i >= 4:
                    pe.wait_ge(gelu_done, count(FT * q + i - 3))
                for k in range(KT):
                    x = mm(psum[:, 4 + i % 4, :], w1[:, k, i * P:(i + 1) * P], ffT[:, k, :], start=k == 0, stop=k == 1)
                x.then_inc(ff_ps, 1)

            def ff_down(q, i):
                for k in range(FT):
                    if i == 0 and k >= FT - 4:
                        pe.wait_ge(gelu_done, FT * q + k + 1)
                    elif i == 0 and k == 0:
                        pe.wait_ge(gelu_done, FT * q + 5)
                    elif i > 0 and k == 0:
                        pe.wait_ge(gelu_done, FT * q + FT)
                    x = mm(psum[:, 4 + i, 0:D], hT[:, k, i * P:(i + 1) * P], w2[:, k, :], start=k == 0,
                           stop=k == FT - 1)
                x.then_inc(c_ps, 1)

            def out_proj(q, m):
                pe.wait_ge(x2t_done, KT * (q + 1))
                for k in range(KT):
                    x = mm(psum[:, 6 + m, :], wout[:, k, m * P:(m + 1) * P], x2T[:, k, :], start=k == 0, stop=k == 1)
                x.then_inc(wout_ps, 1)

            def step(c, q, n):
                nq = n if n is not None else NCH
                after = n + 1 if n is not None else NCH
                for p in range(PAIRS):
                    if c is not None:
                        scores(c, p)
                    if q is None and p == 0:
                        gate_weights()
                    if q is None and p == 1:
                        bias_rows()
                        keys(n, None)
                    if q is None and p == 2:
                        pe.wait_ge(row_done, 2)
                        queries(n, None)
                    if q is None and p == 3:
                        values(n)
                    if q is not None:
                        if p == 0:
                            for i in range(3):
                                project(q, i, nq)
                        if p == 1:
                            pe.wait_ge(abias_done, PAIRS * (q + 1))
                            if since(q, 1):
                                out_proj(q - 1, 0)
                            turn(q, xh1, x1t_ps, 4)
                            if since(q, 1):
                                out_proj(q - 1, 1)
                            for i in range(4):
                                ff_up(q, i)
                        if p == 2:
                            for i in range(5, 8):
                                ff_up(q, i)
                            ff_down(q, 0)
                        if p == 3:
                            ff_down(q, 2)
                            ff_down(q, 3)
                    if c is not None:
                        transposes(c, p)
                    if q is not None:
                        if p == 0:
                            project(q, 3, nq)
                        if p == 1:
                            ff_up(q, 4)
                        if p == 2:
                            ff_down(q, 1)
                    if n is not None and q is not None and p == 3:
                        keys(n, q)
                    if c is not None:
                        pv(c, p)
                if n is not None and q is not None:
                    queries(n, q)
                    values(n)
                if q is not None:
                    pe.wait_ge(qt_done, KT * after)
                    pe.wait_ge(y_done, PAIRS * (q + 1))
                    turn(q, xh2, x2t_ps, 6)

            def first():
                pe.wait_ge(ld_first, LD_FIRST)
                keys(0, None)
                queries(0, None)
                values(0)
                pe.wait_ge(ld_cond, LD_COND)
                pe.wait_ge(qt_done, KT)
                condition()
                pe.wait_ge(mask_done, 2)

            pipeline(pe, first, step)
            for m in range(KT):
                out_proj(NCH - 1, m)
            pe_tail(pe)

        def values_of(i, half, h2):
            src = psum[64 * half:64 * half + 64, 4 + i, :].rearrange("p (b j h e) -> p b j h e", b=2, h=2, e=DH)
            return v_bd[64 * h2:64 * h2 + 64, 4 * i + half:4 * i + 4:2, :, h2, :], src[:, :, :, h2, :]

        def row_stats(dve, q, i, done, st):
            dve.wait_ge(done, PAIRS * q + i + 1)
            dve.bn_stats(bn6[:, i, :], lnb[:, i, :]).then_inc(st, 1)

        def layer_norm(dve, q, ks):
            st, mvs, ves, rs, xh = ks
            for i in range(PAIRS):
                dve.wait_ge(st, PAIRS * q + i + 1)
                apart(dve)
                dve.bn_aggr(mv[:, i, :], bn6[:, i, :]).then_inc(mvs, 1)
            dve.wait_ge(mvs, PAIRS * (q + 1))
            dve.tensor_scalar(ve, mv[:, :, 1], EPS, None, ALU.add).then_inc(ves, 1)
            dve.wait_ge(rs, q + 1)
            for i in range(PAIRS):
                dve.tensor_scalar(lnb[:, i, :], lnb[:, i, :], mv[:, i, 0:1], rstd[:, i:i + 1], ALU.subtract,
                                  ALU.mult).then_inc(xh, 1)

        @block.vector
        def _(dve):
            tt, ts = dve.tensor_tensor, dve.tensor_scalar

            def setup():
                dve.wait_ge(ld_cond, LD_COND)
                dve.tensor_copy(mask_l[:], ident[:, 0:T]).then_inc(mask_done, 1)
                dve.tensor_copy(mask_r[:], mask_f).then_inc(mask_done, 1)
                dve.wait_ge(gt_ps, 1)
                tt(gtT.rearrange("p j k b -> p (j k) b"), psum[:, 6, :].rearrange("p (a b) -> p a b", b=B),
                   bgc.unsqueeze(2).broadcast_to([P, NK * KT, B]), ALU.add).then_inc(gt_done, 1)
                dve.wait_ge(vcs_ps, 1)
                for j in range(NK):
                    dve.tensor_copy(vcs_nat[:, j, :], psum[0:B, 4 + j // 2, (j % 2) * D:(j % 2 + 1) * D]
                                    ).then_inc(vcs_done, 1)
                dve.wait_ge(kcs_ps, 1)
                for g in range(KT):
                    ts(kcsT[:, g].rearrange("p b j -> p j b"),
                       psum[:, 7, g * 256:(g + 1) * 256].rearrange("p (j b) -> p j b", b=B),
                       col("bk_cs", g), None, ALU.add).then_inc(kcs_done, 1)

            def gate_weights():
                dve.wait_ge(gm_ps, 1)
                for i, w in enumerate((w_is, w_cs)):
                    dve.tensor_copy(w[:, :, D:2 * D], psum[:, 4 + i, :].rearrange("p (m n) -> p m n", m=KT)
                                    ).then_inc(pe_w, 1)
                dve.wait_ge(cst_ps, 1)
                tt(c_is, psum[:, 6, 0:2], cols[:, COL["bo_is"]:COL["bo_is"] + 2], ALU.add).then_inc(cst_done, 1)
                tt(c_cs, psum[:, 6, 2:4], cols[:, COL["bo_cs"]:COL["bo_cs"] + 2], ALU.add).then_inc(cst_done, 1)

            def bias_rows():
                dve.wait_ge(ld_w, LD_W)
                tt(x1_b_row, x1_b_row, x1_res[:, 0, :], ALU.add).then_inc(half_done, 1)
                dve.wait_ge(row_ps, 1)
                dve.tensor_copy(bias3[:, 0:2 * D], psum[:, 7, :]).then_inc(row_done, 1)
                tt(bias3[:, 2 * D:3 * D], psum[:, 6, D:2 * D], bias3[:, 2 * D:3 * D], ALU.add
                   ).then_inc(row_done, 1)
                dve.wait_ge(st_vcs, 16)

            def qkv(n):
                dve.wait_ge(scores_ps, PAIRS * n)
                for g in range(KT):
                    dve.wait_ge(kq_ps, 4 * n + 3 + g)
                    ts(qT[:, g, :], psum[:, 6 + g, :], col("bq", g), None, ALU.add).then_inc(qt_done, 1)
                dve.wait_ge(pv_ps, PAIRS * n)
                dve.wait_ge(v_ps, 2 * n + 2)
                for half in range(2):
                    for h2 in range(2):
                        dst, src = values_of(1, half, h2)
                        dve.tensor_copy(dst, src).then_inc(v1_done, 1)

            s3 = s_ps.rearrange("p g (h k) -> p (g h) k", k=T)
            e3 = e.rearrange("p (h k) -> p h k", k=T)
            cs3 = cs_ps.rearrange("p (h j) -> p h j", j=NK)

            def maxima(c, p):
                dve.wait_ge(scores_ps, PAIRS * c + p + 1)
                dve.tensor_reduce(nmax, s3, AX.X, ALU.max).then_inc(nmax_done, 1)
                dve.tensor_reduce(csm, cs3, AX.X, ALU.max).then_inc(csmax_done, 1)

            def shift(c, p):
                u = PAIRS * c + p + 1
                dve.wait_ge(nmax_done, u)
                dve.wait_ge(pt_ps, count(u - 1))
                tt(e3, s3, nmax.unsqueeze(2).broadcast_to([P, H, T]), ALU.subtract).then_inc(sub_done, 1)
                dve.wait_ge(csmax_done, u)
                tt(cs_e, cs3, csm.unsqueeze(2).broadcast_to([P, H, NK]), ALU.subtract).then_inc(cssub_done, 1)

            def sums(c, p):
                u = PAIRS * c + p + 1
                dve.wait_ge(exp_done, u)
                dve.tensor_reduce(rsum, e3, AX.X, ALU.add).then_inc(rsum_done, 1)
                dve.wait_ge(csexp_done, u)
                dve.tensor_reduce(css, cs_e, AX.X, ALU.add).then_inc(cssum_done, 1)
                dve.wait_ge(rsum_done, u)
                dve.reciprocal(rinv, rsum).then_inc(rinv_done, 1)
                dve.wait_ge(rinv_done, u)
                tt(e3, e3, rinv.unsqueeze(2).broadcast_to([P, H, T]), ALU.mult).then_inc(p_done, 1)
                dve.wait_ge(cssum_done, u)
                dve.reciprocal(css, css).then_inc(csrec_done, 1)
                dve.wait_ge(csrec_done, u)
                tt(cs_e, cs_e, css.unsqueeze(2).broadcast_to([P, H, NK]), ALU.mult).then_inc(csp_done, 1)

            def copy_pT(c, p):
                dve.wait_ge(pt_ps, PAIRS * c + p + 1)
                dve.wait_ge(pv_ps, PAIRS * c + p)
                dve.tensor_copy(pT[:, 0:4, :], pT_ps[:, 0:4, :]).then_inc(pt0_done, 1)

            def add_bias(q, i):
                dve.wait_ge(a_ps, PAIRS * q + i + 1)
                dve.wait_ge(f_done, count(PAIRS * q + i - 1))
                banks = psum[:, 4 + 2 * (i % 2):6 + 2 * (i % 2), :].rearrange("p a n -> p (a n)")
                tt(proj3[:, i % 2], banks[:, 0:3 * D], bias3, ALU.add).then_inc(abias_done, 1)

            def fuse(q, i):
                u = PAIRS * q + i + 1
                x3 = proj3[:, i % 2].rearrange("p (a n) -> p a n", a=3)
                dve.wait_ge(th_done, u)
                dve.wait_ge(dd_done, u)
                dve.scalar_tensor_tensor(out=x3[:, 1], in0=x3[:, 2], scalar=1.0, in1=x3[:, 1], op0=ALU.add,
                                         op1=ALU.mult).then_inc(gm_done, 1)
                dve.wait_ge(gm_done, u)
                dve.wait_ge(iz_done, u)
                if i == 0:
                    dve.wait_ge(x2t_ps, KT * q)
                dve.scalar_tensor_tensor(out=lnb[:, i, :], in0=x3[:, 1], scalar=0.5, in1=x3[:, 0], op0=ALU.mult,
                                         op1=ALU.add).then_inc(f_done, 1)

            def copy_xT(q, turned, bank, dst, g, b, copied):
                for k in range(KT):
                    dve.wait_ge(turned, KT * q + k + 1)
                    ts(dst[:, k, :], psum[:, bank + k, :], col(g, k), col(b, k), ALU.mult, ALU.add
                       ).then_inc(copied, 1)

            def add_ff(q, i):
                dve.wait_ge(c_ps, PAIRS * q + i + 1)
                if i == 0:
                    dve.wait_ge(x1r_done, q + 1)
                    dve.wait_ge(x1t_ps, KT * (q + 1))
                tt(lnb[:, i, :], psum[:, 4 + i, 0:D], x1_res[:, i, :], ALU.add).then_inc(y_done, 1)

            def residual(q):
                dve.wait_ge(ld_xr, 16 * (q + 1))
                for m in range(KT):
                    dve.wait_ge(wout_ps, KT * q + m + 1)
                    dve.scalar_tensor_tensor(
                        out=xT_all[:, m, :, bass.ds(q * CB, CB)].rearrange("p t b -> p b t"),
                        in0=psum[:, 6 + m, :].rearrange("p (b t) -> p b t", t=T), scalar=col("bout", m),
                        in1=xres[:, m, :].rearrange("p (b t) -> p b t", t=T), op0=ALU.add,
                        op1=ALU.add).then_inc(xout_done, 1)

            def split_biases():
                dve.wait_ge(ld_bias, 32)
                dve.wait_ge(bones, 3)
                for i in range(3):
                    row = slice(32 * i, 32 * i + 1)
                    dve.wait_ge(brest_done, i)
                    dve.tensor_copy(bparts[row], brow[row]).then_inc(bpart_done, 1)
                    if i < 2:
                        dve.tensor_copy(bpart, brow).then_inc(bpart_done, 1)
                        dve.wait_ge(bpart_done, 2 * i + 2)
                        tt(brow, brow, bpart, ALU.subtract).then_inc(brest_done, 1)

            def step(c, q, n):
                for p in range(PAIRS):
                    if q is not None and p == 1:
                        dve.wait_ge(ff_ps, FT * q)
                        copy_xT(q, x1t_ps, 4, ffT, "ln1_g", "ln1_b", x1t_done)
                    if c is not None:
                        maxima(c, p)
                    if c is not None:
                        shift(c, p)
                    if q is not None and p == 0:
                        add_bias(q, 0)
                    if p == 1 and q is not None and since(q, 1):
                        residual(q - 1)
                        if c is None:
                            split_biases()
                    if c is not None:
                        sums(c, p)
                    if q is None and p == 0:
                        gate_weights()
                    if q is None and p == 1:
                        bias_rows()
                    if q is not None:
                        if p == 0:
                            add_bias(q, 1)
                            fuse(q, 0)
                            add_bias(q, 2)
                        if p == 2:
                            add_ff(q, 0)
                        if p == 3:
                            row_stats(dve, q, 0, y_done, st2)
                            row_stats(dve, q, 1, y_done, st2)
                            add_ff(q, 2)
                            row_stats(dve, q, 2, y_done, st2)
                            add_ff(q, 3)
                    if c is not None:
                        copy_pT(c, p)
                    if q is not None:
                        if p == 0:
                            row_stats(dve, q, 0, f_done, st1)
                            fuse(q, 1)
                            add_bias(q, 3)
                            fuse(q, 2)
                            row_stats(dve, q, 1, f_done, st1)
                            row_stats(dve, q, 2, f_done, st1)
                        if p == 2:
                            add_ff(q, 1)
                    if q is not None and p == 0:
                        fuse(q, 3)
                        row_stats(dve, q, 3, f_done, st1)
                        layer_norm(dve, q, (st1, mv1, ve1, rstd1, xh1))
                    if q is not None and p == 3:
                        row_stats(dve, q, 3, y_done, st2)
                        layer_norm(dve, q, (st2, mv2, ve2, rstd2, xh2))
                if n is not None:
                    qkv(n)
                if q is not None:
                    dve.wait_ge(c_ps, PAIRS * (q + 1))
                    copy_xT(q, x2t_ps, 6, x2T, "ln2_g", "ln2_b", x2t_done)

            def first():
                dve.memset(neg_half, -0.5).then_inc(half_done, 1)
                dve.memset(v_bd, 0.0).then_inc(half_done, 1)
                dve.wait_ge(half_done, 2)
                dve.wait_ge(ld_first, LD_FIRST)
                qkv(0)
                setup()

            pipeline(dve, first, step)
            residual(NCH - 1)
            dve_tail(dve)

        @block.scalar
        def _(act):
            ac = act.activation

            def keys(n):
                act.wait_ge(ld_kbd, 16 * HG * n)
                for g in range(KT):
                    act.wait_ge(kq_ps, 4 * n + g + 1)
                    ac(kT[:, g, :], psum[:, 4 + g, :], ACT.Identity, bias=col("bk_is", g)).then_inc(kt_done, 1)

            def values(n):
                act.wait_ge(pv_ps, PAIRS * n)
                act.wait_ge(v_ps, 2 * n + 1)
                for half in range(2):
                    for h2 in range(2):
                        dst, src = values_of(0, half, h2)
                        ac(dst, src, ACT.Copy).then_inc(v0_done, 1)

            def exps(c, p):
                u = PAIRS * c + p + 1
                act.wait_ge(sub_done, u)
                ac(e, e, ACT.Exp, scale=SCALE).then_inc(exp_done, 1)
                act.wait_ge(cssub_done, u)
                ac(cs_e, cs_e, ACT.Exp, scale=SCALE).then_inc(csexp_done, 1)

            def copies(c, p):
                u = PAIRS * c + p + 1
                act.wait_ge(pt_ps, u)
                act.wait_ge(pv_ps, count(u - 1))
                ac(pT[:, 4:8, :], pT_ps[:, 4:8, :], ACT.Copy).then_inc(pt1_done, 1)
                if p == 0 and isinstance(c, int) and c == 0:
                    act.wait_ge(zero_done, 2)
                for half in range(2):
                    d = slice(half * 64, half * 64 + 64)
                    ac(cs_pT[d, d], cspT_ps[:, d], ACT.Copy).then_inc(cspt_done, 1)

            def copy_contexts(c, p):
                act.wait_ge(pv_ps, PAIRS * c + p + 1)
                if p == 0:
                    act.wait_ge(a_ps, PAIRS * c)
                ac(contexts[:, :, p * P:(p + 1) * P], contexts_ps, ACT.Copy).then_inc(ctx_done, 1)

            def gate(q, i):
                act.wait_ge(abias_done, PAIRS * q + i + 1)
                g = proj3[:, i % 2, 2 * D:3 * D]
                ac(g, g, ACT.Tanh, scale=0.5).then_inc(th_done, 1)

            def gelu(q, i):
                act.wait_ge(ff_ps, FT * q + i + 1)
                if i == 0:
                    act.wait_ge(c_ps, PAIRS * q)
                if i == 4:
                    act.wait_ge(wout_ps, KT * q)
                c0 = COL["b1"] + i
                ac(hT[:, i, :], psum[:, 4 + i % 4, :], ACT.Gelu, bias=cols[:, c0:c0 + 1]
                   ).then_inc(gelu_done, 1)

            def step(c, q, n):
                for p in range(PAIRS):
                    if c is not None:
                        exps(c, p)
                    if q is None and p == 1:
                        keys(n)
                    if q is not None:
                        if p == 0:
                            gate(q, 0)
                            gate(q, 1)
                        if p == 1:
                            for i in range(4):
                                gelu(q, i)
                        if p == 2:
                            for i in range(5, 8):
                                gelu(q, i)
                    if c is not None:
                        copies(c, p)
                    if q is not None:
                        if p == 0:
                            gate(q, 2)
                            gate(q, 3)
                        if p == 1:
                            gelu(q, 4)
                    if n is not None and q is not None and p == 3:
                        keys(n)
                    if c is not None:
                        copy_contexts(c, p)
                if n is not None:
                    values(n)

            def first():
                act.wait_ge(half_done, 2)
                act.wait_ge(ld_first, LD_FIRST)
                keys(0)
                values(0)

            pipeline(act, first, step)
            act_tail(act)

        @block.gpsimd
        def _(pool):
            tt = pool.tensor_tensor

            def spread_cond(c):
                pool.wait_ge(scores_ps, PAIRS * c)
                for g in range(KT):
                    tt(kcs_bd[:, g], kcsT[:, g, bass.ds(c * CB, CB), :].rearrange("p b j -> p (b j)").unsqueeze(1)
                       .broadcast_to([P, HG, CB * NK]), hmask.unsqueeze(2).broadcast_to([P, HG, CB * NK]),
                       ALU.mult).then_inc(kcsbd_done, 1)
                pool.wait_ge(pv_ps, PAIRS * c)
                pool.wait_ge(ld_vcs, 16 * 2 * NK * (c + 1))
                tt(vcs_bd, vcs_rep, vmask.unsqueeze(1).broadcast_to([P, PAIRS, D]),
                   ALU.mult).then_inc(vcsbd_done, 1)

            def clear_biases():
                pool.wait_ge(ld_bias, 32)
                pool.memset(bparts, 0.0).then_inc(bones, 1)
                pool.memset(ones, 1.0).then_inc(bones, 1)
                pool.memset(cc, 0.0).then_inc(bones, 1)

            def step(c, q, n):
                for p in range(PAIRS):
                    if q is not None:
                        tail(q, p)
                if q is None:
                    pool.wait_ge(ld_w, LD_W)
                    pool.wait_ge(half_done, 3)
                if n is not None:
                    spread_cond(n)

            def mix(q, i):
                u = PAIRS * q + i + 1
                x3 = proj3[:, i % 2].rearrange("p (a n) -> p a n", a=3)
                pool.wait_ge(abias_done, u)
                tt(x3[:, 1], x3[:, 1], x3[:, 0], ALU.subtract).then_inc(dd_done, 1)
                pool.wait_ge(dd_done, u)
                if i == 0:
                    pool.wait_ge(ld_zn, 16 * (q + 1))
                tt(x3[:, 0], x3[:, 0], z_nat[:, i, :], ALU.add).then_inc(iz_done, 1)

            def tail(q, p):
                if p == 0:
                    for i in range(PAIRS):
                        mix(q, i)
                    pool.wait_ge(ve1, q + 1)
                    tt(rstd, ve, neg_half, ALU.pow).then_inc(rstd1, 1)
                if p == 1:
                    pool.wait_ge(xh1, PAIRS * (q + 1))
                    pool.wait_ge(y_done, PAIRS * q)
                    tt(x1_res, lnb, ln1_g_row.unsqueeze(1).broadcast_to([P, PAIRS, D]), ALU.mult
                       ).then_inc(x1g_done, 1)
                    pool.wait_ge(x1g_done, q + 1)
                    tt(x1_res, x1_res, x1_b_row.unsqueeze(1).broadcast_to([P, PAIRS, D]), ALU.add
                       ).then_inc(x1r_done, 1)
                if p == 0 and isinstance(q, int) and q == NCH - 1:
                    clear_biases()
                if p == 3:
                    pool.wait_ge(ve2, q + 1)
                    tt(rstd, ve, neg_half, ALU.pow).then_inc(rstd2, 1)

            def first():
                pool.memset(k_bd, 0.0).then_inc(zero_done, 1)
                pool.memset(cs_pT, 0.0).then_inc(zero_done, 1)
                pool.wait_ge(ld_cond, LD_COND)
                pool.wait_ge(kcs_done, 2)
                spread_cond(0)

            pipeline(pool, first, step)
            pool_tail(pool)


def kernel(**inputs):
    import numpy as np
    import concourse.bacc as bacc
    from concourse import mybir as my
    from concourse.bass_utils import run_bass_kernel_spmd

    nc = bacc.Bacc("TRN2", target_bir_lowering=False, num_devices=1)
    arrays = {n: np.asarray(v) for n, v in inputs.items()}
    x, cond = arrays.pop("x"), arrays.pop("cond_1024")
    arrays["xT"] = np.ascontiguousarray(x.reshape(-1, 256).T)
    arrays["x_nat"] = np.ascontiguousarray(x.reshape(-1, 256))
    arrays["condT"] = np.ascontiguousarray(cond.T)
    arrays["cond_pad"] = np.concatenate([np.zeros((64, 256), x.dtype), cond[::-1]])
    arrays["Wo_isT"] = np.ascontiguousarray(arrays["L0_cond_Wo_is"].T)
    arrays["Wo_csT"] = np.ascontiguousarray(arrays["L0_cond_Wo_cs"].T)
    def columns(*names):
        return np.ascontiguousarray(np.concatenate([arrays[n].reshape(-1, 128).T for n in names], 1))

    arrays["cols0"] = columns(*["L0_cond_" + n for n in COLS0])
    arrays["bg_cols"] = columns("L0_cond_bg")
    two = {n: np.tile(arrays[n].reshape(-1, 64), (1, 2)).T for n in ("L3_cond_bs", "L3_cond_bp", "L3_cond_A_log",
                                                                    "L3_cond_dt_log")}
    arrays["cols3"] = np.ascontiguousarray(np.concatenate([*two.values(), columns("L3_cond_conv_b")], 1))
    p = np.arange(128)
    arrays["ident"] = np.eye(128, dtype=np.float32)
    arrays["hmask"] = (p[:, None] // 16 == np.arange(8)[None]).astype(np.float32)
    arrays["vmask"] = (p[:, None] % 64 // 4 == np.arange(256)[None] // 16).astype(np.float32)
    q = np.arange(64)
    arrays["mask"] = np.where((p[:, None] < q[None]) & (p[:, None] < 64), -1e30, 0.0).astype(np.float32)
    used = COLS0 + ("bg",)
    for n in used:
        if n not in ("ln1_g", "ln1_b"):
            del arrays["L0_cond_" + n]
    for n in ("L3_cond_bs", "L3_cond_bp", "L3_cond_A_log", "L3_cond_dt_log", "L3_cond_conv_b"):
        del arrays[n]
    drams = {n: nc.dram_tensor(f"in_{n}", v.shape, my.dt.from_np(v.dtype), kind="ExternalInput").ap()
             for n, v in arrays.items()}
    out = nc.dram_tensor("out_0", (64, 64, 256), my.dt.float32, kind="ExternalOutput").ap()
    cond_resid_kernel(nc, drams, out)
    r = run_bass_kernel_spmd(nc, [{f"in_{n}": v for n, v in arrays.items()}], core_ids=[0])
    return r.results[0]["out_0"]
```
